# Optimizing a Trainium2 kernel written in Bass

```python
import numpy as np
import jax
import jax.numpy as jnp

def _softmax(x, axis=-1):
    return jax.nn.softmax(x, axis=axis)

def _gelu(x):
    return jax.nn.gelu(x, approximate=True)

def _silu(x):
    return jax.nn.silu(x)

def _sigmoid(x):
    return jax.nn.sigmoid(x)

def _layernorm(x, axis=-1, eps=1e-05):
    m = jnp.mean(x, axis=axis, keepdims=True)
    v = jnp.var(x, axis=axis, keepdims=True)
    return (x - m) / jnp.sqrt(v + eps)

def _scatter_add(tgt, idx, src, axis=0):
    return tgt.at[idx].add(src)

def _segment_sum(src, seg, n):
    return jax.ops.segment_sum(src, seg, n)
kernel_name = 'mk_xattn_ffn_d4_seqx_r4_1cd042'

def setup_inputs(seed: int=0):
    np.random.seed(seed)
    _w = jnp.asarray

    def _rec_inputs():
        import jax
        import jax.numpy as jnp
        _rk = jax.random.key(seed)
        x = -0.0005207 + 1.001 * jax.random.normal(jax.random.fold_in(_rk, 1), (2, 512, 256), jnp.float32)
        _lenS = 512 - jax.random.randint(jax.random.fold_in(_rk, 7), (2,), 0, max(1, 512 // 4) + 1, jnp.int32)
        _lenS2 = 1024 - jax.random.randint(jax.random.fold_in(_rk, 8), (2,), 0, max(1, 1024 // 4) + 1, jnp.int32)
        _ctx_1024P = jax.random.normal(jax.random.fold_in(_rk, 11), (2, 16, 256), jnp.float32)
        _ctx_1024c = jax.random.dirichlet(jax.random.fold_in(_rk, 511), 0.3 * jnp.ones((16,), jnp.float32), (2, 1024))
        _ctx_1024t = jnp.einsum('bsk,bkd->bsd', _ctx_1024c, _ctx_1024P)
        _ctx_1024t = _ctx_1024t * jax.lax.rsqrt(jnp.mean(jnp.square(_ctx_1024t)) + 1e-12) * 0.953939
        ctx_1024 = -1.52775e-05 + 0.999936 * (_ctx_1024t + 0.3 * jax.random.normal(jax.random.fold_in(_rk, 611), (2, 1024, 256), jnp.float32))
        return (x, ctx_1024)
    x, ctx_1024 = _rec_inputs()

    def _L0_xattn_setup():
        import jax, jax.numpy as jnp
        import numpy as np
        DIM = 256
        HEADS = 16
        DHEAD = 64
        INNER = HEADS * DHEAD
        EPS = 1e-05

        def layer_norm(x, g, b):
            mu = jnp.mean(x, axis=-1, keepdims=True)
            var = jnp.mean(jnp.square(x - mu), axis=-1, keepdims=True)
            return (x - mu) * jax.lax.rsqrt(var + EPS) * g + b

        def apply_rope(x, cos, sin):
            d2 = x.shape[-1] // 2
            x1, x2 = (x[..., :d2], x[..., d2:])
            return jnp.concatenate([x1 * cos - x2 * sin, x2 * cos + x1 * sin], axis=-1)
        key = jax.random.key(seed)
        ks = jax.random.split(key, 10)
        B, N, S = (8, 64, 1024)
        latents = jax.random.normal(ks[0], (B, N, DIM), dtype=jnp.float32)
        context = jax.random.normal(ks[1], (B, S, DIM), dtype=jnp.float32)
        cos = jax.random.uniform(ks[2], (S, DHEAD // 2), dtype=jnp.float32)
        sin = jax.random.uniform(ks[3], (S, DHEAD // 2), dtype=jnp.float32)
        init = lambda k, shp, fan_in: jax.random.normal(k, shp, dtype=jnp.float32) / np.sqrt(fan_in)
        return {'latents': latents, 'context': context, 'cos': cos, 'sin': sin, 'ln_lat_g': jnp.ones((DIM,), jnp.float32), 'ln_lat_b': jnp.zeros((DIM,), jnp.float32), 'ln_ctx_g': jnp.ones((DIM,), jnp.float32), 'ln_ctx_b': jnp.zeros((DIM,), jnp.float32), 'Wq': init(ks[4], (DIM, INNER), DIM), 'Wkv': init(ks[5], (DIM, 2 * INNER), DIM), 'Wo': init(ks[6], (INNER, DIM), INNER), 'bo': jnp.zeros((DIM,), jnp.float32)}
    _L0_xattn_all = _L0_xattn_setup()
    _L0_xattn_in = {k: v for k, v in _L0_xattn_all.items() if k in ('cos', 'sin', 'ln_lat_g', 'ln_lat_b', 'ln_ctx_g', 'ln_ctx_b', 'Wq', 'Wkv', 'Wo', 'bo')}
    del _L0_xattn_all

    def _L0_ffn_setup():
        import jax, jax.numpy as jnp
        import numpy as np
        B, S, D_MODEL, D_HIDDEN = (4, 512, 256, 1024)

        def act_quant(x):
            scale = 127.0 / jnp.clip(jnp.max(jnp.abs(x), axis=-1, keepdims=True), 1e-05)
            return jnp.clip(jnp.round(x * scale), -128, 127) / scale

        def weight_quant(w):
            scale = 1.0 / jnp.clip(jnp.mean(jnp.abs(w)), 1e-05)
            return jnp.clip(jnp.round(w * scale), -1, 1) / scale

        def bit_linear(x, w):
            xq = x + jax.lax.stop_gradient(act_quant(x) - x)
            wq = w + jax.lax.stop_gradient(weight_quant(w) - w)
            return jnp.einsum('bsd,hd->bsh', xq, wq)

        def depthwise_conv1d(x_bcl, w, b):
            y = jax.lax.conv_general_dilated(x_bcl, w, window_strides=(1,), padding=[(1, 1)], dimension_numbers=('NCH', 'OIH', 'NCH'), feature_group_count=x_bcl.shape[1])
            return y + b[None, :, None]
        key = jax.random.key(seed)
        ks = jax.random.split(key, 5)
        lim1 = 1.0 / np.sqrt(D_MODEL)
        lim2 = 1.0 / np.sqrt(D_HIDDEN)
        limc = 1.0 / np.sqrt(3.0)
        return {'x': jax.random.normal(ks[0], (B, S, D_MODEL), dtype=jnp.float32), 'w1': jax.random.uniform(ks[1], (D_HIDDEN, D_MODEL), jnp.float32, -lim1, lim1), 'conv_w': jax.random.uniform(ks[2], (D_HIDDEN, 1, 3), jnp.float32, -limc, limc), 'conv_b': jax.random.uniform(ks[3], (D_HIDDEN,), jnp.float32, -limc, limc), 'w2': jax.random.uniform(ks[4], (D_MODEL, D_HIDDEN), jnp.float32, -lim2, lim2)}
    _L0_ffn_all = _L0_ffn_setup()
    _L0_ffn_in = {k: v for k, v in _L0_ffn_all.items() if k in ('w1', 'conv_w', 'conv_b', 'w2')}
    del _L0_ffn_all

    def _L1_xattn_setup():
        import jax, jax.numpy as jnp
        import numpy as np
        D_MODEL = 256
        N_HEADS = 16
        HEAD_DIM = D_MODEL // N_HEADS

        def sparsemax(x):
            x = x - jnp.max(x, axis=-1, keepdims=True)
            zs = -jnp.sort(-x, axis=-1)
            L = x.shape[-1]
            rho = jnp.arange(1, L + 1, dtype=x.dtype)
            cssv = jnp.cumsum(zs, axis=-1) - 1.0
            support = zs > cssv / rho
            k = jnp.maximum(jnp.sum(support, axis=-1, keepdims=True), 1)
            tau = jnp.take_along_axis(cssv, k - 1, axis=-1) / k.astype(x.dtype)
            return jnp.clip(x - tau, 0.0)

        def _split_heads(x):
            B, L, _ = x.shape
            return x.reshape(B, L, N_HEADS, HEAD_DIM).transpose(0, 2, 1, 3)
        key = jax.random.key(seed)
        ks = jax.random.split(key, 11)
        B, L = (2, 512)
        s = 0.02
        inp = {'q': jax.random.normal(ks[0], (B, L, D_MODEL), jnp.float32), 'k': jax.random.normal(ks[1], (B, L, D_MODEL), jnp.float32), 'v': jax.random.normal(ks[2], (B, L, D_MODEL), jnp.float32), 'Wq': jax.random.normal(ks[3], (D_MODEL, D_MODEL), jnp.float32) * s, 'bq': jnp.zeros((D_MODEL,), jnp.float32), 'Wk': jax.random.normal(ks[4], (D_MODEL, D_MODEL), jnp.float32) * s, 'bk': jnp.zeros((D_MODEL,), jnp.float32), 'Wv': jax.random.normal(ks[5], (D_MODEL, D_MODEL), jnp.float32) * s, 'bv': jnp.zeros((D_MODEL,), jnp.float32), 'Wo': jax.random.normal(ks[6], (D_MODEL, D_MODEL), jnp.float32) * s, 'bo': jnp.zeros((D_MODEL,), jnp.float32)}
        return inp
    _L1_xattn_all = _L1_xattn_setup()
    _L1_xattn_in = {k: v for k, v in _L1_xattn_all.items() if k in ('Wq', 'bq', 'Wk', 'bk', 'Wv', 'bv', 'Wo', 'bo')}
    del _L1_xattn_all

    def _L1_ffn_setup():
        import jax, jax.numpy as jnp
        import numpy as np
        TOP_K = 2
        ROUTE_SCALE = 1.0
        EPS = 1e-20
        key = jax.random.key(seed)
        ks = jax.random.split(key, 8)
        dim, hid, E, X = (256, 704, 8, 1)
        std = 0.02
        x = jax.random.normal(ks[0], (2, 512, dim), dtype=jnp.float32)
        w1 = jax.random.normal(ks[1], (E, hid, dim), dtype=jnp.float32) * std
        w2 = jax.random.normal(ks[2], (E, dim, hid), dtype=jnp.float32) * std
        w3 = jax.random.normal(ks[3], (E, hid, dim), dtype=jnp.float32) * std
        new_w1 = jax.random.normal(ks[4], (X, hid, dim), dtype=jnp.float32) * std
        new_w2 = jnp.zeros((X, dim, hid), dtype=jnp.float32)
        new_w3 = jax.random.normal(ks[5], (X, hid, dim), dtype=jnp.float32) * std
        gate_weight = jax.random.normal(ks[6], (E, dim), dtype=jnp.float32) * std
        new_gate_weight = jax.random.normal(ks[7], (X, dim), dtype=jnp.float32) * std
        gate_bias = jnp.zeros((X,), dtype=jnp.float32)
        return dict(x=x, w1=w1, w2=w2, w3=w3, new_w1=new_w1, new_w2=new_w2, new_w3=new_w3, gate_weight=gate_weight, new_gate_weight=new_gate_weight, gate_bias=gate_bias)
    _L1_ffn_all = _L1_ffn_setup()
    _L1_ffn_in = {k: v for k, v in _L1_ffn_all.items() if k in ('w1', 'w2', 'w3', 'new_w1', 'new_w2', 'new_w3', 'gate_weight', 'new_gate_weight', 'gate_bias')}
    del _L1_ffn_all

    def _L2_xattn_setup():
        import jax, jax.numpy as jnp
        import numpy as np
        D = 256
        NUM_ITERS = 3
        EPS = 1e-06
        SCALE = D ** (-0.5)

        def rmsnorm(x, w, eps=EPS):
            return x * jax.lax.rsqrt(jnp.mean(x * x, axis=-1, keepdims=True) + eps) * w

        def gru_cell(x, h, wih, whh, bih, bhh):
            gx = x @ wih.T + bih
            gh = h @ whh.T + bhh
            xr, xz, xn = jnp.split(gx, 3, axis=-1)
            hr, hz, hn = jnp.split(gh, 3, axis=-1)
            r = jax.nn.sigmoid(xr + hr)
            z = jax.nn.sigmoid(xz + hz)
            n = jnp.tanh(xn + r * hn)
            return (1.0 - z) * n + z * h
        key = jax.random.key(seed)
        ks = jax.random.split(key, 8)
        B, K, M, d = (8, 64, 1024, D)
        w_std = d ** (-0.5)
        return {'slots': jax.random.normal(ks[0], (B, K, d), jnp.float32), 'P': jax.random.normal(ks[1], (B, M, d), jnp.float32), 'Wq': jax.random.normal(ks[2], (d, d), jnp.float32) * w_std, 'Wk': jax.random.normal(ks[3], (d, d), jnp.float32) * w_std, 'Wv': jax.random.normal(ks[4], (d, d), jnp.float32) * w_std, 'gru_wih': jax.random.normal(ks[5], (3 * d, d), jnp.float32) * w_std, 'gru_whh': jax.random.normal(ks[6], (3 * d, d), jnp.float32) * w_std, 'gru_bih': jnp.zeros((3 * d,), jnp.float32), 'gru_bhh': jnp.zeros((3 * d,), jnp.float32), 'slot_norm_w': jnp.ones((d,), jnp.float32), 'input_norm_w': jnp.ones((d,), jnp.float32)}
    _L2_xattn_all = _L2_xattn_setup()
    _L2_xattn_in = {k: v for k, v in _L2_xattn_all.items() if k in ('Wq', 'Wk', 'Wv', 'gru_wih', 'gru_whh', 'gru_bih', 'gru_bhh', 'slot_norm_w', 'input_norm_w')}
    del _L2_xattn_all

    def _L2_ffn_setup():
        import jax, jax.numpy as jnp
        import numpy as np
        D_MODEL = 256
        NHEAD = 16
        HEAD_DIM = D_MODEL // NHEAD
        FF = 512
        NUM_EXPERTS = 8
        EPS = 1e-05

        def _ln(x, g, b):
            m = x.mean(-1, keepdims=True)
            v = ((x - m) ** 2).mean(-1, keepdims=True)
            return (x - m) / jnp.sqrt(v + EPS) * g + b

        def _attention(src, Wq, bq, Wk, bk, Wv, bv, Wo, bo):
            B, T, d = src.shape
            scale = HEAD_DIM ** (-0.5)
            q = (src @ Wq + bq).reshape(B, T, NHEAD, HEAD_DIM)
            k = (src @ Wk + bk).reshape(B, T, NHEAD, HEAD_DIM)
            v = (src @ Wv + bv).reshape(B, T, NHEAD, HEAD_DIM)
            scores = jnp.einsum('bqhd,bkhd->bhqk', q, k) * scale
            probs = jax.nn.softmax(scores, axis=-1)
            out = jnp.einsum('bhqk,bkhd->bqhd', probs, v).reshape(B, T, d)
            return out @ Wo + bo

        def _moe(x, gW, gb, W1, b1, W2, b2):
            B, T, d = x.shape
            xf = x.reshape(-1, d)
            gates = jax.nn.softmax(xf @ gW + gb, axis=-1)
            top2_scores, top2_idx = jax.lax.top_k(gates, 2)
            w = (jax.nn.one_hot(top2_idx, NUM_EXPERTS, dtype=xf.dtype) * top2_scores[..., None]).sum(1)
            h = jax.nn.relu(jnp.einsum('nd,edf->enf', xf, W1) + b1[:, None, :])
            y = jnp.einsum('enf,efd->end', h, W2) + b2[:, None, :]
            out = jnp.einsum('ne,end->nd', w, y)
            return out.reshape(B, T, d)
        key = jax.random.key(seed)
        ks = jax.random.split(key, 12)
        s = 0.02
        d, f, E = (D_MODEL, FF, NUM_EXPERTS)
        return {'src': jax.random.normal(ks[0], (8, 128, d), dtype=jnp.float32), 'Wq': jax.random.normal(ks[1], (d, d), dtype=jnp.float32) * s, 'bq': jnp.zeros((d,), jnp.float32), 'Wk': jax.random.normal(ks[2], (d, d), dtype=jnp.float32) * s, 'bk': jnp.zeros((d,), jnp.float32), 'Wv': jax.random.normal(ks[3], (d, d), dtype=jnp.float32) * s, 'bv': jnp.zeros((d,), jnp.float32), 'Wo': jax.random.normal(ks[4], (d, d), dtype=jnp.float32) * s, 'bo': jnp.zeros((d,), jnp.float32), 'gW': jax.random.normal(ks[5], (d, E), dtype=jnp.float32) * s, 'gb': jnp.zeros((E,), jnp.float32), 'W1': jax.random.normal(ks[6], (E, d, f), dtype=jnp.float32) * s, 'b1': jnp.zeros((E, f), jnp.float32), 'W2': jax.random.normal(ks[7], (E, f, d), dtype=jnp.float32) * s, 'b2': jnp.zeros((E, d), jnp.float32), 'ln1_g': jnp.ones((d,), jnp.float32), 'ln1_b': jnp.zeros((d,), jnp.float32), 'ln2_g': jnp.ones((d,), jnp.float32), 'ln2_b': jnp.zeros((d,), jnp.float32)}
    _L2_ffn_all = _L2_ffn_setup()
    _L2_ffn_in = {k: v for k, v in _L2_ffn_all.items() if k in ('Wq', 'bq', 'Wk', 'bk', 'Wv', 'bv', 'Wo', 'bo', 'gW', 'gb', 'W1', 'b1', 'W2', 'b2', 'ln1_g', 'ln1_b', 'ln2_g', 'ln2_b')}
    del _L2_ffn_all

    def _L3_xattn_setup():
        import jax, jax.numpy as jnp
        import numpy as np
        DIM = 256
        NUM_HEADS = 16
        HEAD_DIM = DIM // NUM_HEADS

        def _split(x):
            b, l, _ = x.shape
            return x.reshape(b, l, NUM_HEADS, HEAD_DIM).transpose(0, 2, 1, 3)
        key = jax.random.key(seed)
        ks = jax.random.split(key, 8)
        B, N, M = (4, 512, 512)
        scale = DIM ** (-0.5)
        return {'input': jax.random.normal(ks[0], (B, N, DIM), dtype=jnp.float32), 'memory': jax.random.normal(ks[1], (B, M, DIM), dtype=jnp.float32), 'Wq': jax.random.normal(ks[2], (DIM, DIM), dtype=jnp.float32) * scale, 'bq': jnp.zeros((DIM,), dtype=jnp.float32), 'Wk': jax.random.normal(ks[3], (DIM, DIM), dtype=jnp.float32) * scale, 'bk': jnp.zeros((DIM,), dtype=jnp.float32), 'Wv': jax.random.normal(ks[4], (DIM, DIM), dtype=jnp.float32) * scale, 'bv': jnp.zeros((DIM,), dtype=jnp.float32)}
    _L3_xattn_all = _L3_xattn_setup()
    _L3_xattn_in = {k: v for k, v in _L3_xattn_all.items() if k in ('Wq', 'bq', 'Wk', 'bk', 'Wv', 'bv')}
    del _L3_xattn_all

    def _L3_ffn_setup():
        import jax, jax.numpy as jnp
        import numpy as np
        B, S, H = (1, 512, 256)
        E, K = (16, 4)
        G, TG = (4, 2)
        I_MOE = 128
        N_SH = 2
        SCALE = 2.5

        def _mlp(x, gw, uw, dw):
            return jax.nn.silu(x @ gw.T) * (x @ uw.T) @ dw.T

        def _route(x2d, router_weight, e_bias):
            T = x2d.shape[0]
            scores = jax.nn.sigmoid(x2d @ router_weight.T)
            sc = scores + e_bias[None, :]
            group_scores = jnp.sum(jax.lax.top_k(sc.reshape(T, G, E // G), 2)[0], axis=-1)
            _, gidx = jax.lax.top_k(group_scores, TG)
            gmask = jnp.zeros((T, G), sc.dtype).at[jnp.arange(T)[:, None], gidx].set(1.0)
            smask = jnp.repeat(gmask, E // G, axis=1)
            masked = jnp.where(smask > 0, sc, 0.0)
            _, tidx = jax.lax.top_k(masked, K)
            tw = jnp.take_along_axis(scores, tidx, axis=1)
            tw = tw / (jnp.sum(tw, axis=-1, keepdims=True) + 1e-20)
            tw = tw * SCALE
            return (tidx, tw)

        def _moe_forward(hidden_states, router_weight, e_bias, gate_w, up_w, down_w, sh_gate_w, sh_up_w, sh_down_w):
            orig_shape = hidden_states.shape
            x = hidden_states.reshape(-1, H)
            T = x.shape[0]
            tidx, tw = _route(x, router_weight, e_bias)
            g = jnp.einsum('th,eih->tei', x, gate_w)
            u = jnp.einsum('th,eih->tei', x, up_w)
            h = jax.nn.silu(g) * u
            yo = jnp.einsum('tei,ehi->teh', h, down_w)
            combine = jnp.zeros((T, E), tw.dtype).at[jnp.arange(T)[:, None], tidx].add(tw)
            routed = jnp.einsum('te,teh->th', combine, yo)
            shared = _mlp(hidden_states.reshape(-1, H), sh_gate_w, sh_up_w, sh_down_w)
            return (routed + shared).reshape(orig_shape)
        key = jax.random.key(seed)
        ks = jax.random.split(key, 9)
        s = 0.02
        return {'hidden_states': jax.random.normal(ks[0], (B, S, H), jnp.float32), 'router_weight': jax.random.normal(ks[1], (E, H), jnp.float32) * s, 'e_bias': jnp.zeros((E,), jnp.float32), 'gate_w': jax.random.normal(ks[2], (E, I_MOE, H), jnp.float32) * s, 'up_w': jax.random.normal(ks[3], (E, I_MOE, H), jnp.float32) * s, 'down_w': jax.random.normal(ks[4], (E, H, I_MOE), jnp.float32) * s, 'sh_gate_w': jax.random.normal(ks[5], (N_SH * I_MOE, H), jnp.float32) * s, 'sh_up_w': jax.random.normal(ks[6], (N_SH * I_MOE, H), jnp.float32) * s, 'sh_down_w': jax.random.normal(ks[7], (H, N_SH * I_MOE), jnp.float32) * s}
    _L3_ffn_all = _L3_ffn_setup()
    _L3_ffn_in = {k: v for k, v in _L3_ffn_all.items() if k in ('router_weight', 'e_bias', 'gate_w', 'up_w', 'down_w', 'sh_gate_w', 'sh_up_w', 'sh_down_w')}
    del _L3_ffn_all
    return {'x': x, 'ctx_1024': ctx_1024, 'L0_xattn_cos': _L0_xattn_in['cos'], 'L0_xattn_sin': _L0_xattn_in['sin'], 'L0_xattn_ln_lat_g': _L0_xattn_in['ln_lat_g'], 'L0_xattn_ln_lat_b': _L0_xattn_in['ln_lat_b'], 'L0_xattn_ln_ctx_g': _L0_xattn_in['ln_ctx_g'], 'L0_xattn_ln_ctx_b': _L0_xattn_in['ln_ctx_b'], 'L0_xattn_Wq': _L0_xattn_in['Wq'], 'L0_xattn_Wkv': _L0_xattn_in['Wkv'], 'L0_xattn_Wo': _L0_xattn_in['Wo'], 'L0_xattn_bo': _L0_xattn_in['bo'], 'L0_ffn_w1': _L0_ffn_in['w1'], 'L0_ffn_conv_w': _L0_ffn_in['conv_w'], 'L0_ffn_conv_b': _L0_ffn_in['conv_b'], 'L0_ffn_w2': _L0_ffn_in['w2'], 'L1_xattn_Wq': _L1_xattn_in['Wq'], 'L1_xattn_bq': _L1_xattn_in['bq'], 'L1_xattn_Wk': _L1_xattn_in['Wk'], 'L1_xattn_bk': _L1_xattn_in['bk'], 'L1_xattn_Wv': _L1_xattn_in['Wv'], 'L1_xattn_bv': _L1_xattn_in['bv'], 'L1_xattn_Wo': _L1_xattn_in['Wo'], 'L1_xattn_bo': _L1_xattn_in['bo'], 'L1_ffn_w1': _L1_ffn_in['w1'], 'L1_ffn_w2': _L1_ffn_in['w2'], 'L1_ffn_w3': _L1_ffn_in['w3'], 'L1_ffn_new_w1': _L1_ffn_in['new_w1'], 'L1_ffn_new_w2': _L1_ffn_in['new_w2'], 'L1_ffn_new_w3': _L1_ffn_in['new_w3'], 'L1_ffn_gate_weight': _L1_ffn_in['gate_weight'], 'L1_ffn_new_gate_weight': _L1_ffn_in['new_gate_weight'], 'L1_ffn_gate_bias': _L1_ffn_in['gate_bias'], 'L2_xattn_Wq': _L2_xattn_in['Wq'], 'L2_xattn_Wk': _L2_xattn_in['Wk'], 'L2_xattn_Wv': _L2_xattn_in['Wv'], 'L2_xattn_gru_wih': _L2_xattn_in['gru_wih'], 'L2_xattn_gru_whh': _L2_xattn_in['gru_whh'], 'L2_xattn_gru_bih': _L2_xattn_in['gru_bih'], 'L2_xattn_gru_bhh': _L2_xattn_in['gru_bhh'], 'L2_xattn_slot_norm_w': _L2_xattn_in['slot_norm_w'], 'L2_xattn_input_norm_w': _L2_xattn_in['input_norm_w'], 'L2_ffn_Wq': _L2_ffn_in['Wq'], 'L2_ffn_bq': _L2_ffn_in['bq'], 'L2_ffn_Wk': _L2_ffn_in['Wk'], 'L2_ffn_bk': _L2_ffn_in['bk'], 'L2_ffn_Wv': _L2_ffn_in['Wv'], 'L2_ffn_bv': _L2_ffn_in['bv'], 'L2_ffn_Wo': _L2_ffn_in['Wo'], 'L2_ffn_bo': _L2_ffn_in['bo'], 'L2_ffn_gW': _L2_ffn_in['gW'], 'L2_ffn_gb': _L2_ffn_in['gb'], 'L2_ffn_W1': _L2_ffn_in['W1'], 'L2_ffn_b1': _L2_ffn_in['b1'], 'L2_ffn_W2': _L2_ffn_in['W2'], 'L2_ffn_b2': _L2_ffn_in['b2'], 'L2_ffn_ln1_g': _L2_ffn_in['ln1_g'], 'L2_ffn_ln1_b': _L2_ffn_in['ln1_b'], 'L2_ffn_ln2_g': _L2_ffn_in['ln2_g'], 'L2_ffn_ln2_b': _L2_ffn_in['ln2_b'], 'L3_xattn_Wq': _L3_xattn_in['Wq'], 'L3_xattn_bq': _L3_xattn_in['bq'], 'L3_xattn_Wk': _L3_xattn_in['Wk'], 'L3_xattn_bk': _L3_xattn_in['bk'], 'L3_xattn_Wv': _L3_xattn_in['Wv'], 'L3_xattn_bv': _L3_xattn_in['bv'], 'L3_ffn_router_weight': _L3_ffn_in['router_weight'], 'L3_ffn_e_bias': _L3_ffn_in['e_bias'], 'L3_ffn_gate_w': _L3_ffn_in['gate_w'], 'L3_ffn_up_w': _L3_ffn_in['up_w'], 'L3_ffn_down_w': _L3_ffn_in['down_w'], 'L3_ffn_sh_gate_w': _L3_ffn_in['sh_gate_w'], 'L3_ffn_sh_up_w': _L3_ffn_in['sh_up_w'], 'L3_ffn_sh_down_w': _L3_ffn_in['sh_down_w']}

def reference(x, ctx_1024, L0_xattn_cos, L0_xattn_sin, L0_xattn_ln_lat_g, L0_xattn_ln_lat_b, L0_xattn_ln_ctx_g, L0_xattn_ln_ctx_b, L0_xattn_Wq, L0_xattn_Wkv, L0_xattn_Wo, L0_xattn_bo, L0_ffn_w1, L0_ffn_conv_w, L0_ffn_conv_b, L0_ffn_w2, L1_xattn_Wq, L1_xattn_bq, L1_xattn_Wk, L1_xattn_bk, L1_xattn_Wv, L1_xattn_bv, L1_xattn_Wo, L1_xattn_bo, L1_ffn_w1, L1_ffn_w2, L1_ffn_w3, L1_ffn_new_w1, L1_ffn_new_w2, L1_ffn_new_w3, L1_ffn_gate_weight, L1_ffn_new_gate_weight, L1_ffn_gate_bias, L2_xattn_Wq, L2_xattn_Wk, L2_xattn_Wv, L2_xattn_gru_wih, L2_xattn_gru_whh, L2_xattn_gru_bih, L2_xattn_gru_bhh, L2_xattn_slot_norm_w, L2_xattn_input_norm_w, L2_ffn_Wq, L2_ffn_bq, L2_ffn_Wk, L2_ffn_bk, L2_ffn_Wv, L2_ffn_bv, L2_ffn_Wo, L2_ffn_bo, L2_ffn_gW, L2_ffn_gb, L2_ffn_W1, L2_ffn_b1, L2_ffn_W2, L2_ffn_b2, L2_ffn_ln1_g, L2_ffn_ln1_b, L2_ffn_ln2_g, L2_ffn_ln2_b, L3_xattn_Wq, L3_xattn_bq, L3_xattn_Wk, L3_xattn_bk, L3_xattn_Wv, L3_xattn_bv, L3_ffn_router_weight, L3_ffn_e_bias, L3_ffn_gate_w, L3_ffn_up_w, L3_ffn_down_w, L3_ffn_sh_gate_w, L3_ffn_sh_up_w, L3_ffn_sh_down_w):
    import jax
    import jax.numpy as jnp

    def _L0_xattn_ref(latents, context, cos, sin, ln_lat_g, ln_lat_b, ln_ctx_g, ln_ctx_b, Wq, Wkv, Wo, bo):
        import jax, jax.numpy as jnp
        import numpy as np
        DIM = 256
        HEADS = 16
        DHEAD = 64
        INNER = HEADS * DHEAD
        EPS = 1e-05

        def layer_norm(x, g, b):
            mu = jnp.mean(x, axis=-1, keepdims=True)
            var = jnp.mean(jnp.square(x - mu), axis=-1, keepdims=True)
            return (x - mu) * jax.lax.rsqrt(var + EPS) * g + b

        def apply_rope(x, cos, sin):
            d2 = x.shape[-1] // 2
            x1, x2 = (x[..., :d2], x[..., d2:])
            return jnp.concatenate([x1 * cos - x2 * sin, x2 * cos + x1 * sin], axis=-1)
        b, n, _ = latents.shape
        s = context.shape[1]
        lat = layer_norm(latents, ln_lat_g, ln_lat_b)
        ctx = layer_norm(context, ln_ctx_g, ln_ctx_b)
        q = (lat @ Wq).reshape(b, n, HEADS, DHEAD).transpose(0, 2, 1, 3)
        kv = ctx @ Wkv
        k, v = jnp.split(kv, 2, axis=-1)
        k = k.reshape(b, s, HEADS, DHEAD).transpose(0, 2, 1, 3)
        v = v.reshape(b, s, HEADS, DHEAD).transpose(0, 2, 1, 3)
        k = apply_rope(k, cos[None, None], sin[None, None])
        scale = DHEAD ** (-0.5)
        attn = jnp.einsum('bhnd,bhsd->bhns', q, k) * scale
        attn = jnp.clip(attn, -11.0, 11.0)
        attn = jax.nn.softmax(attn, axis=-1)
        out = jnp.einsum('bhns,bhsd->bhnd', attn, v)
        out = out.transpose(0, 2, 1, 3).reshape(b, n, INNER)
        return out @ Wo + bo

    def _L0_ffn_ref(x, w1, conv_w, conv_b, w2):
        import jax, jax.numpy as jnp
        import numpy as np
        B, S, D_MODEL, D_HIDDEN = (4, 512, 256, 1024)

        def act_quant(x):
            scale = 127.0 / jnp.clip(jnp.max(jnp.abs(x), axis=-1, keepdims=True), 1e-05)
            return jnp.clip(jnp.round(x * scale), -128, 127) / scale

        def weight_quant(w):
            scale = 1.0 / jnp.clip(jnp.mean(jnp.abs(w)), 1e-05)
            return jnp.clip(jnp.round(w * scale), -1, 1) / scale

        def bit_linear(x, w):
            xq = x + jax.lax.stop_gradient(act_quant(x) - x)
            wq = w + jax.lax.stop_gradient(weight_quant(w) - w)
            return jnp.einsum('bsd,hd->bsh', xq, wq)

        def depthwise_conv1d(x_bcl, w, b):
            y = jax.lax.conv_general_dilated(x_bcl, w, window_strides=(1,), padding=[(1, 1)], dimension_numbers=('NCH', 'OIH', 'NCH'), feature_group_count=x_bcl.shape[1])
            return y + b[None, :, None]
        h = bit_linear(x, w1)
        h = depthwise_conv1d(h.transpose(0, 2, 1), conv_w, conv_b)
        h = h.transpose(0, 2, 1)
        h = jax.nn.silu(h)
        return bit_linear(h, w2)

    def _L1_xattn_ref(q, k, v, Wq, bq, Wk, bk, Wv, bv, Wo, bo):
        import jax, jax.numpy as jnp
        import numpy as np
        D_MODEL = 256
        N_HEADS = 16
        HEAD_DIM = D_MODEL // N_HEADS

        def sparsemax(x):
            x = x - jnp.max(x, axis=-1, keepdims=True)
            zs = -jnp.sort(-x, axis=-1)
            L = x.shape[-1]
            rho = jnp.arange(1, L + 1, dtype=x.dtype)
            cssv = jnp.cumsum(zs, axis=-1) - 1.0
            support = zs > cssv / rho
            k = jnp.maximum(jnp.sum(support, axis=-1, keepdims=True), 1)
            tau = jnp.take_along_axis(cssv, k - 1, axis=-1) / k.astype(x.dtype)
            return jnp.clip(x - tau, 0.0)

        def _split_heads(x):
            B, L, _ = x.shape
            return x.reshape(B, L, N_HEADS, HEAD_DIM).transpose(0, 2, 1, 3)
        qh = _split_heads(q @ Wq + bq)
        kh = _split_heads(k @ Wk + bk)
        vh = _split_heads(v @ Wv + bv)
        scale = HEAD_DIM ** (-0.5)
        scores = jnp.einsum('bhqd,bhkd->bhqk', qh, kh) * scale
        attn = sparsemax(scores)
        out = jnp.einsum('bhqk,bhkd->bhqd', attn, vh)
        B, L = (q.shape[0], q.shape[1])
        out = out.transpose(0, 2, 1, 3).reshape(B, L, D_MODEL)
        return out @ Wo + bo

    def _L1_ffn_ref(x, w1, w2, w3, new_w1, new_w2, new_w3, gate_weight, new_gate_weight, gate_bias):
        import jax, jax.numpy as jnp
        import numpy as np
        TOP_K = 2
        ROUTE_SCALE = 1.0
        EPS = 1e-20
        bs, slen, dim = x.shape
        x_flat = x.reshape(-1, dim)
        ew1 = jnp.concatenate([w1, new_w1], axis=0)
        ew2 = jnp.concatenate([w2, new_w2], axis=0)
        ew3 = jnp.concatenate([w3, new_w3], axis=0)
        gate = jnp.concatenate([gate_weight, new_gate_weight], axis=0)
        e_orig = w1.shape[0]
        e_tot = gate.shape[0]
        bias = jnp.concatenate([jnp.zeros((e_orig,), x.dtype), gate_bias])
        scores = jax.nn.sigmoid((x_flat @ gate.T + bias).astype(jnp.float32))
        top_scores, selected = jax.lax.top_k(scores, TOP_K)
        top_scores = top_scores / (jnp.sum(top_scores, axis=-1, keepdims=True) + EPS)
        top_scores = top_scores * ROUTE_SCALE
        onehot = jax.nn.one_hot(selected, e_tot, dtype=jnp.float32)
        cw = jnp.einsum('tk,tke->te', top_scores, onehot)
        out = jnp.zeros_like(x_flat)
        for e in range(e_tot):
            h = jax.nn.silu(x_flat @ ew1[e].T) * (x_flat @ ew3[e].T)
            out = out + cw[:, e:e + 1] * (h @ ew2[e].T)
        return out.reshape(bs, slen, dim)

    def _L2_xattn_ref(slots, P, Wq, Wk, Wv, gru_wih, gru_whh, gru_bih, gru_bhh, slot_norm_w, input_norm_w):
        import jax, jax.numpy as jnp
        import numpy as np
        D = 256
        NUM_ITERS = 3
        EPS = 1e-06
        SCALE = D ** (-0.5)

        def rmsnorm(x, w, eps=EPS):
            return x * jax.lax.rsqrt(jnp.mean(x * x, axis=-1, keepdims=True) + eps) * w

        def gru_cell(x, h, wih, whh, bih, bhh):
            gx = x @ wih.T + bih
            gh = h @ whh.T + bhh
            xr, xz, xn = jnp.split(gx, 3, axis=-1)
            hr, hz, hn = jnp.split(gh, 3, axis=-1)
            r = jax.nn.sigmoid(xr + hr)
            z = jax.nn.sigmoid(xz + hz)
            n = jnp.tanh(xn + r * hn)
            return (1.0 - z) * n + z * h
        Pn = rmsnorm(P, input_norm_w)
        k_proj = Pn @ Wk.T
        v_proj = Pn @ Wv.T
        for _ in range(NUM_ITERS):
            sn = rmsnorm(slots, slot_norm_w)
            q_proj = sn @ Wq.T
            scores = jnp.einsum('bkd,bmd->bkm', q_proj, k_proj) * SCALE
            attn = jax.nn.softmax(scores, axis=-2)
            attn = attn / (jnp.sum(attn, axis=-1, keepdims=True) + EPS)
            updates = jnp.einsum('bkm,bmd->bkd', attn, v_proj)
            slots = gru_cell(updates, slots, gru_wih, gru_whh, gru_bih, gru_bhh)
        return slots

    def _L2_ffn_ref(src, Wq, bq, Wk, bk, Wv, bv, Wo, bo, gW, gb, W1, b1, W2, b2, ln1_g, ln1_b, ln2_g, ln2_b):
        import jax, jax.numpy as jnp
        import numpy as np
        D_MODEL = 256
        NHEAD = 16
        HEAD_DIM = D_MODEL // NHEAD
        FF = 512
        NUM_EXPERTS = 8
        EPS = 1e-05

        def _ln(x, g, b):
            m = x.mean(-1, keepdims=True)
            v = ((x - m) ** 2).mean(-1, keepdims=True)
            return (x - m) / jnp.sqrt(v + EPS) * g + b

        def _attention(src, Wq, bq, Wk, bk, Wv, bv, Wo, bo):
            B, T, d = src.shape
            scale = HEAD_DIM ** (-0.5)
            q = (src @ Wq + bq).reshape(B, T, NHEAD, HEAD_DIM)
            k = (src @ Wk + bk).reshape(B, T, NHEAD, HEAD_DIM)
            v = (src @ Wv + bv).reshape(B, T, NHEAD, HEAD_DIM)
            scores = jnp.einsum('bqhd,bkhd->bhqk', q, k) * scale
            probs = jax.nn.softmax(scores, axis=-1)
            out = jnp.einsum('bhqk,bkhd->bqhd', probs, v).reshape(B, T, d)
            return out @ Wo + bo

        def _moe(x, gW, gb, W1, b1, W2, b2):
            B, T, d = x.shape
            xf = x.reshape(-1, d)
            gates = jax.nn.softmax(xf @ gW + gb, axis=-1)
            top2_scores, top2_idx = jax.lax.top_k(gates, 2)
            w = (jax.nn.one_hot(top2_idx, NUM_EXPERTS, dtype=xf.dtype) * top2_scores[..., None]).sum(1)
            h = jax.nn.relu(jnp.einsum('nd,edf->enf', xf, W1) + b1[:, None, :])
            y = jnp.einsum('enf,efd->end', h, W2) + b2[:, None, :]
            out = jnp.einsum('ne,end->nd', w, y)
            return out.reshape(B, T, d)
        attn_out = _attention(src, Wq, bq, Wk, bk, Wv, bv, Wo, bo)
        x = _ln(src + attn_out, ln1_g, ln1_b)
        ff = _moe(x, gW, gb, W1, b1, W2, b2)
        return _ln(x + ff, ln2_g, ln2_b)

    def _L3_xattn_ref(input, memory, Wq, bq, Wk, bk, Wv, bv):
        import jax, jax.numpy as jnp
        import numpy as np
        DIM = 256
        NUM_HEADS = 16
        HEAD_DIM = DIM // NUM_HEADS

        def _split(x):
            b, l, _ = x.shape
            return x.reshape(b, l, NUM_HEADS, HEAD_DIM).transpose(0, 2, 1, 3)
        depth_scale = HEAD_DIM ** (-0.5)
        q = input @ Wq.T + bq
        k = memory @ Wk.T + bk
        v = memory @ Wv.T + bv
        q = _split(q) * depth_scale
        k = _split(k)
        v = _split(v)
        logit = jnp.einsum('bhnd,bhmd->bhnm', q, k)
        attn = jax.nn.softmax(logit, axis=-1)
        out = jnp.einsum('bhnm,bhmd->bhnd', attn, v)
        b, h, n, d = out.shape
        return out.transpose(0, 2, 1, 3).reshape(b, n, h * d)

    def _L3_ffn_ref(hidden_states, router_weight, e_bias, gate_w, up_w, down_w, sh_gate_w, sh_up_w, sh_down_w):
        import jax, jax.numpy as jnp
        import numpy as np
        B, S, H = (1, 512, 256)
        E, K = (16, 4)
        G, TG = (4, 2)
        I_MOE = 128
        N_SH = 2
        SCALE = 2.5

        def _mlp(x, gw, uw, dw):
            return jax.nn.silu(x @ gw.T) * (x @ uw.T) @ dw.T

        def _route(x2d, router_weight, e_bias):
            T = x2d.shape[0]
            scores = jax.nn.sigmoid(x2d @ router_weight.T)
            sc = scores + e_bias[None, :]
            group_scores = jnp.sum(jax.lax.top_k(sc.reshape(T, G, E // G), 2)[0], axis=-1)
            _, gidx = jax.lax.top_k(group_scores, TG)
            gmask = jnp.zeros((T, G), sc.dtype).at[jnp.arange(T)[:, None], gidx].set(1.0)
            smask = jnp.repeat(gmask, E // G, axis=1)
            masked = jnp.where(smask > 0, sc, 0.0)
            _, tidx = jax.lax.top_k(masked, K)
            tw = jnp.take_along_axis(scores, tidx, axis=1)
            tw = tw / (jnp.sum(tw, axis=-1, keepdims=True) + 1e-20)
            tw = tw * SCALE
            return (tidx, tw)

        def _moe_forward(hidden_states, router_weight, e_bias, gate_w, up_w, down_w, sh_gate_w, sh_up_w, sh_down_w):
            orig_shape = hidden_states.shape
            x = hidden_states.reshape(-1, H)
            T = x.shape[0]
            tidx, tw = _route(x, router_weight, e_bias)
            g = jnp.einsum('th,eih->tei', x, gate_w)
            u = jnp.einsum('th,eih->tei', x, up_w)
            h = jax.nn.silu(g) * u
            yo = jnp.einsum('tei,ehi->teh', h, down_w)
            combine = jnp.zeros((T, E), tw.dtype).at[jnp.arange(T)[:, None], tidx].add(tw)
            routed = jnp.einsum('te,teh->th', combine, yo)
            shared = _mlp(hidden_states.reshape(-1, H), sh_gate_w, sh_up_w, sh_down_w)
            return (routed + shared).reshape(orig_shape)
        return _moe_forward(hidden_states, router_weight, e_bias, gate_w, up_w, down_w, sh_gate_w, sh_up_w, sh_down_w)
    x = x + _L0_xattn_ref(_layernorm(x, axis=-1), ctx_1024, L0_xattn_cos, L0_xattn_sin, L0_xattn_ln_lat_g, L0_xattn_ln_lat_b, L0_xattn_ln_ctx_g, L0_xattn_ln_ctx_b, L0_xattn_Wq, L0_xattn_Wkv, L0_xattn_Wo, L0_xattn_bo)
    x = x + _L0_ffn_ref(_layernorm(x, axis=-1), L0_ffn_w1, L0_ffn_conv_w, L0_ffn_conv_b, L0_ffn_w2)
    x = x + _L1_xattn_ref(_layernorm(x, axis=-1), ctx_1024, ctx_1024, L1_xattn_Wq, L1_xattn_bq, L1_xattn_Wk, L1_xattn_bk, L1_xattn_Wv, L1_xattn_bv, L1_xattn_Wo, L1_xattn_bo)
    x = x + _L1_ffn_ref(_layernorm(x, axis=-1), L1_ffn_w1, L1_ffn_w2, L1_ffn_w3, L1_ffn_new_w1, L1_ffn_new_w2, L1_ffn_new_w3, L1_ffn_gate_weight, L1_ffn_new_gate_weight, L1_ffn_gate_bias)
    x = x + _L2_xattn_ref(_layernorm(x, axis=-1), ctx_1024, L2_xattn_Wq, L2_xattn_Wk, L2_xattn_Wv, L2_xattn_gru_wih, L2_xattn_gru_whh, L2_xattn_gru_bih, L2_xattn_gru_bhh, L2_xattn_slot_norm_w, L2_xattn_input_norm_w)
    x = x + _L2_ffn_ref(_layernorm(x, axis=-1), L2_ffn_Wq, L2_ffn_bq, L2_ffn_Wk, L2_ffn_bk, L2_ffn_Wv, L2_ffn_bv, L2_ffn_Wo, L2_ffn_bo, L2_ffn_gW, L2_ffn_gb, L2_ffn_W1, L2_ffn_b1, L2_ffn_W2, L2_ffn_b2, L2_ffn_ln1_g, L2_ffn_ln1_b, L2_ffn_ln2_g, L2_ffn_ln2_b)
    x = x + _L3_xattn_ref(_layernorm(x, axis=-1), ctx_1024, L3_xattn_Wq, L3_xattn_bq, L3_xattn_Wk, L3_xattn_bk, L3_xattn_Wv, L3_xattn_bv)
    x = x + _L3_ffn_ref(_layernorm(x, axis=-1), L3_ffn_router_weight, L3_ffn_e_bias, L3_ffn_gate_w, L3_ffn_up_w, L3_ffn_down_w, L3_ffn_sh_gate_w, L3_ffn_sh_up_w, L3_ffn_sh_down_w)
    return x

_drawn_inputs = setup_inputs


def setup_inputs(seed=0):
    import zlib

    import numpy as np

    out = dict(_drawn_inputs(seed))
    spreads = {'L0_xattn_ln_lat_g': (1.0, 0.6),
     'L0_xattn_ln_lat_b': (0.0, 0.609),
     'L0_xattn_ln_ctx_g': (1.0, 0.2),
     'L0_xattn_ln_ctx_b': (0.0, 0.1),
     'L0_xattn_bo': (0.0, 0.1),
     'L1_xattn_bq': (0.0, 0.316),
     'L1_xattn_bk': (0.0, 0.8),
     'L1_xattn_bv': (0.0, 0.293),
     'L1_xattn_bo': (0.0, 0.1),
     'L1_ffn_new_w2': (0.0, 0.1),
     'L2_xattn_gru_bih': (0.0, 0.1),
     'L2_xattn_gru_bhh': (0.0, 0.27),
     'L2_xattn_slot_norm_w': (1.0, 0.6),
     'L2_xattn_input_norm_w': (1.0, 0.2),
     'L2_ffn_bq': (0.0, 0.8),
     'L2_ffn_bk': (0.0, 0.8),
     'L2_ffn_bv': (0.0, 0.628),
     'L2_ffn_bo': (0.0, 0.1),
     'L2_ffn_gb': (0.0, 0.8),
     'L2_ffn_b1': (0.0, 0.8),
     'L2_ffn_b2': (0.0, 0.765),
     'L2_ffn_ln1_g': (1.0, 0.2),
     'L2_ffn_ln1_b': (0.0, 0.1),
     'L2_ffn_ln2_g': (1.0, 0.2),
     'L2_ffn_ln2_b': (0.0, 0.1),
     'L3_xattn_bq': (0.0, 0.8),
     'L3_xattn_bk': (0.0, 0.8),
     'L3_xattn_bv': (0.0, 0.1),
     'L3_ffn_e_bias': (0.0, 0.8)}
    factors = {'L0_xattn_cos': 5.79,
     'L0_xattn_sin': 5.785,
     'L1_ffn_w1': 3.826,
     'L1_ffn_w2': 3.784,
     'L1_ffn_w3': 3.795,
     'L1_ffn_gate_weight': 2.671,
     'L2_ffn_Wq': 8.0,
     'L2_ffn_Wk': 8.0,
     'L2_ffn_gW': 3.997,
     'L2_ffn_W1': 6.16,
     'L2_ffn_W2': 4.981,
     'L3_ffn_router_weight': 8.0,
     'L3_ffn_gate_w': 8.0,
     'L3_ffn_up_w': 8.0,
     'L3_ffn_down_w': 8.0,
     'L3_ffn_sh_gate_w': 8.0,
     'L3_ffn_sh_up_w': 8.0,
     'L3_ffn_sh_down_w': 8.0}
    for name, (base, spread) in spreads.items():
        noise = np.random.default_rng([zlib.crc32(name.encode()), seed]).standard_normal(out[name].shape)
        drawn = base * np.exp(spread * noise) if base else spread * noise
        out[name] = jnp.asarray(drawn.astype(out[name].dtype))
    for name, factor in factors.items():
        out[name] = (out[name] * factor).astype(out[name].dtype)
    return out
```

```python
import concourse.bass as bass
from concourse import mybir
from contextlib import ExitStack
import numpy as np

F32 = mybir.dt.float32
BF16 = mybir.dt.bfloat16
ALU = mybir.AluOpType
ACT = mybir.ActivationFunctionType
AX = mybir.AxisListType

P = 128
D = 256
KC = D // P
B = 2
NQ = 512
NT = B * NQ
TQ = NT // P
NK = 1024
TK = B * NK // P
BANK = 512
ROUND = 1.5 * 2.0 ** 23


class Stage:

    spent = []

    def __init__(self, nc, name):
        self.nc, self.name, self.stack = nc, name, ExitStack()

    def __enter__(self):
        return self

    def __exit__(self, *a):
        return self.stack.__exit__(*a)

    def sb(self, name, shape, dt=F32):
        return self.stack.enter_context(self.nc.sbuf_tensor(f"{self.name}_{name}_s", shape, dt))

    def sem(self, name):
        handle = self.nc.alloc_semaphore(f"{self.name}_{name}")
        Stage.spent.append(handle)
        return handle

    def block(self):
        return self.stack.enter_context(self.nc.Block())


def clear_semaphores(nc):
    nc.clear_and_free_semaphores(Stage.spent)
    Stage.spent = []
    nc.all_engine_barrier()


class Chain:

    def __init__(self, eng, sem, base=0):
        self.eng, self.sem, self.base, self.n = eng, sem, base, 0

    def done(self, ins):
        ins.then_inc(self.sem, 1)
        self.n += 1
        return self.n

    def wait(self):
        self.eng.wait_ge(self.sem, self.base + self.n)

    def link(self, ins):
        self.done(ins)
        self.wait()


def constants(nc, ident, ones, slot_sum):
    with Stage(nc, "const") as s:
        filled, made = s.sem("filled"), s.sem("made")
        block = s.block()

        @block.gpsimd
        def _(pool):
            pool.memset(ident[:, :], 0.0).then_inc(filled, 1)
            pool.memset(ones[:, :], 1.0).then_inc(filled, 1)
            pool.memset(slot_sum[:, :], 0.0).then_inc(filled, 1)
            pool.wait_ge(filled, 3)
            pool.affine_select(out=ident[:, :], in_=ident[:, :], compare_op=ALU.not_equal, fill=1.0, base=0,
                               pattern=[[-1, P]], channel_multiplier=1).then_inc(made, 1)
            v = slot_sum[:, :].rearrange("p (a c) -> p a c", a=4)
            pool.affine_select(out=v, in_=v, compare_op=ALU.not_equal, fill=1.0, base=-16,
                               pattern=[[-32, 4], [0, 32]], channel_multiplier=1).then_inc(made, 1)
            pool.wait_ge(made, 2)


def load_x(nc, x_dram, x_sb):
    with Stage(nc, "loadx") as s:
        loaded = s.sem("loaded")
        block = s.block()

        @block.sync
        def _(sp):
            sp.dma_start(x_sb[:, :, :], x_dram.rearrange("b (t p) d -> p (b t) d", p=P)).then_inc(loaded, 16)
            sp.wait_ge(loaded, 16)


def store_x(nc, x_sb, out_dram):
    with Stage(nc, "storex") as s:
        stored = s.sem("stored")
        block = s.block()

        @block.sync
        def _(sp):
            sp.dma_start(out_dram.rearrange("b (t p) d -> p (b t) d", p=P), x_sb[:, :, :]).then_inc(stored, 16)
            sp.wait_ge(stored, 16)


def normalize(nc, name, ps, ident, src, nt, dst_t, eps, norms=1, rms=False, gain_dram=None, shift_dram=None,
              keep=None, src_dram=None):
    with Stage(nc, name) as s:
        rows = keep if keep is not None else s.sb("rows", [P, nt, D])
        stats = s.sb("stats", [P, nt, 6])
        mv = s.sb("mv", [P, nt, 2])
        var_eps = s.sb("var_eps", [P, nt])
        dev = s.sb("dev", [P, nt])
        rstd = s.sb("rstd", [P, nt])
        gs = s.sb("gs", [P, 2, KC])
        loaded, src_loaded = s.sem("loaded"), s.sem("src_loaded")
        steps = s.sem("steps")
        var_ready = s.sem("var_ready")
        dev_ready = s.sem("dev_ready")
        rows_ready = s.sem("rows_ready")
        turned = s.sem("turned")
        copied = s.sem("copied")
        block = s.block()
        affine = gain_dram is not None

        @block.sync
        def _(sp):
            if src_dram is not None:
                sp.dma_start(src[:, :, :], src_dram).then_inc(src_loaded, 16)
            if affine:
                sp.dma_start(gs[:, 0, :], gain_dram).then_inc(loaded, 16)
                if shift_dram is not None:
                    sp.dma_start(gs[:, 1, :], shift_dram).then_inc(loaded, 16)

        @block.vector
        def _(dve):
            c = Chain(dve, steps)
            if src_dram is not None:
                dve.wait_ge(src_loaded, 16)
            for n in range(norms):
                x = src if n == 0 else rows
                for t in range(nt):
                    c.done(nc.vector.bn_stats(stats[:, t, :], x[:, t, :]))
                c.wait()
                for t in range(nt):
                    c.done(nc.vector.bn_aggr(mv[:, t, :], stats[:, t, :]))
                c.wait()
                if rms:
                    c.link(nc.vector.tensor_tensor(var_eps[:, :], mv[:, :, 0], mv[:, :, 0], ALU.mult))
                    c.link(nc.vector.tensor_tensor(dev[:, :], var_eps[:, :], mv[:, :, 1], ALU.add))
                    c.done(nc.vector.tensor_scalar(var_eps[:, :], dev[:, :], eps, None, ALU.add))
                else:
                    c.done(nc.vector.tensor_scalar(var_eps[:, :], mv[:, :, 1], eps, None, ALU.add))
                c.wait()
                nc.vector.sem_inc(var_ready, 1)
                dve.wait_ge(dev_ready, n + 1)
                c.link(nc.vector.reciprocal(rstd[:, :], dev[:, :]))
                for t in range(nt):
                    if rms:
                        ins = nc.vector.tensor_scalar(rows[:, t, :], x[:, t, :], rstd[:, t:t + 1], None, ALU.mult)
                    else:
                        ins = nc.vector.tensor_scalar(rows[:, t, :], x[:, t, :], mv[:, t, 0:1], rstd[:, t:t + 1],
                                                      ALU.subtract, ALU.mult)
                    c.done(ins)
                c.wait()
            nc.vector.sem_inc(rows_ready, 1)

        @block.tensor
        def _(pe):
            pe.wait_ge(rows_ready, 1)
            unit = 0
            for k in range(KC):
                for t4 in range(nt // 4):
                    if unit >= 4:
                        pe.wait_ge(copied, unit - 3)
                    for j in range(4):
                        t = 4 * t4 + j
                        ins = nc.tensor.transpose(ps[:, unit % 4, j * P:(j + 1) * P], rows[:, t, k * P:(k + 1) * P],
                                                  ident[:, :])
                    ins.then_inc(turned, 1)
                    unit += 1

        @block.scalar
        def _(act):
            for n in range(norms):
                act.wait_ge(var_ready, n + 1)
                nc.scalar.activation(dev[:, :], var_eps[:, :], ACT.Sqrt).then_inc(dev_ready, 1)
            if affine:
                act.wait_ge(loaded, 32 if shift_dram is not None else 16)
            unit = 0
            for k in range(KC):
                for t4 in range(nt // 4):
                    act.wait_ge(turned, unit + 1)
                    out = dst_t[:, k, t4 * BANK:(t4 + 1) * BANK]
                    if affine and shift_dram is not None:
                        ins = nc.scalar.activation(out, ps[:, unit % 4, :], ACT.Identity, bias=gs[:, 1, k:k + 1],
                                                   scale=gs[:, 0, k:k + 1])
                    elif affine:
                        ins = nc.scalar.activation(out, ps[:, unit % 4, :], ACT.Copy, scale=gs[:, 0, k:k + 1])
                    else:
                        ins = nc.scalar.activation(out, ps[:, unit % 4, :], ACT.Copy)
                    ins.then_inc(copied, 1)
                    unit += 1
            act.wait_ge(copied, unit)


def transpose_rows(nc, name, ps, ident, src, nt, dst_t, src_dram):
    with Stage(nc, name) as s:
        loaded = s.sem("loaded")
        turned, copied = s.sem("turned"), s.sem("copied")
        block = s.block()

        @block.sync
        def _(sp):
            sp.dma_start(src[:, :, :], src_dram).then_inc(loaded, 16)

        @block.tensor
        def _(pe):
            pe.wait_ge(loaded, 16)
            unit = 0
            for k in range(KC):
                for t4 in range(nt // 4):
                    if unit >= 4:
                        pe.wait_ge(copied, unit - 3)
                    for j in range(4):
                        t = 4 * t4 + j
                        ins = nc.tensor.transpose(ps[:, unit % 4, j * P:(j + 1) * P], src[:, t, k * P:(k + 1) * P],
                                                  ident[:, :])
                    ins.then_inc(turned, 1)
                    unit += 1

        @block.scalar
        def _(act):
            unit = 0
            for k in range(KC):
                for t4 in range(nt // 4):
                    act.wait_ge(turned, unit + 1)
                    nc.scalar.activation(dst_t[:, k, t4 * BANK:(t4 + 1) * BANK], ps[:, unit % 4, :],
                                         ACT.Copy).then_inc(copied, 1)
                    unit += 1
            act.wait_ge(copied, unit)


def project_out(nc, name, ps, o_all, ngroups, wo_dram, bo_dram, acc):
    with Stage(nc, name) as s:
        wo = s.sb("wo", [P, ngroups, D])
        bo = s.sb("bo", [P, D])
        w_loaded, b_loaded = s.sem("w_loaded"), s.sem("b_loaded")
        multiplied, added, biased = s.sem("multiplied"), s.sem("added"), s.sem("biased")
        block = s.block()

        @block.sync
        def _(sp):
            sp.dma_start(wo[:, :, :], wo_dram).then_inc(w_loaded, 16)
            if bo_dram is not None:
                sp.dma_start(bo[:, :], bo_dram.partition_broadcast(P)).then_inc(b_loaded, 16)

        @block.tensor
        def _(pe):
            pe.wait_ge(w_loaded, 16)
            for t in range(TQ):
                if t >= 4:
                    pe.wait_ge(added, t - 3)
                for g in range(ngroups):
                    ins = nc.tensor.matmul(ps[:, t % 4, 0:D], o_all[:, g, t * P:(t + 1) * P], wo[:, g, :],
                                           start=(g == 0), stop=(g == ngroups - 1))
                ins.then_inc(multiplied, 1)

        @block.vector
        def _(dve):
            if bo_dram is not None:
                dve.wait_ge(b_loaded, 16)
                for t in range(TQ):
                    nc.vector.tensor_tensor(acc[:, t, :], acc[:, t, :], bo[:, :], ALU.add).then_inc(biased, 1)
                dve.wait_ge(biased, TQ)
            for t in range(TQ):
                dve.wait_ge(multiplied, t + 1)
                nc.vector.tensor_tensor(acc[:, t, :], acc[:, t, :], ps[:, t % 4, 0:D], ALU.add).then_inc(added, 1)
            dve.wait_ge(added, TQ)


def rope_attention(nc, name, ps, ones, q_t, ctx_t, w_dram, cos_dram, sin_dram, o_all):
    DH = 64
    G = 8
    SCALE = DH ** -0.5
    NC_ = NK // P
    with Stage(nc, name) as s:
        w = s.sb("w", [P, 3, KC, P])
        qm = s.sb("qm", [P, 2, NQ])
        cos = s.sb("cos", [P, NK])
        sin = s.sb("sin", [P, NK])
        k_cos = s.sb("k_cos", [P, NK])
        k_sin = s.sb("k_sin", [P, NK])
        k_rot = s.sb("k_rot", [P, NK])
        v = s.sb("v", [P, NC_, P])
        clipped = s.sb("clipped", [P, 3, 2 * NQ])
        probs = s.sb("probs", [P, 3, 2 * NQ])
        rden = s.sb("rden", [P, NQ])
        tables, zeroed, negated = s.sem("tables"), s.sem("zeroed"), s.sem("negated")
        w_loaded, w_free = s.sem("w_loaded"), s.sem("w_free")
        qkv_made = s.sem("qkv_made")
        q_ready, k_ready, v_ready = s.sem("q_ready"), s.sem("k_ready"), s.sem("v_ready")
        kparts = s.sem("kparts")
        scored = s.sem("scored")
        clip_done = s.sem("clip_done")
        exp_done = s.sem("exp_done")
        pv_done = s.sem("pv_done")
        rden_ready, o_done = s.sem("rden_ready"), s.sem("o_done")
        block = s.block()

        @block.sync
        def _(sp):
            for j in range(4):
                sp.dma_start(cos[32 * j:32 * j + 32, :], cos_dram).then_inc(tables, 16)
                sp.dma_start(sin[32 * j:32 * j + 32, :], sin_dram).then_inc(tables, 16)
            for b in range(B):
                with sp.Fori(0, G) as g:
                    sp.wait_ge(w_free, g + (b * G + 1))
                    sp.dma_start(w[:, :, :, :], w_dram[bass.ds(g, 1)].rearrange("a p k c n -> (a p) k c n")
                                 ).then_inc(w_loaded, 16)

        @block.tensor
        def _(pe):
            pe.wait_ge(zeroed, 1)
            nc.tensor.sem_inc(w_free, 1)
            for b in range(B):
                with pe.Fori(0, G) as g:
                    it = g + b * G
                    pe.wait_ge(w_loaded, 16 * it + 16)
                    pe.wait_ge(o_done, it + 1)
                    for c in range(KC):
                        nc.tensor.matmul(ps[:, 0, :], w[:, 0, c, :], q_t[:, c, b * NQ:(b + 1) * NQ],
                                         start=(c == 0), stop=(c == KC - 1))
                    for h in range(2):
                        for c in range(KC):
                            nc.tensor.matmul(ps[:, 1 + h, :], w[:, 1, c, :],
                                             ctx_t[:, c, b * NK + h * BANK:b * NK + (h + 1) * BANK],
                                             start=(c == 0), stop=(c == KC - 1))
                    for t in range(NC_):
                        for c in range(KC):
                            ins = nc.tensor.matmul(ps[:, 3 + t // 4, (t % 4) * P:(t % 4 + 1) * P],
                                                   ctx_t[:, c, b * NK + t * P:b * NK + (t + 1) * P], w[:, 2, c, :],
                                                   start=(c == 0), stop=(c == KC - 1))
                    ins.then_inc(qkv_made, 1)
                    pe.wait_ge(qkv_made, it + 1)
                    nc.tensor.sem_inc(w_free, 1)
                    pe.wait_ge(q_ready, it + 1)
                    pe.wait_ge(k_ready, it + 1)
                    pe.wait_ge(v_ready, it + 1)

                    def value_product(t):
                        pe.wait_ge(exp_done, it * NC_ + t + 1)
                        for h in range(2):
                            nc.tensor.matmul(ps[64 * h:64 * h + 64, 6, :], v[:, t, 64 * h:64 * h + 64],
                                             probs[:, t % 3, h * NQ:(h + 1) * NQ], start=(t == 0), stop=(t == NC_ - 1))
                        for h in range(2):
                            ins = nc.tensor.matmul(ps[64 * h:64 * h + 64, 7, :], ones[:, 0:64],
                                                   probs[:, t % 3, h * NQ:(h + 1) * NQ],
                                                   start=(t == 0), stop=(t == NC_ - 1))
                        ins.then_inc(pv_done, 1)

                    for t in range(NC_):
                        if t >= 3:
                            pe.wait_ge(clip_done, it * NC_ + t - 2)
                        for h in range(2):
                            ins = nc.tensor.matmul(ps[:, 2 * (t % 3) + h, :], k_rot[:, t * P:(t + 1) * P], qm[:, h, :],
                                                   start=True, stop=True)
                        ins.then_inc(scored, 1)
                        if t >= 2:
                            value_product(t - 2)
                    value_product(NC_ - 2)
                    value_product(NC_ - 1)

        @block.vector
        def _(dve):
            nc.vector.memset(qm[:, :, :], 0.0).then_inc(zeroed, 1)
            dve.wait_ge(tables, 8 * 16)
            nc.vector.tensor_scalar(sin[32:64, :], sin[32:64, :], -1.0, None, ALU.mult).then_inc(negated, 1)
            nc.vector.tensor_scalar(sin[96:128, :], sin[96:128, :], -1.0, None, ALU.mult).then_inc(negated, 1)
            dve.wait_ge(negated, 2)
            dve.wait_ge(zeroed, 1)
            nc.vector.sem_inc(o_done, 1)
            for b in range(B):
                with dve.Fori(0, G) as g:
                    it = g + b * G
                    dve.wait_ge(qkv_made, it + 1)
                    for h in range(2):
                        ins = nc.vector.tensor_scalar(qm[64 * h:64 * h + 64, h, :], ps[64 * h:64 * h + 64, 0, :],
                                                      SCALE, None, ALU.mult)
                    ins.then_inc(q_ready, 1)
                    k_ps = ps[:, 1:3, :].rearrange("p a n -> p (a n)")
                    nc.vector.tensor_tensor(k_cos[:, :], cos[:, :], k_ps, ALU.mult).then_inc(kparts, 1)
                    for j in range(4):
                        i = j ^ 1
                        nc.vector.tensor_tensor(k_sin[32 * j:32 * j + 32, :], k_ps[32 * i:32 * i + 32, :],
                                                sin[32 * i:32 * i + 32, :], ALU.mult).then_inc(kparts, 1)
                    dve.wait_ge(kparts, 5 * it + 5)
                    nc.vector.tensor_tensor(k_rot[:, :], k_cos[:, :], k_sin[:, :], ALU.add).then_inc(k_ready, 1)
                    for t in range(NC_):
                        dve.wait_ge(scored, it * NC_ + t + 1)
                        if t >= 3:
                            dve.wait_ge(exp_done, it * NC_ + t - 2)
                        nc.vector.tensor_scalar(
                            clipped[:, t % 3, :], ps[:, 2 * (t % 3):2 * (t % 3) + 2, :].rearrange("p a n -> p (a n)"),
                            11.0, -11.0, ALU.min, ALU.max).then_inc(clip_done, 1)
                    dve.wait_ge(pv_done, it * NC_ + NC_)
                    nc.vector.reciprocal(rden[:, :], ps[:, 7, :]).then_inc(rden_ready, 1)
                    dve.wait_ge(rden_ready, it + 1)
                    nc.vector.tensor_tensor(o_all[:, bass.ds(g, 1), b * NQ:(b + 1) * NQ].rearrange("p a n -> p (a n)"),
                                            ps[:, 6, :], rden[:, :], ALU.mult).then_inc(o_done, 1)
            dve.wait_ge(o_done, B * G + 1)

        @block.scalar
        def _(act):
            for b in range(B):
                with act.Fori(0, G) as g:
                    it = g + b * G
                    act.wait_ge(qkv_made, it + 1)
                    nc.scalar.activation(v[:, :, :].rearrange("p t n -> p (t n)"),
                                         ps[:, 3:5, :].rearrange("p a n -> p (a n)"), ACT.Copy).then_inc(v_ready, 1)
                    for t in range(NC_):
                        act.wait_ge(clip_done, it * NC_ + t + 1)
                        if t >= 3:
                            act.wait_ge(pv_done, it * NC_ + t - 2)
                        nc.scalar.activation(probs[:, t % 3, :], clipped[:, t % 3, :], ACT.Exp).then_inc(exp_done, 1)


def slot_attention(nc, name, ps, ident, slot_sum, q_t, kv_t, nk, w_dram, b_dram, o_all, sparse, newton=8):
    G, S, DH = 4, 4, 16
    SCALE = DH ** -0.5
    NC_ = nk // P
    NH = nk // BANK
    QT = NQ // P
    ROWS = S * QT
    UNITS = NC_ * 2
    W = 2 * KC * P + KC * S * DH
    CAND = (nk // P) * 8
    with Stage(nc, name) as s:
        w = s.sb("w", [P, W])
        bias = s.sb("bias", [P, 3])
        wq = w[:, 0:KC * P].rearrange("p (c n) -> p c n", c=KC)
        wk = w[:, KC * P:2 * KC * P].rearrange("p (c n) -> p c n", c=KC)
        wv = w[:, 2 * KC * P:W].rearrange("p (c n) -> p c n", c=KC)
        qm = s.sb("qm", [P, S, NQ])
        k = s.sb("k", [P, nk])
        v = s.sb("v", [P, NC_, S, 32])
        shift = s.sb("shift", [P, ROWS])
        shift_t = s.sb("shift_t", [ROWS, P])
        probs = s.sb("probs", [P, 4, 2 * NQ])
        o_raw = s.sb("o_raw", [P, NQ])
        rden = s.sb("rden", [P, NQ])
        o_scaled = s.sb("o_scaled", [P, NQ])
        if sparse:
            sc = s.sb("sc", [P, ROWS, nk])
            cand = s.sb("cand", [P, ROWS, CAND])
            above = s.sb("above", [P, ROWS, CAND])
            picked = s.sb("picked", [P, ROWS, CAND])
            count = s.sb("count", [P, ROWS])
            total = s.sb("total", [P, ROWS])
            rcount = s.sb("rcount", [P, ROWS])
            tau = s.sb("tau", [P, ROWS])
            ntau = s.sb("ntau", [P, ROWS])
            over = s.sb("over", [P, nk])
            over2 = s.sb("over2", [P, nk])
        zeroed = s.sem("zeroed")
        w_loaded, w_free = s.sem("w_loaded"), s.sem("w_free")
        qkv_made = s.sem("qkv_made")
        q_ready, k_ready, v_ready = s.sem("q_ready"), s.sem("k_ready"), s.sem("v_ready")
        rows_made = s.sem("rows_made")
        rows_used = s.sem("rows_used")
        rows_kept = s.sem("rows_kept")
        shift_ready = s.sem("shift_ready")
        shift_turned = s.sem("shift_turned")
        shift_copied = s.sem("shift_copied")
        shift_placed = s.sem("shift_placed")
        scored = s.sem("scored")
        exp_done = s.sem("exp_done")
        pv_done = s.sem("pv_done")
        o_copied, o_summed = s.sem("o_copied"), s.sem("o_summed")
        steps = s.sem("steps")
        o_done = s.sem("o_done")
        if sparse:
            rows_seen = s.sem("rows_seen")
            tau_set = s.sem("tau_set")
            summed = s.sem("summed")
        block = s.block()

        @block.sync
        def _(sp):
            for b in range(B):
                with sp.Fori(0, G) as g:
                    it = g + b * G
                    sp.wait_ge(w_free, it + 1)
                    sp.wait_ge(o_done, it + 1)
                    sp.dma_start(w[:, :], w_dram[bass.ds(g, 1)].rearrange("a p n -> (a p) n")).then_inc(w_loaded, 16)
                    sp.dma_start(bias[:, :], b_dram[bass.ds(g, 1)].rearrange("a p n -> (a p) n")
                                 ).then_inc(w_loaded, 16)
                    sp.wait_ge(shift_copied, it + 1)
                    for h in range(S):
                        sp.dma_start(qm[32 * h + DH:32 * h + DH + 1, h, :],
                                     shift_t[h * QT:(h + 1) * QT, :]).then_inc(shift_placed, 16)

        @block.tensor
        def _(pe):
            pe.wait_ge(zeroed, 2)
            nc.tensor.sem_inc(w_free, 1)
            for b in range(B):
                with pe.Fori(0, G) as g:
                    it = g + b * G
                    pe.wait_ge(w_loaded, 32 * it + 32)
                    pe.wait_ge(o_done, it + 1)
                    for c in range(KC):
                        nc.tensor.matmul(ps[:, 0, :], wq[:, c, :], q_t[:, c, b * NQ:(b + 1) * NQ],
                                         start=(c == 0), stop=(c == KC - 1))
                    for h in range(NH):
                        for c in range(KC):
                            nc.tensor.matmul(ps[:, 1 + h, :], wk[:, c, :],
                                             kv_t[:, c, b * nk + h * BANK:b * nk + (h + 1) * BANK],
                                             start=(c == 0), stop=(c == KC - 1))
                    for t in range(NC_):
                        for c in range(KC):
                            ins = nc.tensor.matmul(ps[:, 3, t * S * DH:(t + 1) * S * DH],
                                                   kv_t[:, c, b * nk + t * P:b * nk + (t + 1) * P], wv[:, c, :],
                                                   start=(c == 0), stop=(c == KC - 1))
                    ins.then_inc(qkv_made, 1)
                    pe.wait_ge(qkv_made, it + 1)
                    nc.tensor.sem_inc(w_free, 1)
                    pe.wait_ge(q_ready, it + 1)
                    pe.wait_ge(k_ready, it + 1)
                    for r in range(ROWS):
                        if r >= 2:
                            pe.wait_ge(rows_used, it * ROWS + r - 1)
                            if sparse:
                                pe.wait_ge(rows_kept, it * ROWS + r - 1)
                        h, t = r // QT, r % QT
                        for j in range(NH):
                            ins = nc.tensor.matmul(ps[:, 4 + 2 * (r % 2) + j, :], qm[:, h, t * P:(t + 1) * P],
                                                   k[:, j * BANK:(j + 1) * BANK], start=True, stop=True)
                        ins.then_inc(rows_made, 1)
                    pe.wait_ge(shift_ready, it + 1)
                    nc.tensor.transpose(ps[0:ROWS, 0, 0:P], shift[:, :], ident[:, :]).then_inc(shift_turned, 1)
                    pe.wait_ge(shift_placed, 64 * it + 64)
                    pe.wait_ge(v_ready, it + 1)

                    def value_products(t):
                        pe.wait_ge(exp_done, it * UNITS + 2 * t + 2)
                        for h in range(S):
                            ins = nc.tensor.matmul(ps[32 * h:32 * h + 32, 1, :], v[:, t, h, :],
                                                   probs[:, (2 * t + h // 2) % 4, (h % 2) * NQ:(h % 2 + 1) * NQ],
                                                   start=(t == 0), stop=(t == NC_ - 1))
                        ins.then_inc(pv_done, 1)

                    for u in range(UNITS):
                        t = u // 2
                        if u >= 2:
                            pe.wait_ge(exp_done, it * UNITS + u - 1)
                        for j in range(2):
                            ins = nc.tensor.matmul(ps[:, 4 + 2 * (u % 2) + j, :], k[:, t * P:(t + 1) * P],
                                                   qm[:, 2 * (u % 2) + j, :], start=True, stop=True)
                        ins.then_inc(scored, 1)
                        if u % 2 == 1 and t >= 1:
                            value_products(t - 1)
                    value_products(NC_ - 1)
                    pe.wait_ge(o_copied, it + 1)
                    nc.tensor.matmul(ps[:, 2, :], slot_sum[:, :], o_raw[:, :], start=True, stop=True
                                     ).then_inc(o_summed, 1)

        STEPS = 3 + (threshold_steps(newton, ROWS) if sparse else 0)

        @block.vector
        def _(dve):
            nc.vector.memset(qm[:, :, :], 0.0).then_inc(zeroed, 1)
            nc.vector.memset(v[:, :, :, :], 0.0).then_inc(zeroed, 1)
            dve.wait_ge(zeroed, 2)
            nc.vector.memset(v[:, :, :, DH:DH + 1], 1.0).then_inc(o_done, 1)
            for b in range(B):
                with dve.Fori(0, G) as g:
                    it = g + b * G
                    own = Chain(dve, steps, it * STEPS)
                    dve.wait_ge(qkv_made, it + 1)
                    for h in range(S):
                        ins = nc.vector.tensor_scalar(qm[32 * h:32 * h + 32, h, :], ps[32 * h:32 * h + 32, 0, :],
                                                      bias[32 * h:32 * h + 32, 0:1], SCALE, ALU.add, ALU.mult)
                    ins.then_inc(q_ready, 1)
                    nc.vector.tensor_scalar(k[:, :], ps[:, 1:1 + NH, :].rearrange("p a n -> p (a n)"), bias[:, 1:2],
                                            None, ALU.add).then_inc(k_ready, 1)
                    for r in range(ROWS):
                        dve.wait_ge(rows_made, it * ROWS + r + 1)
                        row = ps[:, 4 + 2 * (r % 2):4 + 2 * (r % 2) + NH, :].rearrange("p a n -> p (a n)")
                        if sparse:
                            nc.vector.sem_inc(rows_seen, 1)
                            for j in range(nk // P):
                                ins = nc.vector.max(cand[:, r, 8 * j:8 * j + 8], row[:, j * P:(j + 1) * P])
                        else:
                            ins = nc.vector.reduce_max(shift[:, r:r + 1], row, AX.X)
                        ins.then_inc(rows_used, 1)
                    if sparse:
                        dve.wait_ge(rows_used, it * ROWS + ROWS)
                        thresholds(nc, dve, own, it, cand, above, picked, count, total, rcount, tau, ntau, over, over2,
                                   sc, rows_kept, tau_set, summed, shift, newton, ROWS, nk)
                        nc.vector.sem_inc(shift_ready, 1)
                    else:
                        dve.wait_ge(rows_used, it * ROWS + ROWS)
                        nc.vector.sem_inc(shift_ready, 1)
                    dve.wait_ge(o_summed, it + 1)
                    own.link(nc.vector.reciprocal(rden[:, :], ps[:, 2, :]))
                    own.link(nc.vector.tensor_tensor(o_scaled[:, :], o_raw[:, :], rden[:, :], ALU.mult))
                    own.link(nc.vector.tensor_scalar(
                        o_all[:, bass.ds(g, 1), b * NQ:(b + 1) * NQ].rearrange("p a n -> p (a n)"), o_scaled[:, :],
                        bias[:, 2:3], None, ALU.add))
                    nc.vector.sem_inc(o_done, 1)
                    assert own.n == STEPS, own.n

        @block.scalar
        def _(act):
            for b in range(B):
                with act.Fori(0, G) as g:
                    it = g + b * G
                    act.wait_ge(qkv_made, it + 1)
                    nc.scalar.activation(v[:, :, :, 0:DH],
                                         ps[:, 3, 0:NC_ * S * DH].rearrange("p (t h n) -> p t h n", t=NC_, h=S),
                                         ACT.Copy).then_inc(v_ready, 1)
                    if sparse:
                        for r in range(ROWS):
                            act.wait_ge(rows_made, it * ROWS + r + 1)
                            act.wait_ge(rows_used, it * ROWS + r + 1)
                            row = ps[:, 4 + 2 * (r % 2):4 + 2 * (r % 2) + NH, :].rearrange("p a n -> p (a n)")
                            nc.scalar.activation(sc[:, r, :], row, ACT.Copy).then_inc(rows_kept, 1)
                        act.wait_ge(rows_kept, it * ROWS + ROWS)
                        for n in range(newton):
                            act.wait_ge(tau_set, it * newton + n + 1)
                            for r in range(ROWS):
                                if r or n:
                                    act.wait_ge(summed, it * newton * ROWS + n * ROWS + r)
                                nc.scalar.activation(over[:, :], sc[:, r, :], ACT.Relu, bias=ntau[:, r:r + 1],
                                                     accum_out=total[:, r:r + 1]).then_inc(summed, 1)
                    act.wait_ge(shift_turned, it + 1)
                    nc.scalar.activation(shift_t[:, :], ps[0:ROWS, 0, 0:P], ACT.Copy, scale=-1.0
                                         ).then_inc(shift_copied, 1)
                    for u in range(UNITS):
                        act.wait_ge(scored, it * UNITS + u + 1)
                        if u >= 4:
                            act.wait_ge(pv_done, it * NC_ + u // 2 - 1)
                        nc.scalar.activation(probs[:, u % 4, :],
                                             ps[:, 4 + 2 * (u % 2):6 + 2 * (u % 2), :].rearrange("p a n -> p (a n)"),
                                             ACT.Relu if sparse else ACT.Exp).then_inc(exp_done, 1)
                    act.wait_ge(pv_done, it * NC_ + NC_)
                    nc.scalar.activation(o_raw[:, :], ps[:, 1, :], ACT.Copy).then_inc(o_copied, 1)


CANDIDATE_STEPS = 20


def threshold_steps(newton, rows):
    return 2 + 6 * CANDIDATE_STEPS + 1 + newton * (rows + 4) + 1


def thresholds(nc, dve, own, it, cand, above, picked, count, total, rcount, tau, ntau, over, over2, sc, rows_kept,
               tau_set, summed, shift, newton, rows, nk):
    CAND = cand.shape[2]

    def wide(a):
        return a[:, :].unsqueeze(2).to_broadcast([P, rows, CAND])

    own.link(nc.vector.reduce_max(tau[:, :], cand[:, :, :], AX.X))
    own.link(nc.vector.tensor_scalar(tau[:, :], tau[:, :], -1.0, None, ALU.add))
    for n in range(CANDIDATE_STEPS):
        own.link(nc.vector.tensor_tensor(above[:, :, :], cand[:, :, :], wide(tau), ALU.is_gt))
        own.done(nc.vector.tensor_tensor(picked[:, :, :], above[:, :, :], cand[:, :, :], ALU.mult))
        own.link(nc.vector.reduce_sum(count[:, :], above[:, :, :], AX.X))
        own.done(nc.vector.reduce_sum(total[:, :], picked[:, :, :], AX.X))
        own.link(nc.vector.reciprocal(rcount[:, :], count[:, :]))
        own.link(nc.vector.scalar_tensor_tensor(tau[:, :], total[:, :], -1.0, rcount[:, :], ALU.add, ALU.mult))
    own.link(nc.vector.tensor_scalar(ntau[:, :], tau[:, :], -1.0, None, ALU.mult))
    dve.wait_ge(rows_kept, it * rows + rows)
    for n in range(newton):
        nc.vector.sem_inc(tau_set, 1)
        for r in range(rows):
            own.done(nc.vector.tensor_scalar(over2[:, :], sc[:, r, :], tau[:, r:r + 1], 0.0, ALU.is_gt, ALU.add,
                                             accum_out=count[:, r:r + 1]))
            own.wait()
        own.link(nc.vector.reciprocal(rcount[:, :], count[:, :]))
        dve.wait_ge(summed, it * newton * rows + (n + 1) * rows)
        own.link(nc.vector.scalar_tensor_tensor(total[:, :], total[:, :], -1.0, rcount[:, :], ALU.add, ALU.mult))
        own.link(nc.vector.tensor_tensor(tau[:, :], tau[:, :], total[:, :], ALU.add))
        own.link(nc.vector.tensor_scalar(ntau[:, :], tau[:, :], -1.0, None, ALU.mult))
    own.link(nc.vector.tensor_copy(shift[:, :], tau[:, :]))


LOW, HIGH = -3.0e38, 3.0e38


def top_mask(nc, own, vals, n, k, buf, top, mask):
    tiles = vals.shape[1]
    own.link(nc.vector.memset(buf[:, :, :], LOW))
    own.link(nc.vector.tensor_copy(buf[:, :, 0:n], vals))
    for t in range(tiles):
        own.done(nc.vector.max(top[:, t, :], buf[:, t, :]))
    own.wait()
    own.link(nc.vector.memset(top[:, :, k:8], LOW))
    for t in range(tiles):
        own.done(nc.vector.match_replace(out=buf[:, t, :], in_to_replace=top[:, t, :], in_values=buf[:, t, :],
                                         imm_value=HIGH))
    own.wait()
    own.link(nc.vector.tensor_scalar(mask, buf[:, :, 0:n], HIGH, None, ALU.is_equal))


def route(nc, name, ps, x_t, n, w_dram, bias_dram, kind, cw):
    with Stage(nc, name) as s:
        w = s.sb("w", [P, KC, n])
        bias = s.sb("bias", [P, n])
        logits = s.sb("logits", [P, TQ, n])
        scores = s.sb("scores", [P, TQ, n])
        picked = s.sb("picked", [P, TQ, n])
        mask = s.sb("mask", [P, TQ, n])
        buf = s.sb("buf", [P, TQ, 24])
        top = s.sb("top", [P, TQ, 8])
        total = s.sb("total", [P, TQ])
        rtotal = s.sb("rtotal", [P, TQ])
        if kind == "grouped":
            low_high = s.sb("low_high", [P, TQ, 4, 2, 2])
            best = s.sb("best", [P, TQ, 4])
            gmask = s.sb("gmask", [P, TQ, 4])
            gbuf = s.sb("gbuf", [P, TQ, 16])
            biased = s.sb("biased", [P, TQ, n])
            masked = s.sb("masked", [P, TQ, n])
        loaded, made = s.sem("loaded"), s.sem("made")
        logits_ready, scores_ready, steps = s.sem("logits_ready"), s.sem("scores_ready"), s.sem("steps")
        block = s.block()

        def wide(a, m):
            return a.unsqueeze(2).to_broadcast([P, TQ, m])

        @block.sync
        def _(sp):
            sp.dma_start(w[:, :, :], w_dram).then_inc(loaded, 16)
            sp.dma_start(bias[:, :], bias_dram.partition_broadcast(P)).then_inc(loaded, 16)

        @block.tensor
        def _(pe):
            pe.wait_ge(loaded, 32)
            for t in range(TQ):
                for c in range(KC):
                    ins = nc.tensor.matmul(ps[:, 0, t * n:(t + 1) * n], x_t[:, c, t * P:(t + 1) * P], w[:, c, :],
                                           start=(c == 0), stop=(c == KC - 1))
            ins.then_inc(made, 1)

        @block.scalar
        def _(act):
            act.wait_ge(logits_ready, 1)
            nc.scalar.activation(scores[:, :, :], logits[:, :, :], ACT.Exp if kind == "softmax" else ACT.Sigmoid
                                 ).then_inc(scores_ready, 1)

        @block.vector
        def _(dve):
            own = Chain(dve, steps)
            dve.wait_ge(loaded, 32)
            dve.wait_ge(made, 1)
            all_logits = ps[:, 0, 0:TQ * n].rearrange("p (t n) -> p t n", t=TQ)
            row_bias = bias[:, :].unsqueeze(1).to_broadcast([P, TQ, n])
            if kind == "grouped":
                own.link(nc.vector.tensor_copy(logits[:, :, :], all_logits))
            else:
                own.link(nc.vector.tensor_tensor(logits[:, :, :], row_bias, all_logits, ALU.add))
            if kind == "softmax":
                own.link(nc.vector.reduce_max(total[:, :], logits[:, :, :], AX.X))
                own.link(nc.vector.tensor_tensor(logits[:, :, :], logits[:, :, :], wide(total[:, :], n),
                                                 ALU.subtract))
            nc.vector.sem_inc(logits_ready, 1)
            dve.wait_ge(scores_ready, 1)
            if kind == "softmax":
                own.link(nc.vector.reduce_sum(total[:, :], scores[:, :, :], AX.X))
                own.link(nc.vector.reciprocal(rtotal[:, :], total[:, :]))
                own.link(nc.vector.tensor_tensor(scores[:, :, :], scores[:, :, :], wide(rtotal[:, :], n), ALU.mult))
                top_mask(nc, own, scores[:, :, :], n, 2, buf, top, mask[:, :, :])
                own.link(nc.vector.tensor_tensor(cw[:, :, 0:n], scores[:, :, :], mask[:, :, :], ALU.mult))
                return
            if kind == "top2":
                top_mask(nc, own, scores[:, :, :], n, 2, buf, top, mask[:, :, :])
                factor = 1.0
            else:
                own.link(nc.vector.tensor_tensor(biased[:, :, :], scores[:, :, :], row_bias, ALU.add))
                v = biased[:, :, :].rearrange("p t (g a c) -> p (t g) a c", g=4, a=2)
                lh = low_high[:, :, :, :, :].rearrange("p t g a c -> p (t g) a c")
                own.done(nc.vector.tensor_tensor(lh[:, :, 0, :], v[:, :, :, 0], v[:, :, :, 1], ALU.add))
                own.link(nc.vector.tensor_tensor(lh[:, :, 1, :], v[:, :, :, 0], v[:, :, :, 1], ALU.max))
                b4 = best[:, :, :].rearrange("p t g -> p (t g)")
                own.link(nc.vector.tensor_tensor(b4, lh[:, :, 1, 0], lh[:, :, 1, 1], ALU.add))
                own.link(nc.vector.tensor_tensor(b4, b4, lh[:, :, 0, 0], ALU.max))
                own.link(nc.vector.tensor_tensor(b4, b4, lh[:, :, 0, 1], ALU.max))
                top_mask(nc, own, best[:, :, :], 4, 2, gbuf, top, gmask[:, :, :])
                own.link(nc.vector.tensor_tensor(
                    masked[:, :, :].rearrange("p t (g c) -> p (t g) c", g=4),
                    biased[:, :, :].rearrange("p t (g c) -> p (t g) c", g=4),
                    gmask[:, :, :].rearrange("p t g -> p (t g)").unsqueeze(2).to_broadcast([P, TQ * 4, 4]),
                    ALU.mult))
                top_mask(nc, own, masked[:, :, :], n, 4, buf, top, mask[:, :, :])
                factor = 2.5
            own.link(nc.vector.tensor_tensor(picked[:, :, :], scores[:, :, :], mask[:, :, :], ALU.mult))
            own.link(nc.vector.reduce_sum(total[:, :], picked[:, :, :], AX.X))
            own.link(nc.vector.tensor_scalar(total[:, :], total[:, :], 1e-20, None, ALU.add))
            own.link(nc.vector.reciprocal(rtotal[:, :], total[:, :]))
            if factor != 1.0:
                own.link(nc.vector.tensor_scalar(rtotal[:, :], rtotal[:, :], factor, None, ALU.mult))
            own.link(nc.vector.tensor_tensor(cw[:, :, 0:n], picked[:, :, :], wide(rtotal[:, :], n), ALU.mult))
            if cw.shape[2] > n:
                own.link(nc.vector.memset(cw[:, :, n:], 1.0))


def experts(nc, name, ps, x_t, rounds, per_round, chunks, gated, up_dram, down_dram, b1_dram, cw, acc):
    CH = per_round * chunks
    WAYS = 2 if gated else 1
    HALVES = NT // BANK
    UNITS = HALVES * CH
    OUTS = TQ * per_round
    with Stage(nc, name) as s:
        up = s.sb("up", [P, KC, WAYS, CH, P])
        down = s.sb("down", [P, CH, D])
        b1 = s.sb("b1", [P, rounds * CH])
        act_out = s.sb("act_out", [P, 2, BANK])
        h = s.sb("h", [P, CH, NT])
        b1_loaded = s.sem("b1_loaded")
        unit_seen = s.sem("unit_seen")
        up_loaded, up_free = s.sem("up_loaded"), s.sem("up_free")
        down_loaded, down_free = s.sem("down_loaded"), s.sem("down_free")
        upped = s.sem("upped")
        activated = s.sem("activated")
        h_ready = s.sem("h_ready")
        downed = s.sem("downed")
        added = s.sem("added")
        block = s.block()

        @block.sync
        def _(sp):
            if b1_dram is not None:
                sp.dma_start(b1[:, :], b1_dram).then_inc(b1_loaded, 16)
            with sp.Fori(0, rounds) as i:
                sp.wait_ge(up_free, i + 1)
                sp.dma_start(up[:, :, :, :, :].rearrange("p k w c n -> p (k w c n)"),
                             up_dram[bass.ds(i, 1)].rearrange("a p n -> (a p) n")).then_inc(up_loaded, 16)
                sp.wait_ge(down_free, i + 1)
                sp.dma_start(down[:, :, :].rearrange("p c n -> p (c n)"),
                             down_dram[bass.ds(i, 1)].rearrange("a p n -> (a p) n")).then_inc(down_loaded, 16)

        @block.tensor
        def _(pe):
            nc.tensor.sem_inc(up_free, 1)
            nc.tensor.sem_inc(down_free, 1)
            nc.tensor.sem_inc(added, 4)
            nc.tensor.sem_inc(h_ready, 2)
            with pe.Fori(0, rounds) as i:
                pe.wait_ge(up_loaded, 16 * i + 16)
                for u in range(UNITS):
                    half, c = u // CH, u % CH
                    pe.wait_ge(h_ready, UNITS * i + u + 1)
                    for way in range(WAYS):
                        for k in range(KC):
                            ins = nc.tensor.matmul(ps[:, 2 * (u % 2) + way, :], up[:, k, way, c, :],
                                                   x_t[:, k, half * BANK:(half + 1) * BANK],
                                                   start=(k == 0), stop=(k == KC - 1))
                    ins.then_inc(upped, 1)
                pe.wait_ge(upped, UNITS * i + UNITS)
                nc.tensor.sem_inc(up_free, 1)
                pe.wait_ge(down_loaded, 16 * i + 16)
                n = 0
                for half in range(HALVES):
                    pe.wait_ge(h_ready, UNITS * i + (half + 1) * CH + 2)
                    for e in range(per_round):
                        for t in range(half * TQ // HALVES, (half + 1) * TQ // HALVES):
                            pe.wait_ge(added, OUTS * i + n + 1)
                            for c in range(chunks):
                                ins = nc.tensor.matmul(ps[:, 4 + n % 4, 0:D], h[:, e * chunks + c, t * P:(t + 1) * P],
                                                       down[:, e * chunks + c, :], start=(c == 0), stop=(c == chunks - 1))
                            ins.then_inc(downed, 1)
                            n += 1
                pe.wait_ge(downed, OUTS * i + OUTS)
                nc.tensor.sem_inc(down_free, 1)

        @block.scalar
        def _(act):
            if not gated:
                act.wait_ge(b1_loaded, 16)
            with act.Fori(0, rounds) as i:
                for u in range(UNITS):
                    half, c = u // CH, u % CH
                    act.wait_ge(upped, UNITS * i + u + 1)
                    if gated:
                        act.wait_ge(h_ready, UNITS * i + u + 1)
                        nc.scalar.activation(act_out[:, u % 2, :], ps[:, 2 * (u % 2), :], ACT.Silu).then_inc(activated, 1)
                    else:
                        if u % CH == 0:
                            act.wait_ge(added, OUTS * i + 4)
                        nc.scalar.sem_inc(unit_seen, 1)
                        nc.scalar.activation(h[:, c, half * BANK:(half + 1) * BANK], ps[:, 2 * (u % 2), :], ACT.Relu,
                                             bias=b1[:, bass.ds(i * CH + c, 1)]).then_inc(h_ready, 1)

        @block.vector
        def _(dve):
            with dve.Fori(0, rounds) as i:
                if gated:
                    for u in range(UNITS):
                        half, c = u // CH, u % CH
                        dve.wait_ge(activated, UNITS * i + u + 1)
                        nc.vector.tensor_tensor(h[:, c, half * BANK:(half + 1) * BANK], act_out[:, u % 2, :],
                                                ps[:, 2 * (u % 2) + 1, :], ALU.mult).then_inc(h_ready, 1)
                n = 0
                for half in range(HALVES):
                    for e in range(per_round):
                        for t in range(half * TQ // HALVES, (half + 1) * TQ // HALVES):
                            dve.wait_ge(downed, OUTS * i + n + 1)
                            dve.wait_ge(added, OUTS * i + n + 1)
                            nc.vector.scalar_tensor_tensor(acc[:, t, :], ps[:, 4 + n % 4, 0:D],
                                                           cw[:, t, bass.ds(i * per_round + e, 1)], acc[:, t, :],
                                                           op0=ALU.mult, op1=ALU.add).then_inc(added, 1)
                            n += 1
            dve.wait_ge(added, OUTS * rounds + 4)


def affine_rows(nc, name, rows, gain_dram, shift_dram, dst, add):
    with Stage(nc, name) as s:
        gain, shift = s.sb("gain", [P, D]), s.sb("shift", [P, D])
        loaded, steps = s.sem("loaded"), s.sem("steps")
        block = s.block()

        @block.sync
        def _(sp):
            sp.dma_start(gain[:, :], gain_dram.partition_broadcast(P)).then_inc(loaded, 16)
            sp.dma_start(shift[:, :], shift_dram.partition_broadcast(P)).then_inc(loaded, 16)

        @block.vector
        def _(dve):
            own = Chain(dve, steps)
            dve.wait_ge(loaded, 32)
            g = gain[:, :].unsqueeze(1).to_broadcast([P, TQ, D])
            b = shift[:, :].unsqueeze(1).to_broadcast([P, TQ, D])
            own.link(nc.vector.tensor_tensor(rows[:, :, :], rows[:, :, :], g, ALU.mult))
            if add:
                own.link(nc.vector.tensor_tensor(dst[:, :, :], dst[:, :, :], b, ALU.add))
                own.link(nc.vector.tensor_tensor(dst[:, :, :], dst[:, :, :], rows[:, :, :], ALU.add))
            else:
                own.link(nc.vector.tensor_tensor(dst[:, :, :], rows[:, :, :], b, ALU.add))


def expert_biases(nc, name, ps, ident, cw, n, b2_dram, acc):
    with Stage(nc, name) as s:
        b2 = s.sb("b2", [n, D])
        cw_t = s.sb("cw_t", [n, NT])
        loaded, turned, copied = s.sem("loaded"), s.sem("turned"), s.sem("copied")
        made, added = s.sem("made"), s.sem("added")
        block = s.block()

        @block.sync
        def _(sp):
            sp.dma_start(b2[:, :], b2_dram).then_inc(loaded, 16)

        @block.tensor
        def _(pe):
            for t in range(TQ):
                ins = nc.tensor.transpose(ps[0:n, t // 4, (t % 4) * P:(t % 4 + 1) * P], cw[:, t, :], ident[:, :])
            ins.then_inc(turned, 1)
            pe.wait_ge(copied, 1)
            pe.wait_ge(loaded, 16)
            for t in range(TQ):
                if t >= 4:
                    pe.wait_ge(added, t - 3)
                nc.tensor.matmul(ps[:, 4 + t % 4, 0:D], cw_t[:, t * P:(t + 1) * P], b2[:, :], start=True, stop=True
                                 ).then_inc(made, 1)

        @block.scalar
        def _(act):
            act.wait_ge(turned, 1)
            nc.scalar.activation(cw_t[:, :], ps[0:n, 0:2, :].rearrange("p a n -> p (a n)"), ACT.Copy
                                 ).then_inc(copied, 1)

        @block.vector
        def _(dve):
            for t in range(TQ):
                dve.wait_ge(made, t + 1)
                nc.vector.tensor_tensor(acc[:, t, :], acc[:, t, :], ps[:, 4 + t % 4, 0:D], ALU.add).then_inc(added, 1)
            dve.wait_ge(added, TQ)


def bit_conv_ffn(nc, name, ps, ident, ones, x, w1_dram, w2_dram, cw_dram, cb_dram):
    CH = 1024 // P
    LO = NQ + 2
    with Stage(nc, name) as s:
        w1 = s.sb("w1", [P, KC, 1024])
        w2 = s.sb("w2", [P, CH, D])
        w1q, w2q = s.sb("w1q", [P, KC, 1024], BF16), s.sb("w2q", [P, CH, D], BF16)
        wabs = s.sb("wabs", [P, 2048])
        wsum = s.sb("wsum", [P, 2])
        wscale, winv = s.sb("wscale", [P, 2]), s.sb("winv", [P, 2])
        rows = s.sb("rows", [P, TQ, D])
        stats, mv = s.sb("stats", [P, TQ, 6]), s.sb("mv", [P, TQ, 2])
        var_eps, dev, rstd = s.sb("var_eps", [P, TQ]), s.sb("dev", [P, TQ]), s.sb("rstd", [P, TQ])
        big, scale, inv = s.sb("big", [P, TQ]), s.sb("scale", [P, TQ]), s.sb("inv", [P, TQ])
        diag = s.sb("diag", [P, TQ, P])
        by_token = s.sb("by_token", [P, NT])
        xq_t = s.sb("xq_t", [P, KC, NT], BF16)
        hid = s.sb("hid", [P, 2, B, LO])
        conv = s.sb("conv", [P, 2, B, NQ])
        act_t = s.sb("act_t", [P, CH, NT])
        hq = s.sb("hq", [P, CH, NT], BF16)
        tmp = s.sb("tmp", [P, 2, NT])
        big4 = s.sb("big4", [P, TQ, 2])
        taps = s.sb("taps", [P, CH, 3])
        cb = s.sb("cb", [P, CH])
        out_scale = s.sb("out_scale", [P, TQ])
        loaded, steps = s.sem("loaded"), s.sem("steps")
        w_summed = s.sem("w_summed")
        w_totalled = s.sem("w_totalled")
        var_ready, dev_ready = s.sem("var_ready"), s.sem("dev_ready")
        rows_ready = s.sem("rows_ready")
        turned, copied, w1_ready = s.sem("turned"), s.sem("copied"), s.sem("w1_ready")
        diag_ready, spread, spread_copied = s.sem("diag_ready"), s.sem("spread"), s.sem("spread_copied")
        upped, conved, activated = s.sem("upped"), s.sem("conved"), s.sem("activated")
        hid_used = s.sem("hid_used")
        act_turned, maxed = s.sem("act_turned"), s.sem("maxed")
        hq_ready, downed, added = s.sem("hq_ready"), s.sem("downed"), s.sem("added")
        block = s.block()

        @block.sync
        def _(sp):
            sp.dma_start(w1[:, :, :], w1_dram).then_inc(loaded, 16)
            sp.dma_start(w2[:, :, :], w2_dram).then_inc(loaded, 16)
            sp.dma_start(taps[:, :, :], cw_dram).then_inc(loaded, 16)
            sp.dma_start(cb[:, :], cb_dram).then_inc(loaded, 16)

        @block.scalar
        def _(act):
            act.wait_ge(loaded, 64)
            nc.scalar.activation(wabs[:, :], w1[:, :, :].rearrange("p k n -> p (k n)"), ACT.Abs,
                                 accum_out=wsum[:, 0:1]).then_inc(w_summed, 1)
            act.wait_ge(w_summed, 1)
            nc.scalar.activation(wabs[:, :], w2[:, :, :].rearrange("p k n -> p (k n)"), ACT.Abs,
                                 accum_out=wsum[:, 1:2]).then_inc(w_summed, 1)
            act.wait_ge(var_ready, 1)
            nc.scalar.activation(dev[:, :], var_eps[:, :], ACT.Sqrt).then_inc(dev_ready, 1)
            for n in range(4):
                act.wait_ge(turned, n + 1)
                nc.scalar.activation(xq_t[:, n // 2, (n % 2) * BANK:(n % 2 + 1) * BANK], ps[:, n, :], ACT.Copy
                                     ).then_inc(copied, 1)
            for n in range(2):
                act.wait_ge(spread, 1)
                nc.scalar.activation(by_token[:, n * BANK:(n + 1) * BANK], ps[:, 4 + n, :], ACT.Copy
                                     ).then_inc(spread_copied, 1)
            for c in range(CH):
                act.wait_ge(conved, c + 1)
                nc.scalar.activation(act_t[:, c, :], conv[:, c % 2, :, :].rearrange("p b n -> p (b n)"), ACT.Silu,
                                     bias=cb[:, c:c + 1]).then_inc(activated, 1)
            for n in range(2):
                act.wait_ge(spread, 2)
                nc.scalar.activation(by_token[:, n * BANK:(n + 1) * BANK], ps[:, 4 + n, :], ACT.Copy
                                     ).then_inc(spread_copied, 1)

        @block.tensor
        def _(pe):
            pe.wait_ge(w_summed, 2)
            nc.tensor.matmul(ps[:, 7, 0:2], ones[:, :], wsum[:, :], start=True, stop=True).then_inc(w_totalled, 1)
            pe.wait_ge(rows_ready, 1)
            for k in range(KC):
                for t in range(TQ):
                    ins = nc.tensor.transpose(ps[:, 2 * k + t // 4, (t % 4) * P:(t % 4 + 1) * P],
                                              rows[:, t, k * P:(k + 1) * P], ident[:, :])
                    if t % 4 == 3:
                        ins.then_inc(turned, 1)
            pe.wait_ge(diag_ready, 1)
            for t in range(TQ):
                ins = nc.tensor.matmul(ps[:, 4 + t // 4, (t % 4) * P:(t % 4 + 1) * P], ones[:, :], diag[:, t, :],
                                       start=True, stop=True)
            ins.then_inc(spread, 1)
            pe.wait_ge(copied, 4)
            pe.wait_ge(w1_ready, 1)
            for c in range(CH):
                if c >= 2:
                    pe.wait_ge(hid_used, 2 * (c - 1))
                for b in range(B):
                    for k in range(KC):
                        ins = nc.tensor.matmul(ps[:, 2 * (c % 2) + b, :], w1q[:, k, c * P:(c + 1) * P],
                                               xq_t[:, k, b * NQ:(b + 1) * NQ], start=(k == 0), stop=(k == KC - 1))
                ins.then_inc(upped, 1)
            pe.wait_ge(activated, CH)
            for t in range(TQ):
                if t >= 2:
                    pe.wait_ge(maxed, t - 1)
                for c in range(CH):
                    ins = nc.tensor.transpose(ps[:, 2 * (t % 2) + c // 4, (c % 4) * P:(c % 4 + 1) * P],
                                              act_t[:, c, t * P:(t + 1) * P], ident[:, :])
                ins.then_inc(act_turned, 1)
            pe.wait_ge(diag_ready, 2)
            for t in range(TQ):
                ins = nc.tensor.matmul(ps[:, 4 + t // 4, (t % 4) * P:(t % 4 + 1) * P], ones[:, :], diag[:, t, :],
                                       start=True, stop=True)
            ins.then_inc(spread, 1)
            pe.wait_ge(hq_ready, CH)
            for t in range(TQ):
                if t >= 4:
                    pe.wait_ge(added, t - 3)
                for c in range(CH):
                    ins = nc.tensor.matmul(ps[:, t % 4, 0:D], hq[:, c, t * P:(t + 1) * P], w2q[:, c, :],
                                           start=(c == 0), stop=(c == CH - 1))
                ins.then_inc(downed, 1)

        @block.vector
        def _(dve):
            own = Chain(dve, steps)
            own.link(nc.vector.memset(hid[:, :, :, :], 0.0))
            for t in range(TQ):
                own.done(nc.vector.bn_stats(stats[:, t, :], x[:, t, :]))
            own.wait()
            for t in range(TQ):
                own.done(nc.vector.bn_aggr(mv[:, t, :], stats[:, t, :]))
            own.wait()
            own.link(nc.vector.tensor_scalar(var_eps[:, :], mv[:, :, 1], 1e-5, None, ALU.add))
            nc.vector.sem_inc(var_ready, 1)
            dve.wait_ge(dev_ready, 1)
            own.link(nc.vector.reciprocal(rstd[:, :], dev[:, :]))
            for t in range(TQ):
                own.done(nc.vector.tensor_scalar(rows[:, t, :], x[:, t, :], mv[:, t, 0:1], rstd[:, t:t + 1],
                                                 ALU.subtract, ALU.mult))
            own.wait()

            def scales():
                own.link(nc.vector.tensor_scalar(big[:, :], big[:, :], 1e-5, None, ALU.max))
                own.link(nc.vector.reciprocal(scale[:, :], big[:, :]))
                own.link(nc.vector.tensor_scalar(scale[:, :], scale[:, :], 127.0, None, ALU.mult))
                own.link(nc.vector.reciprocal(inv[:, :], scale[:, :]))

            own.link(nc.vector.tensor_reduce(big[:, :], rows[:, :, :], AX.X, ALU.max, apply_absolute_value=True))
            scales()
            for t in range(TQ):
                own.done(nc.vector.tensor_scalar(rows[:, t, :], rows[:, t, :], scale[:, t:t + 1], None, ALU.mult))
            own.wait()
            allr = rows[:, :, :].rearrange("p t n -> p (t n)")
            own.link(nc.vector.tensor_scalar(allr, allr, ROUND, -ROUND, ALU.add, ALU.add))
            own.link(nc.vector.tensor_scalar(allr, allr, 127.0, -128.0, ALU.min, ALU.max))
            nc.vector.sem_inc(rows_ready, 1)
            dve.wait_ge(w_totalled, 1)
            own.link(nc.vector.tensor_scalar(winv[:, :], ps[:, 7, 0:2], 1.0 / (1024 * D), 1e-5, ALU.mult, ALU.max))
            own.link(nc.vector.reciprocal(wscale[:, :], winv[:, :]))
            own.link(nc.vector.reciprocal(winv[:, :], wscale[:, :]))
            for t in range(TQ):
                own.done(nc.vector.tensor_scalar(diag[:, t, :], ident[:, :], inv[:, t:t + 1], winv[:, 0:1], ALU.mult,
                                                 ALU.mult))
            own.wait()
            nc.vector.sem_inc(diag_ready, 1)
            for n, (w, wq) in enumerate(((w1[:, :, :].rearrange("p k n -> p (k n)"), w1q[:, :, :].rearrange("p k n -> p (k n)")),
                                         (w2[:, :, :].rearrange("p k n -> p (k n)"), w2q[:, :, :].rearrange("p k n -> p (k n)")))):
                own.link(nc.vector.tensor_scalar(w, w, wscale[:, n:n + 1], None, ALU.mult))
                own.link(nc.vector.tensor_scalar(w, w, ROUND, -ROUND, ALU.add, ALU.add))
                own.link(nc.vector.tensor_scalar(wq, w, 1.0, -1.0, ALU.min, ALU.max))
                if n == 0:
                    nc.vector.sem_inc(w1_ready, 1)
            dve.wait_ge(spread_copied, 2)
            for c in range(CH):
                dve.wait_ge(upped, c + 1)
                for b in range(B):
                    own.done(nc.vector.tensor_tensor(hid[:, c % 2, b, 1:1 + NQ], by_token[:, b * NQ:(b + 1) * NQ],
                                                     ps[:, 2 * (c % 2) + b, :], ALU.mult))
                own.wait()
                nc.vector.sem_inc(hid_used, 2)
                if c >= 2:
                    dve.wait_ge(activated, c - 1)
                y, v = conv[:, c % 2, :, :], hid[:, c % 2, :, :]
                own.link(nc.vector.tensor_scalar(y, v[:, :, 0:NQ], taps[:, c, 0:1], None, ALU.mult))
                own.link(nc.vector.scalar_tensor_tensor(y, v[:, :, 1:NQ + 1], taps[:, c, 1:2], y, ALU.mult, ALU.add))
                own.link(nc.vector.scalar_tensor_tensor(y, v[:, :, 2:NQ + 2], taps[:, c, 2:3], y, ALU.mult, ALU.add))
                nc.vector.sem_inc(conved, 1)
            for t in range(TQ):
                dve.wait_ge(act_turned, t + 1)
                own.link(nc.vector.tensor_reduce(big[:, t:t + 1], ps[:, 2 * (t % 2):2 * (t % 2) + 2, :].rearrange("p a n -> p (a n)"),
                                                 AX.X, ALU.max, apply_absolute_value=True))
                nc.vector.sem_inc(maxed, 1)
            scales()
            own.link(nc.vector.tensor_scalar(out_scale[:, :], inv[:, :], winv[:, 1:2], None, ALU.mult))
            for t in range(TQ):
                own.done(nc.vector.tensor_scalar(diag[:, t, :], ident[:, :], scale[:, t:t + 1], None, ALU.mult))
            own.wait()
            nc.vector.sem_inc(diag_ready, 1)
            dve.wait_ge(spread_copied, 4)
            for c in range(CH):
                y = tmp[:, c % 2, :]
                own.link(nc.vector.tensor_tensor(y, act_t[:, c, :], by_token[:, :], ALU.mult))
                own.link(nc.vector.tensor_scalar(y, y, ROUND, -ROUND, ALU.add, ALU.add))
                nc.vector.tensor_scalar(hq[:, c, :], y, 127.0, -128.0, ALU.min, ALU.max).then_inc(hq_ready, 1)
            for t in range(TQ):
                dve.wait_ge(downed, t + 1)
                nc.vector.scalar_tensor_tensor(x[:, t, :], ps[:, t % 4, 0:D], out_scale[:, t:t + 1], x[:, t, :],
                                               ALU.mult, ALU.add).then_inc(added, 1)
            dve.wait_ge(added, TQ)


def slot_gru(nc, name, ps, ident, ones, slots, p_t, w, x):
    ITERS = 3
    EPS = 1e-6
    SCALE = D ** -0.5
    NC_ = NK // P
    with Stage(nc, name) as s:
        wk, wv = s.sb("wk", [P, KC, D]), s.sb("wv", [P, KC, D])
        wq = s.sb("wq", [P, KC, D])
        wih, whh = s.sb("wih", [P, KC, 3 * D]), s.sb("whh", [P, KC, 3 * D])
        bih, bhh = s.sb("bih", [P, 6]), s.sb("bhh", [P, 6])
        brz = s.sb("brz", [P, 4])
        norm_w = s.sb("norm_w", [P, KC])
        k_t = s.sb("k_t", [P, KC, B * NK])
        v = s.sb("v", [P, TK, D])
        sq = s.sb("sq", [P, KC, NT])
        sn = s.sb("sn", [P, KC, NT])
        q_t = s.sb("q_t", [P, KC, NT])
        rs = s.sb("rs", [P, NT])
        dev = s.sb("dev", [P, NT])
        top = s.sb("top", [P, 4])
        esum, resum = s.sb("esum", [P, 4]), s.sb("resum", [P, 4])
        probs = s.sb("probs", [P, 2, NQ])
        attn = s.sb("attn", [P, 2, NQ])
        rden = s.sb("rden", [P, NQ])
        upd = s.sb("upd", [P, KC, NT])
        r_t, z_t, n_t = (s.sb(c, [P, KC, NT]) for c in ("r_t", "z_t", "n_t"))
        loaded = s.sem("loaded")
        kv_made, kv_copied = s.sem("kv_made"), s.sem("kv_copied")
        steps = s.sem("steps")
        sq_ready, sq_summed = s.sem("sq_ready"), s.sem("sq_summed")
        mean_ready, dev_ready = s.sem("mean_ready"), s.sem("dev_ready")
        sn_ready, q_made, q_ready = s.sem("sn_ready"), s.sem("q_made"), s.sem("q_ready")
        scored, top_ready, exp_done = s.sem("scored"), s.sem("top_ready"), s.sem("exp_done")
        attn_ready, attn_used = s.sem("attn_ready"), s.sem("attn_used")
        upd_ready = s.sem("upd_ready")
        gates_made, gates_done = s.sem("gates_made"), s.sem("gates_done")
        hn_ready, n_ready = s.sem("hn_ready"), s.sem("n_ready")
        slots_ready = s.sem("slots_ready")
        turned = s.sem("turned")
        block = s.block()
        HG = NT // BANK * KC

        @block.sync
        def _(sp):
            for dst, src in ((wk, w["wk"]), (wv, w["wv"]), (wq, w["wq"]), (wih, w["wih"]), (whh, w["whh"])):
                sp.dma_start(dst[:, :, :], src).then_inc(loaded, 16)
            for dst, src in ((bih, w["bih"]), (bhh, w["bhh"]), (norm_w, w["norm"])):
                sp.dma_start(dst[:, :], src).then_inc(loaded, 16)

        @block.tensor
        def _(pe):
            pe.wait_ge(loaded, 8 * 16)
            unit = 0
            for m in range(KC):
                for n in range(B * NK // BANK):
                    if unit >= 4:
                        pe.wait_ge(kv_copied, unit - 3)
                    for c in range(KC):
                        ins = nc.tensor.matmul(ps[:, unit % 4, :], wk[:, c, m * P:(m + 1) * P],
                                               p_t[:, c, n * BANK:(n + 1) * BANK], start=(c == 0), stop=(c == KC - 1))
                    ins.then_inc(kv_made, 1)
                    unit += 1
            for t2 in range(TK // 2):
                pe.wait_ge(kv_copied, unit - 3)
                for j in range(2):
                    t = 2 * t2 + j
                    for c in range(KC):
                        ins = nc.tensor.matmul(ps[:, unit % 4, j * D:(j + 1) * D], p_t[:, c, t * P:(t + 1) * P],
                                               wv[:, c, :], start=(c == 0), stop=(c == KC - 1))
                ins.then_inc(kv_made, 1)
                unit += 1
            pe.wait_ge(kv_copied, unit)
            with pe.Fori(0, ITERS) as i:
                pe.wait_ge(sq_ready, i + 1)
                for n in range(2):
                    for c in range(KC):
                        ins = nc.tensor.matmul(ps[:, n, :], ones[:, :], sq[:, c, n * BANK:(n + 1) * BANK],
                                               start=(c == 0), stop=(c == KC - 1))
                ins.then_inc(sq_summed, 1)
                pe.wait_ge(sn_ready, i + 1)
                for m in range(KC):
                    for n in range(2):
                        for c in range(KC):
                            ins = nc.tensor.matmul(ps[:, 2 + 2 * m + n, :], wq[:, c, m * P:(m + 1) * P],
                                                   sn[:, c, n * BANK:(n + 1) * BANK], start=(c == 0), stop=(c == KC - 1))
                ins.then_inc(q_made, 1)
                pe.wait_ge(q_ready, i + 1)
                for b in range(B):
                    def update(t):
                        n = i * (B * NC_) + (b * NC_ + t)
                        pe.wait_ge(attn_ready, n + 1)
                        for m in range(KC):
                            nc.tensor.matmul(ps[:, 2 + m, :], v[:, b * NC_ + t, m * P:(m + 1) * P], attn[:, t % 2, :],
                                             start=(t == 0), stop=(t == NC_ - 1))
                        nc.tensor.matmul(ps[:, 4, :], ones[:, :], attn[:, t % 2, :], start=(t == 0),
                                         stop=(t == NC_ - 1)).then_inc(attn_used, 1)

                    if b:
                        pe.wait_ge(upd_ready, i * B + b)
                    for t in range(NC_):
                        n = i * (B * NC_) + (b * NC_ + t)
                        if b * NC_ + t >= 2:
                            pe.wait_ge(exp_done, n - 1)
                        for c in range(KC):
                            ins = nc.tensor.matmul(ps[:, t % 2, :], k_t[:, c, b * NK + t * P:b * NK + (t + 1) * P],
                                                   q_t[:, c, b * NQ:(b + 1) * NQ], start=(c == 0), stop=(c == KC - 1))
                        ins.then_inc(scored, 1)
                        if t >= 1:
                            update(t - 1)
                    update(NC_ - 1)
                pe.wait_ge(upd_ready, i * B + B)
                for u in range(HG):
                    n, m = u // KC, u % KC
                    if u >= 2:
                        pe.wait_ge(hn_ready, i * HG + u - 1)
                    tok = slice(n * BANK, (n + 1) * BANK)
                    for gate in range(3):
                        for c in range(KC):
                            nc.tensor.matmul(ps[:, 4 * (u % 2) + gate, :],
                                             wih[:, c, gate * D + m * P:gate * D + (m + 1) * P], upd[:, c, tok],
                                             start=(c == 0), stop=(gate == 2 and c == KC - 1))
                        for c in range(KC):
                            last = nc.tensor.matmul(ps[:, 4 * (u % 2) + (3 if gate == 2 else gate), :],
                                                    whh[:, c, gate * D + m * P:gate * D + (m + 1) * P], slots[:, c, tok],
                                                    start=(gate == 2 and c == 0), stop=(c == KC - 1))
                    last.then_inc(gates_made, 1)
            pe.wait_ge(slots_ready, ITERS * 1 + 1)
            for t in range(TQ):
                for c in range(KC):
                    ins = nc.tensor.transpose(ps[:, t // 2, (t % 2) * D + c * P:(t % 2) * D + (c + 1) * P],
                                              slots[:, c, t * P:(t + 1) * P], ident[:, :])
            ins.then_inc(turned, 1)

        @block.scalar
        def _(act):
            unit = 0
            for m in range(KC):
                for n in range(B * NK // BANK):
                    act.wait_ge(kv_made, unit + 1)
                    nc.scalar.activation(k_t[:, m, n * BANK:(n + 1) * BANK], ps[:, unit % 4, :], ACT.Copy
                                         ).then_inc(kv_copied, 1)
                    unit += 1
            for t2 in range(TK // 2):
                act.wait_ge(kv_made, unit + 1)
                nc.scalar.activation(v[:, 2 * t2:2 * t2 + 2, :].rearrange("p a n -> p (a n)"), ps[:, unit % 4, :],
                                     ACT.Copy).then_inc(kv_copied, 1)
                unit += 1
            with act.Fori(0, ITERS) as i:
                act.wait_ge(mean_ready, i + 1)
                nc.scalar.activation(dev[:, :], rs[:, :], ACT.Sqrt).then_inc(dev_ready, 1)
                act.wait_ge(q_made, i + 1)
                for m in range(KC):
                    ins = nc.scalar.activation(q_t[:, m, :], ps[:, 2 + 2 * m:4 + 2 * m, :].rearrange("p a n -> p (a n)"),
                                               ACT.Copy)
                ins.then_inc(q_ready, 1)
                for b in range(B):
                    for t in range(NC_):
                        n = i * (B * NC_) + (b * NC_ + t)
                        act.wait_ge(top_ready, n + 1)
                        nc.scalar.activation(probs[:, t % 2, :], ps[:, t % 2, :], ACT.Exp, bias=top[:, t % 2:t % 2 + 1],
                                             scale=SCALE, accum_out=esum[:, t % 2:t % 2 + 1]).then_inc(exp_done, 1)
                for u in range(HG):
                    n, m = u // KC, u % KC
                    tok = slice(n * BANK, (n + 1) * BANK)
                    act.wait_ge(gates_made, i * HG + u + 1)
                    nc.scalar.activation(r_t[:, m, tok], ps[:, 4 * (u % 2), :], ACT.Sigmoid, bias=brz[:, m:m + 1])
                    nc.scalar.activation(z_t[:, m, tok], ps[:, 4 * (u % 2) + 1, :], ACT.Sigmoid,
                                         bias=brz[:, 2 + m:3 + m]).then_inc(gates_done, 1)
                    act.wait_ge(hn_ready, i * HG + u + 1)
                    nc.scalar.activation(n_t[:, m, tok], n_t[:, m, tok], ACT.Tanh, bias=bih[:, 4 + m:5 + m]
                                         ).then_inc(n_ready, 1)

        PER_ITER = 2 + 6 + 2 + 3 * B * NC_ + B * 4 + HG + HG * 3

        @block.vector
        def _(dve):
            dve.wait_ge(loaded, 8 * 16)
            nc.vector.tensor_tensor(brz[:, :], bih[:, 0:4], bhh[:, 0:4], ALU.add).then_inc(slots_ready, 1)
            with dve.Fori(0, ITERS) as i:
                own = Chain(dve, steps, i * PER_ITER)
                dve.wait_ge(slots_ready, i + 1)
                for c in range(KC):
                    own.done(nc.vector.tensor_tensor(sq[:, c, :], slots[:, c, :], slots[:, c, :], ALU.mult))
                own.wait()
                nc.vector.sem_inc(sq_ready, 1)
                dve.wait_ge(sq_summed, i + 1)
                own.link(nc.vector.tensor_scalar(rs[:, :], ps[:, 0:2, :].rearrange("p a n -> p (a n)"), 1.0 / D, EPS,
                                                 ALU.mult, ALU.add))
                nc.vector.sem_inc(mean_ready, 1)
                dve.wait_ge(dev_ready, i + 1)
                own.link(nc.vector.reciprocal(rs[:, :], dev[:, :]))
                for c in range(KC):
                    own.done(nc.vector.tensor_tensor(sn[:, c, :], slots[:, c, :], rs[:, :], ALU.mult))
                own.wait()
                for c in range(KC):
                    own.done(nc.vector.tensor_scalar(sn[:, c, :], sn[:, c, :], norm_w[:, c:c + 1], None, ALU.mult))
                own.wait()
                nc.vector.sem_inc(sn_ready, 1)
                own.n += 2
                nc.vector.sem_inc(steps, 2)
                own.wait()
                for b in range(B):
                    for t in range(NC_):
                        n = i * (B * NC_) + (b * NC_ + t)
                        j = t % 2
                        dve.wait_ge(scored, n + 1)
                        own.link(nc.vector.reduce_max(top[:, 2 + j:3 + j], ps[:, j, :], AX.X))
                        own.link(nc.vector.tensor_scalar(top[:, j:j + 1], top[:, 2 + j:3 + j], -SCALE, None, ALU.mult))
                        nc.vector.sem_inc(top_ready, 1)
                        dve.wait_ge(exp_done, n + 1)
                        own.link(nc.vector.reciprocal(resum[:, j:j + 1], esum[:, j:j + 1]))
                        if b * NC_ + t >= 2:
                            dve.wait_ge(attn_used, n - 1)
                        nc.vector.tensor_scalar(attn[:, j, :], probs[:, j, :], resum[:, j:j + 1], None, ALU.mult
                                                ).then_inc(attn_ready, 1)
                    dve.wait_ge(attn_used, i * (B * NC_) + (b + 1) * NC_)
                    own.link(nc.vector.tensor_scalar(rden[:, :], ps[:, 4, :], EPS, None, ALU.add))
                    own.link(nc.vector.reciprocal(rden[:, :], rden[:, :]))
                    for m in range(KC):
                        own.done(nc.vector.tensor_tensor(upd[:, m, b * NQ:(b + 1) * NQ], rden[:, :], ps[:, 2 + m, :],
                                                         ALU.mult))
                    own.wait()
                    nc.vector.sem_inc(upd_ready, 1)
                for u in range(HG):
                    n, m = u // KC, u % KC
                    tok = slice(n * BANK, (n + 1) * BANK)
                    dve.wait_ge(gates_done, i * HG + u + 1)
                    own.link(nc.vector.scalar_tensor_tensor(n_t[:, m, tok], ps[:, 4 * (u % 2) + 3, :], bhh[:, 4 + m:5 + m],
                                                            r_t[:, m, tok], ALU.add, ALU.mult))
                    nc.vector.tensor_tensor(n_t[:, m, tok], n_t[:, m, tok], ps[:, 4 * (u % 2) + 2, :], ALU.add
                                            ).then_inc(hn_ready, 1)
                for u in range(HG):
                    n, m = u // KC, u % KC
                    tok = slice(n * BANK, (n + 1) * BANK)
                    dve.wait_ge(n_ready, i * HG + u + 1)
                    own.link(nc.vector.tensor_tensor(slots[:, m, tok], slots[:, m, tok], n_t[:, m, tok], ALU.subtract))
                    own.link(nc.vector.tensor_tensor(slots[:, m, tok], slots[:, m, tok], z_t[:, m, tok], ALU.mult))
                    own.link(nc.vector.tensor_tensor(slots[:, m, tok], slots[:, m, tok], n_t[:, m, tok], ALU.add))
                nc.vector.sem_inc(slots_ready, 1)
                assert own.n == PER_ITER, (own.n, PER_ITER)
            dve.wait_ge(turned, 1)
            for t4 in range(4):
                ins = nc.vector.tensor_tensor(x[:, 2 * t4:2 * t4 + 2, :].rearrange("p a n -> p (a n)"),
                                              x[:, 2 * t4:2 * t4 + 2, :].rearrange("p a n -> p (a n)"), ps[:, t4, :],
                                              ALU.add)
                ins.then_inc(turned, 1)
            dve.wait_ge(turned, 5)


def build(nc, A, out, stages=range(8)):
    Stage.spent = []
    with ExitStack() as top:
        ps = top.enter_context(nc.psum_tensor("ps", [P, 8, BANK], F32))

        def sb(name, shape, dt=F32, stack=top):
            return stack.enter_context(nc.sbuf_tensor(name, shape, dt))

        ident, ones, slot_sum = sb("ident", [P, P]), sb("ones", [P, P]), sb("slot_sum", [P, P])
        x = sb("x_rows", [P, TQ, D])
        ctx_rows_dram = A["ctx_1024"].rearrange("b (t p) d -> p (b t) d", p=P)

        def by_feature(name):
            return A[name + "_f"]

        constants(nc, ident, ones, slot_sum)
        load_x(nc, A["x"], x)
        def slots(name, tag, xin, kv_t, nk, sparse, wo_dram, bo_dram, acc):
            with ExitStack() as st:
                o_all = sb(tag + "_o_all", [P, 4, NT], stack=st)
                slot_attention(nc, tag + "a", ps, ident, slot_sum, xin, kv_t, nk, A[tag + "_w"], A[tag + "_b"],
                               o_all, sparse)
                project_out(nc, tag + "o", ps, o_all, 4, wo_dram, bo_dram, acc)

        if 0 in stages:
            with ExitStack() as l0:
                q_t = sb("l0_q_t", [P, KC, NT], stack=l0)
                c_t = sb("l0_c_t", [P, KC, B * NK], stack=l0)
                with ExitStack() as t:
                    c = sb("l0_c_rows", [P, TK, D], stack=t)
                    normalize(nc, "l0lnc", ps, ident, c, TK, c_t, 1e-5, gain_dram=by_feature("L0_xattn_ln_ctx_g"),
                              shift_dram=by_feature("L0_xattn_ln_ctx_b"), src_dram=ctx_rows_dram)
                    normalize(nc, "l0lnx", ps, ident, x, TQ, q_t, 1e-5, norms=2,
                              gain_dram=by_feature("L0_xattn_ln_lat_g"), shift_dram=by_feature("L0_xattn_ln_lat_b"))
                o_all = sb("l0_o_all", [P, 8, NT], stack=l0)
                rope_attention(nc, "l0a", ps, ones, q_t, c_t, A["l0_w"], A["l0_cos"], A["l0_sin"], o_all)
                project_out(nc, "l0o", ps, o_all, 8, A["l0_wo"], A["L0_xattn_bo"], x)
        if 1 in stages:
            bit_conv_ffn(nc, "f0", ps, ident, ones, x, A["f0_w1"], A["f0_w2"], A["f0_taps"], A["f0_cb"])
        if 2 in stages or 6 in stages:
            ctx_t = sb("ctx_t", [P, KC, B * NK])
            with ExitStack() as t:
                c = sb("c_rows", [P, TK, D], stack=t)
                transpose_rows(nc, "ctxt", ps, ident, c, TK, ctx_t, ctx_rows_dram)
        if 2 in stages:
            with ExitStack() as st:
                x_t = sb("l1_x_t", [P, KC, NT], stack=st)
                normalize(nc, "l1ln", ps, ident, x, TQ, x_t, 1e-5)
                slots("L1", "l1", x_t, ctx_t, NK, True, A["l1_wo"], A["L1_xattn_bo"], x)
        clear_semaphores(nc)
        if 3 in stages:
            with ExitStack() as st:
                x_t = sb("m1_x_t", [P, KC, NT], stack=st)
                cw = sb("m1_cw", [P, TQ, 9], stack=st)
                normalize(nc, "m1ln", ps, ident, x, TQ, x_t, 1e-5)
                route(nc, "m1r", ps, x_t, 9, A["m1_router"], A["m1_bias"], "top2", cw)
                experts(nc, "m1e", ps, x_t, 9, 1, 6, True, A["m1_up"], A["m1_down"], None, cw, x)
        if 4 in stages:
            with ExitStack() as st:
                slots_t = sb("g2_slots", [P, KC, NT], stack=st)
                p_t = sb("g2_p_t", [P, KC, B * NK], stack=st)
                with ExitStack() as t:
                    c = sb("g2_c_rows", [P, TK, D], stack=t)
                    normalize(nc, "g2lnc", ps, ident, c, TK, p_t, 1e-6, rms=True,
                              gain_dram=by_feature("L2_xattn_input_norm_w"), src_dram=ctx_rows_dram)
                    normalize(nc, "g2lnx", ps, ident, x, TQ, slots_t, 1e-5)
                slot_gru(nc, "g2", ps, ident, ones, slots_t, p_t,
                         {k: A["g2_" + k] for k in ("wk", "wv", "wq", "wih", "whh", "bih", "bhh", "norm")}, x)
        clear_semaphores(nc)
        if 5 in stages:
            with ExitStack() as st:
                src = sb("m2_src", [P, TQ, D], stack=st)
                x1 = sb("m2_x1", [P, TQ, D], stack=st)
                x_t = sb("m2_x_t", [P, KC, NT], stack=st)
                cw = sb("m2_cw", [P, TQ, 8], stack=st)
                normalize(nc, "m2ln", ps, ident, x, TQ, x_t, 1e-5, keep=src)
                with ExitStack() as st2:
                    o_all = sb("m2_o_all", [P, 4, NT], stack=st2)
                    slot_attention(nc, "m2a", ps, ident, slot_sum, x_t, x_t, NQ, A["m2_w"], A["m2_b"], o_all, False)
                    project_out(nc, "m2o", ps, o_all, 4, A["m2_wo"], A["L2_ffn_bo"], src)
                normalize(nc, "m2ln1", ps, ident, src, TQ, x_t, 1e-5, keep=x1,
                          gain_dram=by_feature("L2_ffn_ln1_g"), shift_dram=by_feature("L2_ffn_ln1_b"))
                affine_rows(nc, "m2af1", x1, A["L2_ffn_ln1_g"], A["L2_ffn_ln1_b"], src, False)
                route(nc, "m2r", ps, x_t, 8, A["m2_router"], A["L2_ffn_gb"], "softmax", cw)
                experts(nc, "m2e", ps, x_t, 8, 1, 4, False, A["m2_up"], A["m2_down"], A["m2_b1"], cw, src)
                expert_biases(nc, "m2eb", ps, ident, cw, 8, A["L2_ffn_b2"], src)
                normalize(nc, "m2ln2", ps, ident, src, TQ, x_t, 1e-5, keep=x1)
                affine_rows(nc, "m2af2", x1, A["L2_ffn_ln2_g"], A["L2_ffn_ln2_b"], x, True)
        if 6 in stages:
            with ExitStack() as st:
                x_t = sb("l3_x_t", [P, KC, NT], stack=st)
                normalize(nc, "l3ln", ps, ident, x, TQ, x_t, 1e-5)
                slots("L3", "l3", x_t, ctx_t, NK, False, A["l3_wo"], None, x)
        if 7 in stages:
            with ExitStack() as st:
                x_t = sb("m3_x_t", [P, KC, NT], stack=st)
                cw = sb("m3_cw", [P, TQ, 18], stack=st)
                normalize(nc, "m3ln", ps, ident, x, TQ, x_t, 1e-5)
                route(nc, "m3r", ps, x_t, 16, A["m3_router"], A["m3_bias"], "grouped", cw)
                experts(nc, "m3e", ps, x_t, 6, 3, 1, True, A["m3_up"], A["m3_down"], None, cw, x)
        store_x(nc, x, out)


def layout(i):
    import numpy as np
    f = {k: np.ascontiguousarray(v) for k, v in i.items()}
    a = {k: f[k] for k in ("x", "ctx_1024", "L0_xattn_bo")}
    for k in ("L0_xattn_ln_lat_g", "L0_xattn_ln_lat_b", "L0_xattn_ln_ctx_g", "L0_xattn_ln_ctx_b"):
        a[k + "_f"] = np.ascontiguousarray(f[k].reshape(-1, 128).T)

    def groups(w, n):
        return w.reshape(2, 128, n, -1).transpose(2, 1, 0, 3)

    def padded(w):
        return np.pad(w.reshape(w.shape[0], 16, 16), ((0, 0), (0, 0), (0, 16))).reshape(w.shape[0], 512)

    def slot_weights(tag, wq, bq, wk, bk, wv, bv):
        a[tag + "_w"] = np.ascontiguousarray(np.concatenate(
            [groups(padded(wq), 4).reshape(4, 128, -1), groups(padded(wk), 4).reshape(4, 128, -1),
             groups(wv, 4).reshape(4, 128, -1)], axis=2))
        b = [padded(v[None])[0].reshape(4, 128) for v in (bq, bk, bv)]
        b[1].reshape(4, 4, 32)[:, :, 16] = 1.0
        a[tag + "_b"] = np.ascontiguousarray(np.stack(b, axis=2))

    def slot_rows(wo):
        return np.ascontiguousarray(
            np.pad(wo.reshape(16, 16, 256), ((0, 0), (0, 16), (0, 0))).reshape(4, 128, 256).transpose(1, 0, 2))

    n = "L1_xattn_"
    slot_weights("l1", *(f[n + k] for k in ("Wq", "bq", "Wk", "bk", "Wv", "bv")))
    a["l1_wo"] = slot_rows(f[n + "Wo"])
    a[n + "bo"] = f[n + "bo"]
    n = "L3_xattn_"
    slot_weights("l3", f[n + "Wq"].T, f[n + "bq"], f[n + "Wk"].T, f[n + "bk"], f[n + "Wv"].T, f[n + "bv"])
    a["l3_wo"] = slot_rows(np.eye(256, dtype=np.float32))
    wkv = f["L0_xattn_Wkv"]
    a["l0_w"] = np.ascontiguousarray(np.stack(
        [groups(f["L0_xattn_Wq"], 8), groups(wkv[:, :1024], 8), groups(wkv[:, 1024:], 8)], axis=2))
    a["l0_cos"] = np.ascontiguousarray(f["L0_xattn_cos"].T)
    a["l0_sin"] = np.ascontiguousarray(f["L0_xattn_sin"].T)
    a["l0_wo"] = np.ascontiguousarray(f["L0_xattn_Wo"].reshape(8, 128, 256).transpose(1, 0, 2))

    def router(w):
        return np.ascontiguousarray(w.T.reshape(2, 128, -1).transpose(1, 0, 2))

    def expert_weights(tag, ups, down, per_round):
        e, hid = ups[0].shape[:2]
        ch = -(-hid // 128)
        fill = ((0, 0), (0, ch * 128 - hid), (0, 0))
        u = np.stack([np.pad(w, fill).reshape(e, ch, 128, 2, 128) for w in ups], axis=1)
        u = u.reshape(e // per_round, per_round, len(ups), ch, 128, 2, 128).transpose(0, 6, 5, 2, 1, 3, 4)
        a[tag + "_up"] = np.ascontiguousarray(u.reshape(e // per_round, 128, -1))
        d = np.pad(down.transpose(0, 2, 1), fill).reshape(e // per_round, per_round * ch, 128, 256)
        a[tag + "_down"] = np.ascontiguousarray(d.transpose(0, 2, 1, 3).reshape(e // per_round, 128, -1))

    n = "L1_ffn_"
    cat = lambda x, y: np.concatenate([f[n + x], f[n + y]], axis=0)
    a["m1_router"] = router(cat("gate_weight", "new_gate_weight"))
    a["m1_bias"] = np.concatenate([np.zeros(8, np.float32), f[n + "gate_bias"]])
    expert_weights("m1", [cat("w1", "new_w1"), cat("w3", "new_w3")], cat("w2", "new_w2"), 1)
    n = "L3_ffn_"
    a["m3_router"] = router(f[n + "router_weight"])
    a["m3_bias"] = f[n + "e_bias"]
    shared = lambda w: w.reshape(2, 128, 256)
    expert_weights("m3", [np.concatenate([f[n + "gate_w"], shared(f[n + "sh_gate_w"])]),
                          np.concatenate([f[n + "up_w"], shared(f[n + "sh_up_w"])])],
                   np.concatenate([f[n + "down_w"], f[n + "sh_down_w"].reshape(256, 2, 128).transpose(1, 0, 2)]), 3)
    n = "L2_ffn_"
    slot_weights("m2", *(f[n + k] for k in ("Wq", "bq", "Wk", "bk", "Wv", "bv")))
    a["m2_wo"] = slot_rows(f[n + "Wo"])
    a["m2_router"] = router(f[n + "gW"].T)
    for k in ("bo", "gb", "b2", "ln1_g", "ln1_b", "ln2_g", "ln2_b"):
        a[n + k] = f[n + k]
    for k in ("L2_ffn_ln1_g", "L2_ffn_ln1_b", "L2_xattn_input_norm_w"):
        a[k + "_f"] = np.ascontiguousarray(f[k].reshape(-1, 128).T)
    expert_weights("m2", [f[n + "W1"].transpose(0, 2, 1)], f[n + "W2"].transpose(0, 2, 1), 1)
    a["m2_b1"] = np.ascontiguousarray(f[n + "b1"].reshape(32, 128).T)
    rows = lambda w: np.ascontiguousarray(w.reshape(-1, 128, w.shape[1]).transpose(1, 0, 2))
    a["f0_w1"] = rows(f["L0_ffn_w1"].T)
    a["f0_w2"] = rows(f["L0_ffn_w2"].T)
    a["f0_taps"] = rows(f["L0_ffn_conv_w"][:, 0, :])
    a["f0_cb"] = np.ascontiguousarray(f["L0_ffn_conv_b"].reshape(8, 128).T)
    n = "L2_xattn_"
    for k, src in (("wk", "Wk"), ("wv", "Wv"), ("wq", "Wq"), ("wih", "gru_wih"), ("whh", "gru_whh")):
        a["g2_" + k] = rows(f[n + src].T)
    for k, src in (("bih", "gru_bih"), ("bhh", "gru_bhh"), ("norm", "slot_norm_w")):
        a["g2_" + k] = np.ascontiguousarray(f[n + src].reshape(-1, 128).T)
    return a


def kernel(**inputs):
    import concourse.bacc as bacc
    from concourse.bass_utils import run_bass_kernel_spmd

    nc = bacc.Bacc("TRN2", target_bir_lowering=False, num_devices=1)
    arrays = layout(inputs)
    aps = {k: nc.dram_tensor(k, v.shape, mybir.dt.from_np(v.dtype), kind="ExternalInput").ap()
           for k, v in arrays.items()}
    out = nc.dram_tensor("out", (B, NQ, D), F32, kind="ExternalOutput").ap()
    build(nc, aps, out)
    return run_bass_kernel_spmd(nc, [arrays], core_ids=[0]).results[0]["out"]
```

```python
import concourse.bass as bass
from concourse import mybir
from contextlib import ExitStack
import numpy as np

F32 = mybir.dt.float32
BF16 = mybir.dt.bfloat16
F32R = mybir.dt.float32r
ALU = mybir.AluOpType
ACT = mybir.ActivationFunctionType
AX = mybir.AxisListType

P = 128
D = 256
KC = D // P
B = 2
NQ = 512
NT = B * NQ
TQ = NT // P
NK = 1024
TK = B * NK // P
BANK = 512
ROUND = 1.5 * 2.0 ** 23


class Stage:

    spent = []

    def __init__(self, nc, name):
        self.nc, self.name, self.stack = nc, name, ExitStack()

    def __enter__(self):
        return self

    def __exit__(self, *a):
        return self.stack.__exit__(*a)

    def sb(self, name, shape, dt=F32):
        return self.stack.enter_context(self.nc.sbuf_tensor(f"{self.name}_{name}_s", shape, dt))

    def sem(self, name):
        handle = self.nc.alloc_semaphore(f"{self.name}_{name}")
        Stage.spent.append(handle)
        return handle

    def block(self):
        return self.stack.enter_context(self.nc.Block())


def clear_semaphores(nc):
    nc.clear_and_free_semaphores(Stage.spent)
    Stage.spent = []
    nc.all_engine_barrier()


class Chain:

    def __init__(self, eng, sem, base=0):
        self.eng, self.sem, self.base, self.n = eng, sem, base, 0

    def done(self, ins):
        ins.then_inc(self.sem, 1)
        self.n += 1
        return self.n

    def wait(self):
        self.eng.wait_ge(self.sem, self.base + self.n)

    def link(self, ins):
        self.done(ins)
        self.wait()


def constants(nc, ident, ones, slot_sum):
    with Stage(nc, "const") as s:
        filled, made = s.sem("filled"), s.sem("made")
        block = s.block()

        @block.gpsimd
        def _(pool):
            pool.memset(ident[:, :], 0.0).then_inc(filled, 1)
            pool.memset(ones[:, :], 1.0).then_inc(filled, 1)
            pool.memset(slot_sum[:, :], 0.0).then_inc(filled, 1)
            pool.wait_ge(filled, 3)
            pool.affine_select(out=ident[:, :], in_=ident[:, :], compare_op=ALU.not_equal, fill=1.0, base=0,
                               pattern=[[-1, P]], channel_multiplier=1).then_inc(made, 1)
            v = slot_sum[:, :].rearrange("p (a c) -> p a c", a=4)
            pool.affine_select(out=v, in_=v, compare_op=ALU.not_equal, fill=1.0, base=-16,
                               pattern=[[-32, 4], [0, 32]], channel_multiplier=1).then_inc(made, 1)
            pool.wait_ge(made, 2)


def load_x(nc, x_dram, x_sb):
    with Stage(nc, "loadx") as s:
        loaded = s.sem("loaded")
        block = s.block()

        @block.sync
        def _(sp):
            sp.dma_start(x_sb[:, :, :], x_dram.rearrange("b (t p) d -> p (b t) d", p=P)).then_inc(loaded, 16)
            sp.wait_ge(loaded, 16)


def store_x(nc, x_sb, out_dram):
    with Stage(nc, "storex") as s:
        stored = s.sem("stored")
        block = s.block()

        @block.sync
        def _(sp):
            sp.dma_start(out_dram.rearrange("b (t p) d -> p (b t) d", p=P), x_sb[:, :, :]).then_inc(stored, 16)
            sp.wait_ge(stored, 16)


def normalize(nc, name, ps, ident, src, nt, dst_t, eps, norms=1, rms=False, gain_dram=None, shift_dram=None,
              keep=None, src_dram=None):
    with Stage(nc, name) as s:
        rows = keep if keep is not None else s.sb("rows", [P, nt, D])
        stats = s.sb("stats", [P, nt, 6])
        mv = s.sb("mv", [P, nt, 2])
        var_eps = s.sb("var_eps", [P, nt])
        dev = s.sb("dev", [P, nt])
        rstd = s.sb("rstd", [P, nt])
        gs = s.sb("gs", [P, 2, KC])
        loaded, src_loaded = s.sem("loaded"), s.sem("src_loaded")
        steps = s.sem("steps")
        var_ready = s.sem("var_ready")
        dev_ready = s.sem("dev_ready")
        rows_ready = s.sem("rows_ready")
        turned = s.sem("turned")
        copied = s.sem("copied")
        block = s.block()
        affine = gain_dram is not None

        @block.sync
        def _(sp):
            if src_dram is not None:
                sp.dma_start(src[:, :, :], src_dram).then_inc(src_loaded, 16)
            if affine:
                sp.dma_start(gs[:, 0, :], gain_dram).then_inc(loaded, 16)
                if shift_dram is not None:
                    sp.dma_start(gs[:, 1, :], shift_dram).then_inc(loaded, 16)

        @block.vector
        def _(dve):
            c = Chain(dve, steps)
            if src_dram is not None:
                dve.wait_ge(src_loaded, 16)
            for n in range(norms):
                x = src if n == 0 else rows
                for t in range(nt):
                    c.done(nc.vector.bn_stats(stats[:, t, :], x[:, t, :]))
                c.wait()
                for t in range(nt):
                    c.done(nc.vector.bn_aggr(mv[:, t, :], stats[:, t, :]))
                c.wait()
                if rms:
                    c.link(nc.vector.tensor_tensor(var_eps[:, :], mv[:, :, 0], mv[:, :, 0], ALU.mult))
                    c.link(nc.vector.tensor_tensor(dev[:, :], var_eps[:, :], mv[:, :, 1], ALU.add))
                    c.done(nc.vector.tensor_scalar(var_eps[:, :], dev[:, :], eps, None, ALU.add))
                else:
                    c.done(nc.vector.tensor_scalar(var_eps[:, :], mv[:, :, 1], eps, None, ALU.add))
                c.wait()
                nc.vector.sem_inc(var_ready, 1)
                dve.wait_ge(dev_ready, n + 1)
                c.link(nc.vector.reciprocal(rstd[:, :], dev[:, :]))
                for t in range(nt):
                    if rms:
                        ins = nc.vector.tensor_scalar(rows[:, t, :], x[:, t, :], rstd[:, t:t + 1], None, ALU.mult)
                    else:
                        ins = nc.vector.tensor_scalar(rows[:, t, :], x[:, t, :], mv[:, t, 0:1], rstd[:, t:t + 1],
                                                      ALU.subtract, ALU.mult)
                    c.done(ins)
                c.wait()
            nc.vector.sem_inc(rows_ready, 1)

        @block.tensor
        def _(pe):
            pe.wait_ge(rows_ready, 1)
            unit = 0
            for k in range(KC):
                for t4 in range(nt // 4):
                    if unit >= 4:
                        pe.wait_ge(copied, unit - 3)
                    for j in range(4):
                        t = 4 * t4 + j
                        ins = nc.tensor.transpose(ps[:, unit % 4, j * P:(j + 1) * P], rows[:, t, k * P:(k + 1) * P],
                                                  ident[:, :])
                    ins.then_inc(turned, 1)
                    unit += 1

        @block.scalar
        def _(act):
            for n in range(norms):
                act.wait_ge(var_ready, n + 1)
                nc.scalar.activation(dev[:, :], var_eps[:, :], ACT.Sqrt).then_inc(dev_ready, 1)
            if affine:
                act.wait_ge(loaded, 32 if shift_dram is not None else 16)
            unit = 0
            for k in range(KC):
                for t4 in range(nt // 4):
                    act.wait_ge(turned, unit + 1)
                    out = dst_t[:, k, t4 * BANK:(t4 + 1) * BANK]
                    if affine and shift_dram is not None:
                        ins = nc.scalar.activation(out, ps[:, unit % 4, :], ACT.Identity, bias=gs[:, 1, k:k + 1],
                                                   scale=gs[:, 0, k:k + 1])
                    elif affine:
                        ins = nc.scalar.activation(out, ps[:, unit % 4, :], ACT.Copy, scale=gs[:, 0, k:k + 1])
                    else:
                        ins = nc.scalar.activation(out, ps[:, unit % 4, :], ACT.Copy)
                    ins.then_inc(copied, 1)
                    unit += 1
            act.wait_ge(copied, unit)


def transpose_rows(nc, name, ps, ident, src, nt, dst_t, src_dram):
    with Stage(nc, name) as s:
        loaded = s.sem("loaded")
        turned, copied = s.sem("turned"), s.sem("copied")
        block = s.block()

        @block.sync
        def _(sp):
            sp.dma_start(src[:, :, :], src_dram).then_inc(loaded, 16)

        @block.tensor
        def _(pe):
            pe.wait_ge(loaded, 16)
            unit = 0
            for k in range(KC):
                for t4 in range(nt // 4):
                    if unit >= 4:
                        pe.wait_ge(copied, unit - 3)
                    for j in range(4):
                        t = 4 * t4 + j
                        ins = nc.tensor.transpose(ps[:, unit % 4, j * P:(j + 1) * P], src[:, t, k * P:(k + 1) * P],
                                                  ident[:, :])
                    ins.then_inc(turned, 1)
                    unit += 1

        @block.scalar
        def _(act):
            unit = 0
            for k in range(KC):
                for t4 in range(nt // 4):
                    act.wait_ge(turned, unit + 1)
                    nc.scalar.activation(dst_t[:, k, t4 * BANK:(t4 + 1) * BANK], ps[:, unit % 4, :],
                                         ACT.Copy).then_inc(copied, 1)
                    unit += 1
            act.wait_ge(copied, unit)


def project_out(nc, name, ps, o_all, ngroups, wo_dram, bo_dram, acc, by_batch=False):
    with Stage(nc, name) as s:
        wo = s.sb("wo", [P, ngroups, D])
        bo = s.sb("bo", [P, D])
        w_loaded, b_loaded = s.sem("w_loaded"), s.sem("b_loaded")
        multiplied, added, biased = s.sem("multiplied"), s.sem("added"), s.sem("biased")
        block = s.block()

        @block.sync
        def _(sp):
            sp.dma_start(wo[:, :, :], wo_dram).then_inc(w_loaded, 16)
            if bo_dram is not None:
                sp.dma_start(bo[:, :], bo_dram.partition_broadcast(P)).then_inc(b_loaded, 16)

        @block.tensor
        def _(pe):
            pe.wait_ge(w_loaded, 16)
            for t in range(TQ):
                if t >= 4:
                    pe.wait_ge(added, t - 3)
                for g in range(ngroups):
                    o = (o_all[:, t // 4 * ngroups + g, t % 4 * P:(t % 4 + 1) * P] if by_batch
                         else o_all[:, g, t * P:(t + 1) * P])
                    ins = nc.tensor.matmul(ps[:, t % 4, 0:D], o, wo[:, g, :],
                                           start=(g == 0), stop=(g == ngroups - 1))
                ins.then_inc(multiplied, 1)

        @block.vector
        def _(dve):
            if bo_dram is not None:
                dve.wait_ge(b_loaded, 16)
                for t in range(TQ):
                    nc.vector.tensor_tensor(acc[:, t, :], acc[:, t, :], bo[:, :], ALU.add).then_inc(biased, 1)
                dve.wait_ge(biased, TQ)
            for t in range(TQ):
                dve.wait_ge(multiplied, t + 1)
                nc.vector.tensor_tensor(acc[:, t, :], acc[:, t, :], ps[:, t % 4, 0:D], ALU.add).then_inc(added, 1)
            dve.wait_ge(added, TQ)


def rope_attention(nc, name, ps, ones, q_t, ctx_t, w_dram, cos_dram, sin_dram, o_all):
    DH = 64
    G = 8
    SCALE = DH ** -0.5
    NC_ = NK // P
    with Stage(nc, name) as s:
        w = s.sb("w", [P, 3, KC, P])
        qm = s.sb("qm", [P, 2, NQ])
        cos = s.sb("cos", [P, NK])
        sin = s.sb("sin", [P, NK])
        k_cos = s.sb("k_cos", [P, NK])
        k_sin = s.sb("k_sin", [P, NK])
        k_rot = s.sb("k_rot", [P, NK])
        v = s.sb("v", [P, NC_, P])
        clipped = s.sb("clipped", [P, 3, 2 * NQ])
        probs = s.sb("probs", [P, 3, 2 * NQ])
        rden = s.sb("rden", [P, NQ])
        tables, zeroed, negated = s.sem("tables"), s.sem("zeroed"), s.sem("negated")
        w_loaded, w_free = s.sem("w_loaded"), s.sem("w_free")
        qkv_made = s.sem("qkv_made")
        q_ready, k_ready, v_ready = s.sem("q_ready"), s.sem("k_ready"), s.sem("v_ready")
        kparts = s.sem("kparts")
        scored = s.sem("scored")
        clip_done = s.sem("clip_done")
        exp_done = s.sem("exp_done")
        pv_done = s.sem("pv_done")
        rden_ready, o_done = s.sem("rden_ready"), s.sem("o_done")
        block = s.block()

        @block.sync
        def _(sp):
            for j in range(4):
                sp.dma_start(cos[32 * j:32 * j + 32, :], cos_dram).then_inc(tables, 16)
                sp.dma_start(sin[32 * j:32 * j + 32, :], sin_dram).then_inc(tables, 16)
            for b in range(B):
                with sp.Fori(0, G) as g:
                    sp.wait_ge(w_free, g + (b * G + 1))
                    sp.dma_start(w[:, :, :, :], w_dram[bass.ds(g, 1)].rearrange("a p k c n -> (a p) k c n")
                                 ).then_inc(w_loaded, 16)

        @block.tensor
        def _(pe):
            pe.wait_ge(zeroed, 1)
            nc.tensor.sem_inc(w_free, 1)
            for b in range(B):
                with pe.Fori(0, G) as g:
                    it = g + b * G
                    pe.wait_ge(w_loaded, 16 * it + 16)
                    pe.wait_ge(o_done, it + 1)
                    for c in range(KC):
                        nc.tensor.matmul(ps[:, 0, :], w[:, 0, c, :], q_t[:, c, b * NQ:(b + 1) * NQ],
                                         start=(c == 0), stop=(c == KC - 1))
                    for h in range(2):
                        for c in range(KC):
                            nc.tensor.matmul(ps[:, 1 + h, :], w[:, 1, c, :],
                                             ctx_t[:, c, b * NK + h * BANK:b * NK + (h + 1) * BANK],
                                             start=(c == 0), stop=(c == KC - 1))
                    for t in range(NC_):
                        for c in range(KC):
                            ins = nc.tensor.matmul(ps[:, 3 + t // 4, (t % 4) * P:(t % 4 + 1) * P],
                                                   ctx_t[:, c, b * NK + t * P:b * NK + (t + 1) * P], w[:, 2, c, :],
                                                   start=(c == 0), stop=(c == KC - 1))
                    ins.then_inc(qkv_made, 1)
                    pe.wait_ge(qkv_made, it + 1)
                    nc.tensor.sem_inc(w_free, 1)
                    pe.wait_ge(q_ready, it + 1)
                    pe.wait_ge(k_ready, it + 1)
                    pe.wait_ge(v_ready, it + 1)

                    def value_product(t):
                        pe.wait_ge(exp_done, it * NC_ + t + 1)
                        for h in range(2):
                            nc.tensor.matmul(ps[64 * h:64 * h + 64, 6, :], v[:, t, 64 * h:64 * h + 64],
                                             probs[:, t % 3, h * NQ:(h + 1) * NQ], start=(t == 0), stop=(t == NC_ - 1))
                        for h in range(2):
                            ins = nc.tensor.matmul(ps[64 * h:64 * h + 64, 7, :], ones[:, 0:64],
                                                   probs[:, t % 3, h * NQ:(h + 1) * NQ],
                                                   start=(t == 0), stop=(t == NC_ - 1))
                        ins.then_inc(pv_done, 1)

                    for t in range(NC_):
                        if t >= 3:
                            pe.wait_ge(clip_done, it * NC_ + t - 2)
                        for h in range(2):
                            ins = nc.tensor.matmul(ps[:, 2 * (t % 3) + h, :], k_rot[:, t * P:(t + 1) * P], qm[:, h, :],
                                                   start=True, stop=True)
                        ins.then_inc(scored, 1)
                        if t >= 2:
                            value_product(t - 2)
                    value_product(NC_ - 2)
                    value_product(NC_ - 1)

        @block.vector
        def _(dve):
            nc.vector.memset(qm[:, :, :], 0.0).then_inc(zeroed, 1)
            dve.wait_ge(tables, 8 * 16)
            nc.vector.tensor_scalar(sin[32:64, :], sin[32:64, :], -1.0, None, ALU.mult).then_inc(negated, 1)
            nc.vector.tensor_scalar(sin[96:128, :], sin[96:128, :], -1.0, None, ALU.mult).then_inc(negated, 1)
            dve.wait_ge(negated, 2)
            dve.wait_ge(zeroed, 1)
            nc.vector.sem_inc(o_done, 1)
            for b in range(B):
                with dve.Fori(0, G) as g:
                    it = g + b * G
                    dve.wait_ge(qkv_made, it + 1)
                    for h in range(2):
                        ins = nc.vector.tensor_scalar(qm[64 * h:64 * h + 64, h, :], ps[64 * h:64 * h + 64, 0, :],
                                                      SCALE, None, ALU.mult)
                    ins.then_inc(q_ready, 1)
                    k_ps = ps[:, 1:3, :].rearrange("p a n -> p (a n)")
                    nc.vector.tensor_tensor(k_cos[:, :], cos[:, :], k_ps, ALU.mult).then_inc(kparts, 1)
                    for j in range(4):
                        i = j ^ 1
                        nc.vector.tensor_tensor(k_sin[32 * j:32 * j + 32, :], k_ps[32 * i:32 * i + 32, :],
                                                sin[32 * i:32 * i + 32, :], ALU.mult).then_inc(kparts, 1)
                    dve.wait_ge(kparts, 5 * it + 5)
                    nc.vector.tensor_tensor(k_rot[:, :], k_cos[:, :], k_sin[:, :], ALU.add).then_inc(k_ready, 1)
                    for t in range(NC_):
                        dve.wait_ge(scored, it * NC_ + t + 1)
                        if t >= 3:
                            dve.wait_ge(exp_done, it * NC_ + t - 2)
                        nc.vector.tensor_scalar(
                            clipped[:, t % 3, :], ps[:, 2 * (t % 3):2 * (t % 3) + 2, :].rearrange("p a n -> p (a n)"),
                            11.0, -11.0, ALU.min, ALU.max).then_inc(clip_done, 1)
                    dve.wait_ge(pv_done, it * NC_ + NC_)
                    nc.vector.reciprocal(rden[:, :], ps[:, 7, :]).then_inc(rden_ready, 1)
                    dve.wait_ge(rden_ready, it + 1)
                    nc.vector.tensor_tensor(o_all[:, bass.ds(g, 1), b * NQ:(b + 1) * NQ].rearrange("p a n -> p (a n)"),
                                            ps[:, 6, :], rden[:, :], ALU.mult).then_inc(o_done, 1)
            dve.wait_ge(o_done, B * G + 1)

        @block.scalar
        def _(act):
            for b in range(B):
                with act.Fori(0, G) as g:
                    it = g + b * G
                    act.wait_ge(qkv_made, it + 1)
                    nc.scalar.activation(v[:, :, :].rearrange("p t n -> p (t n)"),
                                         ps[:, 3:5, :].rearrange("p a n -> p (a n)"), ACT.Copy).then_inc(v_ready, 1)
                    for t in range(NC_):
                        act.wait_ge(clip_done, it * NC_ + t + 1)
                        if t >= 3:
                            act.wait_ge(pv_done, it * NC_ + t - 2)
                        nc.scalar.activation(probs[:, t % 3, :], clipped[:, t % 3, :], ACT.Exp).then_inc(exp_done, 1)



def project_heads(nc, name, ps, x_t, kv_t, nk, w_dram, b_dram, q_parts, k_parts, v_groups):
    SCALE = 16 ** -0.5
    TV = B * nk // P
    with Stage(nc, name) as s:
        w = s.sb("w", [P, 3, KC, D])
        bias = s.sb("bias", [P, 2, KC])
        v_all = s.sb("v_all", [P, 8, nk // P, 4, 32])
        full = s.sb("full", [P, 3, BANK])
        hi, lo = s.sb("hi", [P, 3, BANK], F32R), s.sb("lo", [P, 3, BANK], F32R)
        loaded, scaled = s.sem("loaded"), s.sem("scaled")
        made = s.sem("made")
        full_ready = s.sem("full_ready")
        hi_ready = s.sem("hi_ready")
        lo_ready = s.sem("lo_ready")
        hi_stored = [s.sem(f"hi_stored{j}") for j in range(3)]
        lo_stored = [s.sem(f"lo_stored{j}") for j in range(3)]
        v_ready, v_cleared, v_stored = s.sem("v_ready"), s.sem("v_cleared"), s.sem("v_stored")
        block = s.block()
        units = [(0, m, b, 0) for m in range(KC) for b in range(B)]
        units += [(1, m, b, j) for m in range(KC) for b in range(B) for j in range(nk // BANK)]
        U = len(units)

        def dest(what, part, m, b, j):
            if what == 0:
                return q_parts[part, b * 4 + 2 * m:b * 4 + 2 * m + 2].rearrange("g r h n -> (g r h) n")
            return k_parts[b * 4 + 2 * m:b * 4 + 2 * m + 2, :, part, :, j * BANK:(j + 1) * BANK].rearrange(
                "g r h n -> (g r) h n")

        @block.sync
        def _(sp):
            sp.dma_start(w[:, :, :, :], w_dram).then_inc(loaded, 16)
            sp.dma_start(bias[:, :, :], b_dram).then_inc(loaded, 16)
            for u, (what, m, b, j) in enumerate(units):
                sp.wait_ge(hi_ready, u + 1)
                sp.dma_start(dest(what, 0, m, b, j), hi[:, u % 3, :].bitcast(F32)).then_inc(hi_stored[u % 3], 16)
                sp.wait_ge(lo_ready, u + 1)
                sp.dma_start(dest(what, 1, m, b, j), lo[:, u % 3, :].bitcast(F32)).then_inc(lo_stored[u % 3], 16)
            sp.wait_ge(v_cleared, 2)
            sp.dma_start(v_groups.rearrange("g p n -> p g n"), v_all[:, :, :, :, :].rearrange("p g c h n -> p g (c h n)")
                         ).then_inc(v_stored, 16)
            sp.wait_ge(v_stored, 16)
            for j in range(3):
                sp.wait_ge(hi_stored[j], 16 * len(range(j, U, 3)))
                sp.wait_ge(lo_stored[j], 16 * len(range(j, U, 3)))

        @block.tensor
        def _(pe):
            pe.wait_ge(loaded, 32)
            for u, (what, m, b, j) in enumerate(units):
                if u >= 4:
                    pe.wait_ge(full_ready, u - 3)
                src = x_t[:, :, b * NQ:(b + 1) * NQ] if what == 0 else kv_t[:, :, b * nk + j * BANK:b * nk + (j + 1) * BANK]
                for c in range(KC):
                    ins = nc.tensor.matmul(ps[:, u % 4, :], w[:, what, c, m * P:(m + 1) * P], src[:, c, :],
                                           start=(c == 0), stop=(c == KC - 1))
                ins.then_inc(made, 1)
            for t in range(TV):
                if t >= 4:
                    pe.wait_ge(v_ready, t - 3)
                for c in range(KC):
                    ins = nc.tensor.matmul(ps[:, 4 + t % 4, 0:D], kv_t[:, c, t * P:(t + 1) * P], w[:, 2, c, :],
                                           start=(c == 0), stop=(c == KC - 1))
                ins.then_inc(made, 1)

        @block.scalar
        def _(act):
            act.wait_ge(scaled, 1)
            for u, (what, m, b, j) in enumerate(units):
                act.wait_ge(made, u + 1)
                if u >= 3:
                    act.wait_ge(lo_ready, u - 2)
                nc.scalar.activation(full[:, u % 3, :], ps[:, u % 4, :], ACT.Identity, bias=bias[:, what, m:m + 1],
                                     scale=SCALE if what == 0 else 1.0).then_inc(full_ready, 1)

        @block.vector
        def _(dve):
            dve.wait_ge(loaded, 32)
            nc.vector.tensor_scalar(bias[:, 0, :], bias[:, 0, :], SCALE, None, ALU.mult).then_inc(scaled, 1)
            for u in range(U):
                dve.wait_ge(full_ready, u + 1)
                if u >= 3:
                    dve.wait_ge(hi_stored[u % 3], 16 * (u // 3))
                    dve.wait_ge(lo_stored[u % 3], 16 * (u // 3))
                nc.vector.tensor_copy(hi[:, u % 3, :], full[:, u % 3, :]).then_inc(hi_ready, 1)
                dve.wait_ge(hi_ready, u + 1)
                nc.vector.tensor_tensor(lo[:, u % 3, :], full[:, u % 3, :], hi[:, u % 3, :].bitcast(F32), ALU.subtract
                                        ).then_inc(lo_ready, 1)
            dve.wait_ge(v_cleared, 1)
            for t in range(TV):
                dve.wait_ge(made, U + t + 1)
                b, c = divmod(t, nk // P)
                nc.vector.tensor_copy(v_all[:, b * 4:b * 4 + 4, c, :, 0:16],
                                      ps[:, 4 + t % 4, 0:D].rearrange("p (g h n) -> p g h n", g=4, h=4)
                                      ).then_inc(v_ready, 1)
            dve.wait_ge(v_ready, TV)
            nc.vector.memset(v_all[:, :, :, :, 16:17].rearrange("p g c h o -> p (g c) (h o)"), 1.0
                             ).then_inc(v_cleared, 1)
            dve.wait_ge(v_cleared, 2)

        @block.gpsimd
        def _(pool):
            pool.memset(v_all[:, :, :, :, :].rearrange("p g c h n -> p (g c h n)"), 0.0).then_inc(v_cleared, 1)


def head_attention(nc, name, ps, ident, slot_sum, nk, q_parts, k_parts, v_groups, bv_dram, o_all, sparse):
    G, S = 8, 4
    NC_ = nk // P
    NH = nk // BANK
    QT = NQ // P
    ROWS = S * QT
    FIRST = ROWS * NH
    SECOND = NC_ * 2
    CAND = NC_ * 8
    LOADS = 16 * 5
    with Stage(nc, name) as s:
        qa = s.sb("qa", [P, 2, S, NQ], F32R)
        ka = s.sb("ka", [P, 2, S, nk], F32R)
        v = s.sb("v", [P, 2, NC_, S, 32])
        bv = s.sb("bv", [P, G])
        shift = s.sb("shift", [P, ROWS])
        half_max = s.sb("half_max", [P, ROWS, NH])
        minus_hi, minus_lo = s.sb("minus_hi", [ROWS, P], F32R), s.sb("minus_lo", [ROWS, P], F32R)
        probs = s.sb("probs", [P, 4, 2 * NQ])
        o_raw = s.sb("o_raw", [P, NQ])
        rden = s.sb("rden", [P, NQ])
        if sparse:
            T = {}
            T["sc"] = s.sb("sc", [P, ROWS, nk])
            T["cand"] = s.sb("cand", [P, ROWS, CAND])
            T["above"] = s.sb("above", [P, ROWS, CAND])
            T["best"] = s.sb("best", [P, ROWS, 8])
            T["ranks"] = s.sb("ranks", [P, 8])
            for n in ("count", "total", "rcount", "tau", "ntau"):
                T[n] = s.sb(n, [P, ROWS])
            T["over"] = s.sb("over", [P, nk], BF16)
            T["over2"] = s.sb("over2", [P, nk], BF16)
            T["zero"] = s.sb("zero", [P, nk], BF16)
            T["worst"] = s.sb("worst", [P, 1])
            T["worst_all"] = s.sb("worst_all", [1, 1])
            T["flag"] = s.sb("flag", [1, 1], mybir.dt.int32)
        zeroed, ones_set, bv_loaded = s.sem("zeroed"), s.sem("ones_set"), s.sem("bv_loaded")
        qk_loaded = [s.sem("qk_loaded0"), s.sem("qk_loaded1")]
        rows_made = s.sem("rows_made")
        rows_used = s.sem("rows_used")
        rows_kept = s.sem("rows_kept")
        shift_ready = s.sem("shift_ready")
        shift_turned = s.sem("shift_turned")
        hi_ready, lo_ready = s.sem("hi_ready"), s.sem("lo_ready")
        shift_clearing = s.sem("shift_clearing")
        shift_cleared = s.sem("shift_cleared")
        shift_placed = s.sem("shift_placed")
        scored = s.sem("scored")
        exp_done = s.sem("exp_done")
        pv_done = s.sem("pv_done")
        o_copied, o_summed, o_scaled, o_done = s.sem("o_copied"), s.sem("o_summed"), s.sem("o_scaled"), s.sem("o_done")
        rden_ready = s.sem("rden_ready")
        steps = s.sem("steps")
        if sparse:
            for n in ("rows_seen", "tau_set", "summed", "worst_ready", "worst_turned", "rescue"):
                T[n] = s.sem(n)
        block = s.block()

        def over_groups(eng, first, step):
            first()
            with eng.Fori(0, G // 2 - 1) as i:
                step(2 * i, 0, True)
                step(2 * i + 1, 1, True)
            step(G - 2, 0, True)
            step(G - 1, 1, False)

        @block.sync
        def _(sp):
            def load(n, buf):
                for i in range(2):
                    sp.dma_start(qa[32 * i:32 * i + 32, buf, :, :].rearrange("r h n -> r (h n)").bitcast(F32),
                                 q_parts[i, bass.ds(n, 1)].rearrange("o r h n -> (o r) (h n)").unsqueeze(1).to_broadcast(
                                     [16, 2, S * NQ])).then_inc(qk_loaded[buf], 16)
                    sp.dma_start(ka[32 * i:32 * i + 32, buf, :, :].rearrange("r h n -> r (h n)").bitcast(F32),
                                 k_parts[bass.ds(n, 1)].rearrange("o r a h n -> (o r a) (h n)")
                                 ).then_inc(qk_loaded[buf], 16)
                sp.dma_start(v[:, buf, :, :, :].rearrange("p c h n -> p (c h n)"),
                             v_groups[bass.ds(n, 1)].rearrange("o p n -> (o p) n")).then_inc(qk_loaded[buf], 16)

            def place(n, buf):
                sp.wait_ge(lo_ready, n + 1)
                for part, src in enumerate((minus_hi, minus_lo)):
                    sp.dma_start(qa[64 + part:65 + part, buf, :, :].rearrange("o h (t n) -> o (h t) n", n=P).bitcast(F32),
                                 src[:, :].bitcast(F32)).then_inc(shift_placed, 16)

            sp.dma_start(bv[:, :], bv_dram).then_inc(bv_loaded, 16)
            sp.wait_ge(zeroed, 3)
            load(0, 0)
            load(1, 1)

            def step(n, buf, more):
                if more:
                    place(n + 1, 1 - buf)
                    sp.wait_ge(pv_done, NC_ * n + NC_)
                    if not isinstance(n, int):
                        load(n + 2, buf)

            place(0, 0)
            with sp.Fori(0, G // 2 - 1) as i:
                step(2 * i, 0, True)
                step(2 * i + 1, 1, True)
            step(G - 2, 0, True)

        @block.gpsimd
        def _(pool):
            pool.memset(qa[:, :, :, :].bitcast(F32), 0.0).then_inc(zeroed, 1)
            pool.memset(ka[:, :, :, :].bitcast(F32), 0.0).then_inc(zeroed, 1)
            pool.wait_ge(zeroed, 2)
            pool.memset(ka[64:66, :, :, :].bitcast(F32), 1.0).then_inc(zeroed, 1)
            pool.wait_ge(zeroed, 3)

            def clear(n, buf):
                pool.wait_ge(pv_done, NC_ * n + NC_)
                nc.gpsimd.sem_inc(shift_clearing, 1)
                pool.memset(qa[64:66, buf, :, :].bitcast(F32), 0.0).then_inc(shift_cleared, 1)

            with pool.Fori(0, G // 2 - 1) as i:
                clear(2 * i, 0)
                clear(2 * i + 1, 1)

        @block.tensor
        def _(pe):
            pe.wait_ge(zeroed, 3)

            def first_bank(n, buf, f):
                if f == 0:
                    pe.wait_ge(qk_loaded[buf], (n - buf) * (LOADS // 2) + LOADS)
                    pe.wait_ge(shift_cleared, n + 1)
                if f < 2:
                    pe.wait_ge(rows_used, n * FIRST + 2)
                else:
                    pe.wait_ge(rows_used, n * FIRST + f + 1)
                if sparse:
                    pe.wait_ge(rows_kept, n * FIRST + f + 1)
                r, j = divmod(f, NH)
                h, t = divmod(r, QT)
                nc.tensor.matmul(ps[:, f % 2, :], qa[:, buf, h, t * P:(t + 1) * P],
                                 ka[:, buf, h, j * BANK:(j + 1) * BANK], start=True, stop=True).then_inc(rows_made, 1)

            def turn(n):
                pe.wait_ge(shift_ready, n + 1)
                if not (isinstance(n, int) and n == 0):
                    pe.wait_ge(o_done, n)
                nc.tensor.transpose(ps[0:ROWS, 7, 0:P], shift[:, :], ident[:, :]).then_inc(shift_turned, 1)

            def second_pair(n, buf, u):
                t = u // 2
                if u == 0:
                    pe.wait_ge(shift_placed, 32 * n + 32)
                    pe.wait_ge(o_copied, n + 1)
                if u < 2:
                    pe.wait_ge(exp_done, n * SECOND + 2)
                else:
                    pe.wait_ge(exp_done, n * SECOND + u + 1)
                for j in range(2):
                    ins = nc.tensor.matmul(ps[:, 2 + 2 * (u % 2) + j, :], ka[:, buf, 2 * (u % 2) + j, t * P:(t + 1) * P],
                                           qa[:, buf, 2 * (u % 2) + j, :], start=True, stop=True)
                ins.then_inc(scored, 1)

            def value_products(n, buf, t):
                pe.wait_ge(exp_done, n * SECOND + 2 * t + 4)
                for h in range(S):
                    ins = nc.tensor.matmul(ps[32 * h:32 * h + 32, 6, :], v[:, buf, t, h, :],
                                           probs[:, (2 * t + h // 2) % 4, (h % 2) * NQ:(h % 2 + 1) * NQ],
                                           start=(t == 0), stop=(t == NC_ - 1))
                ins.then_inc(pv_done, 1)

            def denominators(n, more):
                pe.wait_ge(o_copied, n + 2)
                if more:
                    pe.wait_ge(lo_ready, n + 2)
                nc.tensor.matmul(ps[:, 7, :], slot_sum[:, :], o_raw[:, :], start=True, stop=True).then_inc(o_summed, 1)

            def worst(n):
                pe.wait_ge(T["worst_ready"], n + 1)
                nc.tensor.transpose(ps[0:1, 7, 0:P], T["worst"][:, :], ident[:, :]).then_inc(T["worst_turned"], 1)

            def first():
                nc.tensor.sem_inc(rows_used, 2)
                nc.tensor.sem_inc(shift_cleared, 2)
                nc.tensor.sem_inc(o_done, 1)
                nc.tensor.sem_inc(exp_done, 2)
                nc.tensor.sem_inc(o_copied, 1)
                if sparse:
                    nc.tensor.sem_inc(rows_kept, 2)
                for f in range(FIRST):
                    first_bank(0, 0, f)
                if sparse:
                    worst(0)
                turn(0)

            def step(n, buf, more):
                f = 0
                if sparse and more:
                    for f in range(FIRST):
                        first_bank(n + 1, 1 - buf, f)
                    f = FIRST
                for u in range(SECOND):
                    second_pair(n, buf, u)
                    if u % 2 == 1 and u >= 3:
                        value_products(n, buf, u // 2 - 1)
                    if more and not sparse and u >= SECOND // 4:
                        while f < min(FIRST, (u + 1 - SECOND // 4) * 4 * FIRST // (SECOND * 2)):
                            first_bank(n + 1, 1 - buf, f)
                            f += 1
                value_products(n, buf, NC_ - 1)
                if more:
                    for f in range(f, FIRST):
                        first_bank(n + 1, 1 - buf, f)
                    if not sparse:
                        turn(n + 1)
                denominators(n, more and not sparse)
                if more and sparse:
                    pe.wait_ge(o_done, n + 2)
                    worst(n + 1)
                    turn(n + 1)

            over_groups(pe, first, step)

        FINISH = 0

        @block.vector
        def _(dve):
            def first_product(n):
                for f in range(FIRST):
                    r, j = divmod(f, NH)
                    dve.wait_ge(rows_made, n * FIRST + f + 1)
                    if sparse:
                        nc.vector.sem_inc(T["rows_seen"], 1)
                        for c in range(BANK // P):
                            ins = nc.vector.max(T["cand"][:, r, 8 * (c + j * 4):8 * (c + j * 4) + 8],
                                                ps[:, f % 2, c * P:(c + 1) * P])
                    else:
                        ins = nc.vector.reduce_max(half_max[:, r, j:j + 1], ps[:, f % 2, :], AX.X)
                    ins.then_inc(rows_used, 1)
                dve.wait_ge(rows_used, n * FIRST + FIRST + 2)
                if sparse:
                    thresholds(nc, dve, T, n, ps, rows_kept, shift, ROWS, nk, steps)
                    nc.vector.sem_inc(shift_ready, 1)
                else:
                    nc.vector.reduce_max(shift[:, :], half_max[:, :, :], AX.X).then_inc(shift_ready, 1)

            def cut(n):
                dve.wait_ge(shift_turned, n + 1)
                if not (isinstance(n, int) and n == 0):
                    dve.wait_ge(shift_placed, 32 * n)
                nc.vector.tensor_scalar(minus_hi[:, :], ps[0:ROWS, 7, 0:P], -1.0, None, ALU.mult).then_inc(hi_ready, 1)
                dve.wait_ge(hi_ready, n + 1)
                nc.vector.scalar_tensor_tensor(minus_lo[:, :], ps[0:ROWS, 7, 0:P], -1.0, minus_hi[:, :].bitcast(F32),
                                               ALU.mult, ALU.subtract).then_inc(lo_ready, 1)

            def finish(n):
                dve.wait_ge(o_summed, n + 1)
                nc.vector.reciprocal(rden[:, :], ps[:, 7, :]).then_inc(rden_ready, 1)
                dve.wait_ge(rden_ready, n + 1)
                nc.vector.tensor_tensor(rden[:, :], o_raw[:, :], rden[:, :], ALU.mult).then_inc(o_scaled, 1)
                dve.wait_ge(o_scaled, n + 1)
                nc.vector.tensor_scalar(o_all[:, bass.ds(n, 1), :].rearrange("p a n -> p (a n)"), rden[:, :],
                                        bv[:, bass.ds(n, 1)], None, ALU.add).then_inc(o_done, 1)

            def first():
                if sparse:
                    for j in range(8):
                        nc.vector.memset(T["ranks"][:, j:j + 1], 1.0 / (j + 1)).then_inc(ones_set, 1)
                    nc.vector.memset(T["zero"][:, :], 0.0).then_inc(ones_set, 1)
                    dve.wait_ge(ones_set, 9)
                dve.wait_ge(bv_loaded, 16)
                first_product(0)
                cut(0)

            def step(n, buf, more):
                if more:
                    if sparse:
                        first_product_and_finish(n)
                    else:
                        first_product(n + 1)
                    cut(n + 1)
                    if not sparse:
                        finish(n)
                else:
                    finish(n)

            def first_product_and_finish(n):
                T["between"] = lambda: finish(n)
                first_product(n + 1)
                T["between"] = None

            T_ = T if sparse else None
            if sparse:
                T["between"] = None
            over_groups(dve, first, step)
            dve.wait_ge(o_done, G + 1)

        @block.scalar
        def _(act):
            def keep(n):
                for f in range(FIRST):
                    r, j = divmod(f, NH)
                    act.wait_ge(rows_used, n * FIRST + f + 3)
                    nc.scalar.activation(T["sc"][:, r, j * BANK:(j + 1) * BANK], ps[:, f % 2, :], ACT.Copy
                                         ).then_inc(rows_kept, 1)

            def first():
                if sparse:
                    keep(0)
                    sums(nc, act, T, 0, ROWS, nk, rows_kept, FIRST)

            def step(n, buf, more):
                if sparse and more:
                    keep(n + 1)
                for u in range(SECOND):
                    act.wait_ge(scored, n * SECOND + u + 1)
                    if u >= 4:
                        act.wait_ge(pv_done, n * NC_ + u // 2 - 1)
                    nc.scalar.activation(probs[:, u % 4, :],
                                         ps[:, 2 + 2 * (u % 2):4 + 2 * (u % 2), :].rearrange("p a n -> p (a n)"),
                                         ACT.Relu if sparse else ACT.Exp).then_inc(exp_done, 1)
                act.wait_ge(o_done, n + 1)
                act.wait_ge(pv_done, n * NC_ + NC_)
                nc.scalar.activation(o_raw[:, :], ps[:, 6, :], ACT.Copy).then_inc(o_copied, 1)
                if more and sparse:
                    sums(nc, act, T, n + 1, ROWS, nk, rows_kept, FIRST)

            over_groups(act, first, step)


CANDIDATE_STEPS = 4
NEWTON = 2
RESCUE = 20
EXCESS = 3e-5
THRESHOLD_STEPS = 1 + 8 + 2 + 4 * CANDIDATE_STEPS + 1 + NEWTON * 3 + 1 + 1 + 1 + 1 + 2
COUNTS = 16


def sums(nc, act, T, n, rows, nk, rows_kept, first):
    act.wait_ge(rows_kept, n * first + first + 2)
    per = NEWTON * rows + rows // 2
    for k in range(NEWTON + 1):
        act.wait_ge(T["tau_set"], n * (NEWTON + 1) + k + 1)
        for r in range(rows if k < NEWTON else rows // 2):
            done = n * per + k * rows + r
            if not (isinstance(n, int) and n == 0 and k == 0 and r == 0):
                act.wait_ge(T["summed"], done)
            nc.scalar.activation(T["over"][:, :], T["sc"][:, r, :], ACT.Relu, bias=T["ntau"][:, r:r + 1],
                                 accum_out=T["total"][:, r:r + 1]).then_inc(T["summed"], 1)


def thresholds(nc, dve, T, n, ps, rows_kept, shift, rows, nk, steps):
    cand, above, best, tau, ntau = T["cand"], T["above"], T["best"], T["tau"], T["ntau"]
    count, total, rcount = T["count"], T["total"], T["rcount"]
    CAND = cand.shape[2]
    PER = rows + 7 + 2 + 6 * CANDIDATE_STEPS + 1 + NEWTON * (rows + 4) + rows // 2 + 1 + 2 + 1
    own = Chain(dve, steps, n * PER)

    def wide(a, m):
        return a[:, :].unsqueeze(2).to_broadcast([P, rows, m])

    nc.vector.sem_inc(T["rows_seen"], 1)
    for r in range(rows):
        own.done(nc.vector.max(best[:, r, :], cand[:, r, :]))
    own.wait()
    for j in range(1, 8):
        own.link(nc.vector.tensor_tensor(best[:, :, j], best[:, :, j], best[:, :, j - 1], ALU.add))
    own.link(nc.vector.scalar_tensor_tensor(best[:, :, :], best[:, :, :], -1.0,
                                            T["ranks"][:, :].unsqueeze(1).to_broadcast([P, rows, 8]), ALU.add, ALU.mult))
    own.link(nc.vector.reduce_max(tau[:, :], best[:, :, :], AX.X))
    for k in range(CANDIDATE_STEPS):
        own.link(nc.vector.tensor_tensor(above[:, :, :], cand[:, :, :], wide(tau, CAND), ALU.is_gt))
        own.link(nc.vector.reduce_sum(count[:, :], above[:, :, :], AX.X))
        own.link(nc.vector.tensor_tensor(above[:, :, :], above[:, :, :], cand[:, :, :], ALU.mult))
        own.link(nc.vector.reduce_sum(total[:, :], above[:, :, :], AX.X))
        own.link(nc.vector.reciprocal(rcount[:, :], count[:, :]))
        own.link(nc.vector.scalar_tensor_tensor(tau[:, :], total[:, :], -1.0, rcount[:, :], ALU.add, ALU.mult))
    own.link(nc.vector.tensor_scalar(ntau[:, :], tau[:, :], -1.0, None, ALU.mult))
    dve.wait_ge(rows_kept, n * rows * (nk // BANK) + rows * (nk // BANK) + 2)
    per = NEWTON * rows + rows // 2
    for k in range(NEWTON):
        nc.vector.sem_inc(T["tau_set"], 1)
        for r in range(rows):
            own.link(nc.vector.tensor_scalar(T["over2"][:, :], T["sc"][:, r, :], tau[:, r:r + 1], 0.0, ALU.is_gt,
                                             ALU.add, accum_out=count[:, r:r + 1]))
        own.link(nc.vector.reciprocal(rcount[:, :], count[:, :]))
        if k == 0 and T["between"] is not None:
            T["between"]()
        dve.wait_ge(T["summed"], n * per + (k + 1) * rows)
        own.link(nc.vector.scalar_tensor_tensor(total[:, :], total[:, :], -1.0, rcount[:, :], ALU.add, ALU.mult))
        own.link(nc.vector.tensor_tensor(tau[:, :], tau[:, :], total[:, :], ALU.add))
        own.link(nc.vector.tensor_scalar(ntau[:, :], tau[:, :], -1.0, None, ALU.mult))
    nc.vector.sem_inc(T["tau_set"], 1)
    for r in range(rows // 2, rows):
        own.link(nc.vector.scalar_tensor_tensor(T["over2"][:, :], T["sc"][:, r, :], tau[:, r:r + 1], T["zero"][:, :],
                                                ALU.subtract, ALU.max, accum_out=total[:, r:r + 1]))
    dve.wait_ge(T["summed"], n * per + per)
    own.link(nc.vector.reduce_max(T["worst"][:, :], total[:, :], AX.X))
    nc.vector.sem_inc(T["worst_ready"], 1)
    dve.wait_ge(T["worst_turned"], n + 1)
    own.link(nc.vector.reduce_max(T["worst_all"][:, :], ps[0:1, 7, 0:P], AX.X))
    own.link(nc.vector.tensor_scalar(T["flag"][:, :], T["worst_all"][:, :], 1.0 + EXCESS, None, ALU.is_gt))
    nc.vector.sem_inc(T["rows_seen"], 1)
    late = dve.value_load(T["flag"][0:1, 0:1], min_val=0, max_val=1)
    LONG = RESCUE * (2 * rows + 3)
    with dve.If(late > 0):
        with dve.Fori(0, RESCUE) as k:
            more = Chain(dve, T["rescue"], n * LONG + k * (2 * rows + 3))
            for r in range(rows):
                more.link(nc.vector.tensor_scalar(T["over2"][:, :], T["sc"][:, r, :], tau[:, r:r + 1], 0.0, ALU.is_gt,
                                                  ALU.add, accum_out=count[:, r:r + 1]))
                more.link(nc.vector.scalar_tensor_tensor(T["over2"][:, :], T["sc"][:, r, :], tau[:, r:r + 1],
                                                         T["zero"][:, :], ALU.subtract, ALU.max,
                                                         accum_out=total[:, r:r + 1]))
            more.link(nc.vector.reciprocal(rcount[:, :], count[:, :]))
            more.link(nc.vector.scalar_tensor_tensor(total[:, :], total[:, :], -1.0, rcount[:, :], ALU.add, ALU.mult))
            more.link(nc.vector.tensor_tensor(tau[:, :], tau[:, :], total[:, :], ALU.add))
            assert more.n == 2 * rows + 3
    with dve.Else():
        nc.vector.sem_inc(T["rescue"], LONG)
    own.link(nc.vector.tensor_copy(shift[:, :], tau[:, :]))
    assert own.n == PER, (own.n, PER)

LOW, HIGH = -3.0e38, 3.0e38


def top_mask(nc, own, vals, n, k, buf, top, mask):
    tiles = vals.shape[1]
    own.link(nc.vector.memset(buf[:, :, :], LOW))
    own.link(nc.vector.tensor_copy(buf[:, :, 0:n], vals))
    for t in range(tiles):
        own.done(nc.vector.max(top[:, t, :], buf[:, t, :]))
    own.wait()
    own.link(nc.vector.memset(top[:, :, k:8], LOW))
    for t in range(tiles):
        own.done(nc.vector.match_replace(out=buf[:, t, :], in_to_replace=top[:, t, :], in_values=buf[:, t, :],
                                         imm_value=HIGH))
    own.wait()
    own.link(nc.vector.tensor_scalar(mask, buf[:, :, 0:n], HIGH, None, ALU.is_equal))


def route(nc, name, ps, x_t, n, w_dram, bias_dram, kind, cw):
    with Stage(nc, name) as s:
        w = s.sb("w", [P, KC, n])
        bias = s.sb("bias", [P, n])
        logits = s.sb("logits", [P, TQ, n])
        scores = s.sb("scores", [P, TQ, n])
        picked = s.sb("picked", [P, TQ, n])
        mask = s.sb("mask", [P, TQ, n])
        buf = s.sb("buf", [P, TQ, 24])
        top = s.sb("top", [P, TQ, 8])
        total = s.sb("total", [P, TQ])
        rtotal = s.sb("rtotal", [P, TQ])
        if kind == "grouped":
            low_high = s.sb("low_high", [P, TQ, 4, 2, 2])
            best = s.sb("best", [P, TQ, 4])
            gmask = s.sb("gmask", [P, TQ, 4])
            gbuf = s.sb("gbuf", [P, TQ, 16])
            biased = s.sb("biased", [P, TQ, n])
            masked = s.sb("masked", [P, TQ, n])
        loaded, made = s.sem("loaded"), s.sem("made")
        logits_ready, scores_ready, steps = s.sem("logits_ready"), s.sem("scores_ready"), s.sem("steps")
        block = s.block()

        def wide(a, m):
            return a.unsqueeze(2).to_broadcast([P, TQ, m])

        @block.sync
        def _(sp):
            sp.dma_start(w[:, :, :], w_dram).then_inc(loaded, 16)
            sp.dma_start(bias[:, :], bias_dram.partition_broadcast(P)).then_inc(loaded, 16)

        @block.tensor
        def _(pe):
            pe.wait_ge(loaded, 32)
            for t in range(TQ):
                for c in range(KC):
                    ins = nc.tensor.matmul(ps[:, 0, t * n:(t + 1) * n], x_t[:, c, t * P:(t + 1) * P], w[:, c, :],
                                           start=(c == 0), stop=(c == KC - 1))
            ins.then_inc(made, 1)

        @block.scalar
        def _(act):
            act.wait_ge(logits_ready, 1)
            nc.scalar.activation(scores[:, :, :], logits[:, :, :], ACT.Exp if kind == "softmax" else ACT.Sigmoid
                                 ).then_inc(scores_ready, 1)

        @block.vector
        def _(dve):
            own = Chain(dve, steps)
            dve.wait_ge(loaded, 32)
            dve.wait_ge(made, 1)
            all_logits = ps[:, 0, 0:TQ * n].rearrange("p (t n) -> p t n", t=TQ)
            row_bias = bias[:, :].unsqueeze(1).to_broadcast([P, TQ, n])
            if kind == "grouped":
                own.link(nc.vector.tensor_copy(logits[:, :, :], all_logits))
            else:
                own.link(nc.vector.tensor_tensor(logits[:, :, :], row_bias, all_logits, ALU.add))
            if kind == "softmax":
                own.link(nc.vector.reduce_max(total[:, :], logits[:, :, :], AX.X))
                own.link(nc.vector.tensor_tensor(logits[:, :, :], logits[:, :, :], wide(total[:, :], n),
                                                 ALU.subtract))
            nc.vector.sem_inc(logits_ready, 1)
            dve.wait_ge(scores_ready, 1)
            if kind == "softmax":
                own.link(nc.vector.reduce_sum(total[:, :], scores[:, :, :], AX.X))
                own.link(nc.vector.reciprocal(rtotal[:, :], total[:, :]))
                own.link(nc.vector.tensor_tensor(scores[:, :, :], scores[:, :, :], wide(rtotal[:, :], n), ALU.mult))
                top_mask(nc, own, scores[:, :, :], n, 2, buf, top, mask[:, :, :])
                own.link(nc.vector.tensor_tensor(cw[:, :, 0:n], scores[:, :, :], mask[:, :, :], ALU.mult))
                return
            if kind == "top2":
                top_mask(nc, own, scores[:, :, :], n, 2, buf, top, mask[:, :, :])
                factor = 1.0
            else:
                own.link(nc.vector.tensor_tensor(biased[:, :, :], scores[:, :, :], row_bias, ALU.add))
                v = biased[:, :, :].rearrange("p t (g a c) -> p (t g) a c", g=4, a=2)
                lh = low_high[:, :, :, :, :].rearrange("p t g a c -> p (t g) a c")
                own.done(nc.vector.tensor_tensor(lh[:, :, 0, :], v[:, :, :, 0], v[:, :, :, 1], ALU.add))
                own.link(nc.vector.tensor_tensor(lh[:, :, 1, :], v[:, :, :, 0], v[:, :, :, 1], ALU.max))
                b4 = best[:, :, :].rearrange("p t g -> p (t g)")
                own.link(nc.vector.tensor_tensor(b4, lh[:, :, 1, 0], lh[:, :, 1, 1], ALU.add))
                own.link(nc.vector.tensor_tensor(b4, b4, lh[:, :, 0, 0], ALU.max))
                own.link(nc.vector.tensor_tensor(b4, b4, lh[:, :, 0, 1], ALU.max))
                top_mask(nc, own, best[:, :, :], 4, 2, gbuf, top, gmask[:, :, :])
                own.link(nc.vector.tensor_tensor(
                    masked[:, :, :].rearrange("p t (g c) -> p (t g) c", g=4),
                    biased[:, :, :].rearrange("p t (g c) -> p (t g) c", g=4),
                    gmask[:, :, :].rearrange("p t g -> p (t g)").unsqueeze(2).to_broadcast([P, TQ * 4, 4]),
                    ALU.mult))
                top_mask(nc, own, masked[:, :, :], n, 4, buf, top, mask[:, :, :])
                factor = 2.5
            own.link(nc.vector.tensor_tensor(picked[:, :, :], scores[:, :, :], mask[:, :, :], ALU.mult))
            own.link(nc.vector.reduce_sum(total[:, :], picked[:, :, :], AX.X))
            own.link(nc.vector.tensor_scalar(total[:, :], total[:, :], 1e-20, None, ALU.add))
            own.link(nc.vector.reciprocal(rtotal[:, :], total[:, :]))
            if factor != 1.0:
                own.link(nc.vector.tensor_scalar(rtotal[:, :], rtotal[:, :], factor, None, ALU.mult))
            own.link(nc.vector.tensor_tensor(cw[:, :, 0:n], picked[:, :, :], wide(rtotal[:, :], n), ALU.mult))
            if cw.shape[2] > n:
                own.link(nc.vector.memset(cw[:, :, n:], 1.0))


def experts(nc, name, ps, x_t, rounds, per_round, chunks, gated, up_dram, down_dram, b1_dram, cw, acc):
    CH = per_round * chunks
    WAYS = 2 if gated else 1
    HALVES = NT // BANK
    UNITS = HALVES * CH
    OUTS = TQ * per_round
    with Stage(nc, name) as s:
        up = s.sb("up", [P, KC, WAYS, CH, P])
        down = s.sb("down", [P, CH, D])
        b1 = s.sb("b1", [P, rounds * CH])
        act_out = s.sb("act_out", [P, 2, BANK])
        h = s.sb("h", [P, CH, NT])
        b1_loaded = s.sem("b1_loaded")
        unit_seen = s.sem("unit_seen")
        up_loaded, up_free = s.sem("up_loaded"), s.sem("up_free")
        down_loaded, down_free = s.sem("down_loaded"), s.sem("down_free")
        upped = s.sem("upped")
        activated = s.sem("activated")
        h_ready = s.sem("h_ready")
        downed = s.sem("downed")
        added = s.sem("added")
        block = s.block()

        @block.sync
        def _(sp):
            if b1_dram is not None:
                sp.dma_start(b1[:, :], b1_dram).then_inc(b1_loaded, 16)
            with sp.Fori(0, rounds) as i:
                sp.wait_ge(up_free, i + 1)
                sp.dma_start(up[:, :, :, :, :].rearrange("p k w c n -> p (k w c n)"),
                             up_dram[bass.ds(i, 1)].rearrange("a p n -> (a p) n")).then_inc(up_loaded, 16)
                sp.wait_ge(down_free, i + 1)
                sp.dma_start(down[:, :, :].rearrange("p c n -> p (c n)"),
                             down_dram[bass.ds(i, 1)].rearrange("a p n -> (a p) n")).then_inc(down_loaded, 16)

        @block.tensor
        def _(pe):
            nc.tensor.sem_inc(up_free, 1)
            nc.tensor.sem_inc(down_free, 1)
            nc.tensor.sem_inc(added, 4)
            nc.tensor.sem_inc(h_ready, 2)
            with pe.Fori(0, rounds) as i:
                pe.wait_ge(up_loaded, 16 * i + 16)
                for u in range(UNITS):
                    half, c = u // CH, u % CH
                    pe.wait_ge(h_ready, UNITS * i + u + 1)
                    for way in range(WAYS):
                        for k in range(KC):
                            ins = nc.tensor.matmul(ps[:, 2 * (u % 2) + way, :], up[:, k, way, c, :],
                                                   x_t[:, k, half * BANK:(half + 1) * BANK],
                                                   start=(k == 0), stop=(k == KC - 1))
                    ins.then_inc(upped, 1)
                pe.wait_ge(upped, UNITS * i + UNITS)
                nc.tensor.sem_inc(up_free, 1)
                pe.wait_ge(down_loaded, 16 * i + 16)
                n = 0
                for half in range(HALVES):
                    pe.wait_ge(h_ready, UNITS * i + (half + 1) * CH + 2)
                    for e in range(per_round):
                        for t in range(half * TQ // HALVES, (half + 1) * TQ // HALVES):
                            pe.wait_ge(added, OUTS * i + n + 1)
                            for c in range(chunks):
                                ins = nc.tensor.matmul(ps[:, 4 + n % 4, 0:D], h[:, e * chunks + c, t * P:(t + 1) * P],
                                                       down[:, e * chunks + c, :], start=(c == 0), stop=(c == chunks - 1))
                            ins.then_inc(downed, 1)
                            n += 1
                pe.wait_ge(downed, OUTS * i + OUTS)
                nc.tensor.sem_inc(down_free, 1)

        @block.scalar
        def _(act):
            if not gated:
                act.wait_ge(b1_loaded, 16)
            with act.Fori(0, rounds) as i:
                for u in range(UNITS):
                    half, c = u // CH, u % CH
                    act.wait_ge(upped, UNITS * i + u + 1)
                    if gated:
                        act.wait_ge(h_ready, UNITS * i + u + 1)
                        nc.scalar.activation(act_out[:, u % 2, :], ps[:, 2 * (u % 2), :], ACT.Silu).then_inc(activated, 1)
                    else:
                        if u % CH == 0:
                            act.wait_ge(added, OUTS * i + 4)
                        nc.scalar.sem_inc(unit_seen, 1)
                        nc.scalar.activation(h[:, c, half * BANK:(half + 1) * BANK], ps[:, 2 * (u % 2), :], ACT.Relu,
                                             bias=b1[:, bass.ds(i * CH + c, 1)]).then_inc(h_ready, 1)

        @block.vector
        def _(dve):
            with dve.Fori(0, rounds) as i:
                if gated:
                    for u in range(UNITS):
                        half, c = u // CH, u % CH
                        dve.wait_ge(activated, UNITS * i + u + 1)
                        nc.vector.tensor_tensor(h[:, c, half * BANK:(half + 1) * BANK], act_out[:, u % 2, :],
                                                ps[:, 2 * (u % 2) + 1, :], ALU.mult).then_inc(h_ready, 1)
                n = 0
                for half in range(HALVES):
                    for e in range(per_round):
                        for t in range(half * TQ // HALVES, (half + 1) * TQ // HALVES):
                            dve.wait_ge(downed, OUTS * i + n + 1)
                            dve.wait_ge(added, OUTS * i + n + 1)
                            nc.vector.scalar_tensor_tensor(acc[:, t, :], ps[:, 4 + n % 4, 0:D],
                                                           cw[:, t, bass.ds(i * per_round + e, 1)], acc[:, t, :],
                                                           op0=ALU.mult, op1=ALU.add).then_inc(added, 1)
                            n += 1
            dve.wait_ge(added, OUTS * rounds + 4)


def affine_rows(nc, name, rows, gain_dram, shift_dram, dst, add):
    with Stage(nc, name) as s:
        gain, shift = s.sb("gain", [P, D]), s.sb("shift", [P, D])
        loaded, steps = s.sem("loaded"), s.sem("steps")
        block = s.block()

        @block.sync
        def _(sp):
            sp.dma_start(gain[:, :], gain_dram.partition_broadcast(P)).then_inc(loaded, 16)
            sp.dma_start(shift[:, :], shift_dram.partition_broadcast(P)).then_inc(loaded, 16)

        @block.vector
        def _(dve):
            own = Chain(dve, steps)
            dve.wait_ge(loaded, 32)
            g = gain[:, :].unsqueeze(1).to_broadcast([P, TQ, D])
            b = shift[:, :].unsqueeze(1).to_broadcast([P, TQ, D])
            own.link(nc.vector.tensor_tensor(rows[:, :, :], rows[:, :, :], g, ALU.mult))
            if add:
                own.link(nc.vector.tensor_tensor(dst[:, :, :], dst[:, :, :], b, ALU.add))
                own.link(nc.vector.tensor_tensor(dst[:, :, :], dst[:, :, :], rows[:, :, :], ALU.add))
            else:
                own.link(nc.vector.tensor_tensor(dst[:, :, :], rows[:, :, :], b, ALU.add))


def expert_biases(nc, name, ps, ident, cw, n, b2_dram, acc):
    with Stage(nc, name) as s:
        b2 = s.sb("b2", [n, D])
        cw_t = s.sb("cw_t", [n, NT])
        loaded, turned, copied = s.sem("loaded"), s.sem("turned"), s.sem("copied")
        made, added = s.sem("made"), s.sem("added")
        block = s.block()

        @block.sync
        def _(sp):
            sp.dma_start(b2[:, :], b2_dram).then_inc(loaded, 16)

        @block.tensor
        def _(pe):
            for t in range(TQ):
                ins = nc.tensor.transpose(ps[0:n, t // 4, (t % 4) * P:(t % 4 + 1) * P], cw[:, t, :], ident[:, :])
            ins.then_inc(turned, 1)
            pe.wait_ge(copied, 1)
            pe.wait_ge(loaded, 16)
            for t in range(TQ):
                if t >= 4:
                    pe.wait_ge(added, t - 3)
                nc.tensor.matmul(ps[:, 4 + t % 4, 0:D], cw_t[:, t * P:(t + 1) * P], b2[:, :], start=True, stop=True
                                 ).then_inc(made, 1)

        @block.scalar
        def _(act):
            act.wait_ge(turned, 1)
            nc.scalar.activation(cw_t[:, :], ps[0:n, 0:2, :].rearrange("p a n -> p (a n)"), ACT.Copy
                                 ).then_inc(copied, 1)

        @block.vector
        def _(dve):
            for t in range(TQ):
                dve.wait_ge(made, t + 1)
                nc.vector.tensor_tensor(acc[:, t, :], acc[:, t, :], ps[:, 4 + t % 4, 0:D], ALU.add).then_inc(added, 1)
            dve.wait_ge(added, TQ)


def bit_conv_ffn(nc, name, ps, ident, ones, x, w1_dram, w2_dram, cw_dram, cb_dram):
    CH = 1024 // P
    LO = NQ + 2
    with Stage(nc, name) as s:
        w1 = s.sb("w1", [P, KC, 1024])
        w2 = s.sb("w2", [P, CH, D])
        w1q, w2q = s.sb("w1q", [P, KC, 1024], BF16), s.sb("w2q", [P, CH, D], BF16)
        wabs = s.sb("wabs", [P, 2048])
        wsum = s.sb("wsum", [P, 2])
        wscale, winv = s.sb("wscale", [P, 2]), s.sb("winv", [P, 2])
        rows = s.sb("rows", [P, TQ, D])
        stats, mv = s.sb("stats", [P, TQ, 6]), s.sb("mv", [P, TQ, 2])
        var_eps, dev, rstd = s.sb("var_eps", [P, TQ]), s.sb("dev", [P, TQ]), s.sb("rstd", [P, TQ])
        big, scale, inv = s.sb("big", [P, TQ]), s.sb("scale", [P, TQ]), s.sb("inv", [P, TQ])
        diag = s.sb("diag", [P, TQ, P])
        by_token = s.sb("by_token", [P, NT])
        xq_t = s.sb("xq_t", [P, KC, NT], BF16)
        hid = s.sb("hid", [P, 2, B, LO])
        conv = s.sb("conv", [P, 2, B, NQ])
        act_t = s.sb("act_t", [P, CH, NT])
        hq = s.sb("hq", [P, CH, NT], BF16)
        tmp = s.sb("tmp", [P, 2, NT])
        big4 = s.sb("big4", [P, TQ, 2])
        taps = s.sb("taps", [P, CH, 3])
        cb = s.sb("cb", [P, CH])
        out_scale = s.sb("out_scale", [P, TQ])
        loaded, steps = s.sem("loaded"), s.sem("steps")
        w_summed = s.sem("w_summed")
        w_totalled = s.sem("w_totalled")
        var_ready, dev_ready = s.sem("var_ready"), s.sem("dev_ready")
        rows_ready = s.sem("rows_ready")
        turned, copied, w1_ready = s.sem("turned"), s.sem("copied"), s.sem("w1_ready")
        diag_ready, spread, spread_copied = s.sem("diag_ready"), s.sem("spread"), s.sem("spread_copied")
        upped, conved, activated = s.sem("upped"), s.sem("conved"), s.sem("activated")
        hid_used = s.sem("hid_used")
        act_turned, maxed = s.sem("act_turned"), s.sem("maxed")
        hq_ready, downed, added = s.sem("hq_ready"), s.sem("downed"), s.sem("added")
        block = s.block()

        @block.sync
        def _(sp):
            sp.dma_start(w1[:, :, :], w1_dram).then_inc(loaded, 16)
            sp.dma_start(w2[:, :, :], w2_dram).then_inc(loaded, 16)
            sp.dma_start(taps[:, :, :], cw_dram).then_inc(loaded, 16)
            sp.dma_start(cb[:, :], cb_dram).then_inc(loaded, 16)

        @block.scalar
        def _(act):
            act.wait_ge(loaded, 64)
            nc.scalar.activation(wabs[:, :], w1[:, :, :].rearrange("p k n -> p (k n)"), ACT.Abs,
                                 accum_out=wsum[:, 0:1]).then_inc(w_summed, 1)
            act.wait_ge(w_summed, 1)
            nc.scalar.activation(wabs[:, :], w2[:, :, :].rearrange("p k n -> p (k n)"), ACT.Abs,
                                 accum_out=wsum[:, 1:2]).then_inc(w_summed, 1)
            act.wait_ge(var_ready, 1)
            nc.scalar.activation(dev[:, :], var_eps[:, :], ACT.Sqrt).then_inc(dev_ready, 1)
            for n in range(4):
                act.wait_ge(turned, n + 1)
                nc.scalar.activation(xq_t[:, n // 2, (n % 2) * BANK:(n % 2 + 1) * BANK], ps[:, n, :], ACT.Copy
                                     ).then_inc(copied, 1)
            for n in range(2):
                act.wait_ge(spread, 1)
                nc.scalar.activation(by_token[:, n * BANK:(n + 1) * BANK], ps[:, 4 + n, :], ACT.Copy
                                     ).then_inc(spread_copied, 1)
            for c in range(CH):
                act.wait_ge(conved, c + 1)
                nc.scalar.activation(act_t[:, c, :], conv[:, c % 2, :, :].rearrange("p b n -> p (b n)"), ACT.Silu,
                                     bias=cb[:, c:c + 1]).then_inc(activated, 1)
            for n in range(2):
                act.wait_ge(spread, 2)
                nc.scalar.activation(by_token[:, n * BANK:(n + 1) * BANK], ps[:, 4 + n, :], ACT.Copy
                                     ).then_inc(spread_copied, 1)

        @block.tensor
        def _(pe):
            pe.wait_ge(w_summed, 2)
            nc.tensor.matmul(ps[:, 7, 0:2], ones[:, :], wsum[:, :], start=True, stop=True).then_inc(w_totalled, 1)
            pe.wait_ge(rows_ready, 1)
            for k in range(KC):
                for t in range(TQ):
                    ins = nc.tensor.transpose(ps[:, 2 * k + t // 4, (t % 4) * P:(t % 4 + 1) * P],
                                              rows[:, t, k * P:(k + 1) * P], ident[:, :])
                    if t % 4 == 3:
                        ins.then_inc(turned, 1)
            pe.wait_ge(diag_ready, 1)
            for t in range(TQ):
                ins = nc.tensor.matmul(ps[:, 4 + t // 4, (t % 4) * P:(t % 4 + 1) * P], ones[:, :], diag[:, t, :],
                                       start=True, stop=True)
            ins.then_inc(spread, 1)
            pe.wait_ge(copied, 4)
            pe.wait_ge(w1_ready, 1)
            for c in range(CH):
                if c >= 2:
                    pe.wait_ge(hid_used, 2 * (c - 1))
                for b in range(B):
                    for k in range(KC):
                        ins = nc.tensor.matmul(ps[:, 2 * (c % 2) + b, :], w1q[:, k, c * P:(c + 1) * P],
                                               xq_t[:, k, b * NQ:(b + 1) * NQ], start=(k == 0), stop=(k == KC - 1))
                ins.then_inc(upped, 1)
            pe.wait_ge(activated, CH)
            for t in range(TQ):
                if t >= 2:
                    pe.wait_ge(maxed, t - 1)
                for c in range(CH):
                    ins = nc.tensor.transpose(ps[:, 2 * (t % 2) + c // 4, (c % 4) * P:(c % 4 + 1) * P],
                                              act_t[:, c, t * P:(t + 1) * P], ident[:, :])
                ins.then_inc(act_turned, 1)
            pe.wait_ge(diag_ready, 2)
            for t in range(TQ):
                ins = nc.tensor.matmul(ps[:, 4 + t // 4, (t % 4) * P:(t % 4 + 1) * P], ones[:, :], diag[:, t, :],
                                       start=True, stop=True)
            ins.then_inc(spread, 1)
            pe.wait_ge(hq_ready, CH)
            for t in range(TQ):
                if t >= 4:
                    pe.wait_ge(added, t - 3)
                for c in range(CH):
                    ins = nc.tensor.matmul(ps[:, t % 4, 0:D], hq[:, c, t * P:(t + 1) * P], w2q[:, c, :],
                                           start=(c == 0), stop=(c == CH - 1))
                ins.then_inc(downed, 1)

        @block.vector
        def _(dve):
            own = Chain(dve, steps)
            own.link(nc.vector.memset(hid[:, :, :, :], 0.0))
            for t in range(TQ):
                own.done(nc.vector.bn_stats(stats[:, t, :], x[:, t, :]))
            own.wait()
            for t in range(TQ):
                own.done(nc.vector.bn_aggr(mv[:, t, :], stats[:, t, :]))
            own.wait()
            own.link(nc.vector.tensor_scalar(var_eps[:, :], mv[:, :, 1], 1e-5, None, ALU.add))
            nc.vector.sem_inc(var_ready, 1)
            dve.wait_ge(dev_ready, 1)
            own.link(nc.vector.reciprocal(rstd[:, :], dev[:, :]))
            for t in range(TQ):
                own.done(nc.vector.tensor_scalar(rows[:, t, :], x[:, t, :], mv[:, t, 0:1], rstd[:, t:t + 1],
                                                 ALU.subtract, ALU.mult))
            own.wait()

            def scales():
                own.link(nc.vector.tensor_scalar(big[:, :], big[:, :], 1e-5, None, ALU.max))
                own.link(nc.vector.reciprocal(scale[:, :], big[:, :]))
                own.link(nc.vector.tensor_scalar(scale[:, :], scale[:, :], 127.0, None, ALU.mult))
                own.link(nc.vector.reciprocal(inv[:, :], scale[:, :]))

            own.link(nc.vector.tensor_reduce(big[:, :], rows[:, :, :], AX.X, ALU.max, apply_absolute_value=True))
            scales()
            for t in range(TQ):
                own.done(nc.vector.tensor_scalar(rows[:, t, :], rows[:, t, :], scale[:, t:t + 1], None, ALU.mult))
            own.wait()
            allr = rows[:, :, :].rearrange("p t n -> p (t n)")
            own.link(nc.vector.tensor_scalar(allr, allr, ROUND, -ROUND, ALU.add, ALU.add))
            own.link(nc.vector.tensor_scalar(allr, allr, 127.0, -128.0, ALU.min, ALU.max))
            nc.vector.sem_inc(rows_ready, 1)
            dve.wait_ge(w_totalled, 1)
            own.link(nc.vector.tensor_scalar(winv[:, :], ps[:, 7, 0:2], 1.0 / (1024 * D), 1e-5, ALU.mult, ALU.max))
            own.link(nc.vector.reciprocal(wscale[:, :], winv[:, :]))
            own.link(nc.vector.reciprocal(winv[:, :], wscale[:, :]))
            for t in range(TQ):
                own.done(nc.vector.tensor_scalar(diag[:, t, :], ident[:, :], inv[:, t:t + 1], winv[:, 0:1], ALU.mult,
                                                 ALU.mult))
            own.wait()
            nc.vector.sem_inc(diag_ready, 1)
            for n, (w, wq) in enumerate(((w1[:, :, :].rearrange("p k n -> p (k n)"), w1q[:, :, :].rearrange("p k n -> p (k n)")),
                                         (w2[:, :, :].rearrange("p k n -> p (k n)"), w2q[:, :, :].rearrange("p k n -> p (k n)")))):
                own.link(nc.vector.tensor_scalar(w, w, wscale[:, n:n + 1], None, ALU.mult))
                own.link(nc.vector.tensor_scalar(w, w, ROUND, -ROUND, ALU.add, ALU.add))
                own.link(nc.vector.tensor_scalar(wq, w, 1.0, -1.0, ALU.min, ALU.max))
                if n == 0:
                    nc.vector.sem_inc(w1_ready, 1)
            dve.wait_ge(spread_copied, 2)
            for c in range(CH):
                dve.wait_ge(upped, c + 1)
                for b in range(B):
                    own.done(nc.vector.tensor_tensor(hid[:, c % 2, b, 1:1 + NQ], by_token[:, b * NQ:(b + 1) * NQ],
                                                     ps[:, 2 * (c % 2) + b, :], ALU.mult))
                own.wait()
                nc.vector.sem_inc(hid_used, 2)
                if c >= 2:
                    dve.wait_ge(activated, c - 1)
                y, v = conv[:, c % 2, :, :], hid[:, c % 2, :, :]
                own.link(nc.vector.tensor_scalar(y, v[:, :, 0:NQ], taps[:, c, 0:1], None, ALU.mult))
                own.link(nc.vector.scalar_tensor_tensor(y, v[:, :, 1:NQ + 1], taps[:, c, 1:2], y, ALU.mult, ALU.add))
                own.link(nc.vector.scalar_tensor_tensor(y, v[:, :, 2:NQ + 2], taps[:, c, 2:3], y, ALU.mult, ALU.add))
                nc.vector.sem_inc(conved, 1)
            for t in range(TQ):
                dve.wait_ge(act_turned, t + 1)
                own.link(nc.vector.tensor_reduce(big[:, t:t + 1], ps[:, 2 * (t % 2):2 * (t % 2) + 2, :].rearrange("p a n -> p (a n)"),
                                                 AX.X, ALU.max, apply_absolute_value=True))
                nc.vector.sem_inc(maxed, 1)
            scales()
            own.link(nc.vector.tensor_scalar(out_scale[:, :], inv[:, :], winv[:, 1:2], None, ALU.mult))
            for t in range(TQ):
                own.done(nc.vector.tensor_scalar(diag[:, t, :], ident[:, :], scale[:, t:t + 1], None, ALU.mult))
            own.wait()
            nc.vector.sem_inc(diag_ready, 1)
            dve.wait_ge(spread_copied, 4)
            for c in range(CH):
                y = tmp[:, c % 2, :]
                own.link(nc.vector.tensor_tensor(y, act_t[:, c, :], by_token[:, :], ALU.mult))
                own.link(nc.vector.tensor_scalar(y, y, ROUND, -ROUND, ALU.add, ALU.add))
                nc.vector.tensor_scalar(hq[:, c, :], y, 127.0, -128.0, ALU.min, ALU.max).then_inc(hq_ready, 1)
            for t in range(TQ):
                dve.wait_ge(downed, t + 1)
                nc.vector.scalar_tensor_tensor(x[:, t, :], ps[:, t % 4, 0:D], out_scale[:, t:t + 1], x[:, t, :],
                                               ALU.mult, ALU.add).then_inc(added, 1)
            dve.wait_ge(added, TQ)


def slot_gru(nc, name, ps, ident, ones, slots, p_t, w, x):
    ITERS = 3
    EPS = 1e-6
    SCALE = D ** -0.5
    NC_ = NK // P
    with Stage(nc, name) as s:
        wk, wv = s.sb("wk", [P, KC, D]), s.sb("wv", [P, KC, D])
        wq = s.sb("wq", [P, KC, D])
        wih, whh = s.sb("wih", [P, KC, 3 * D]), s.sb("whh", [P, KC, 3 * D])
        bih, bhh = s.sb("bih", [P, 6]), s.sb("bhh", [P, 6])
        brz = s.sb("brz", [P, 4])
        norm_w = s.sb("norm_w", [P, KC])
        k_t = s.sb("k_t", [P, KC, B * NK])
        v = s.sb("v", [P, TK, D])
        sq = s.sb("sq", [P, KC, NT])
        sn = s.sb("sn", [P, KC, NT])
        q_t = s.sb("q_t", [P, KC, NT])
        rs = s.sb("rs", [P, NT])
        dev = s.sb("dev", [P, NT])
        top = s.sb("top", [P, 4])
        esum, resum = s.sb("esum", [P, 4]), s.sb("resum", [P, 4])
        probs = s.sb("probs", [P, 2, NQ])
        attn = s.sb("attn", [P, 2, NQ])
        rden = s.sb("rden", [P, NQ])
        upd = s.sb("upd", [P, KC, NT])
        r_t, z_t, n_t = (s.sb(c, [P, KC, NT]) for c in ("r_t", "z_t", "n_t"))
        loaded = s.sem("loaded")
        kv_made, kv_copied = s.sem("kv_made"), s.sem("kv_copied")
        steps = s.sem("steps")
        sq_ready, sq_summed = s.sem("sq_ready"), s.sem("sq_summed")
        mean_ready, dev_ready = s.sem("mean_ready"), s.sem("dev_ready")
        sn_ready, q_made, q_ready = s.sem("sn_ready"), s.sem("q_made"), s.sem("q_ready")
        scored, top_ready, exp_done = s.sem("scored"), s.sem("top_ready"), s.sem("exp_done")
        attn_ready, attn_used = s.sem("attn_ready"), s.sem("attn_used")
        upd_ready = s.sem("upd_ready")
        gates_made, gates_done = s.sem("gates_made"), s.sem("gates_done")
        hn_ready, n_ready = s.sem("hn_ready"), s.sem("n_ready")
        slots_ready = s.sem("slots_ready")
        turned = s.sem("turned")
        block = s.block()
        HG = NT // BANK * KC

        @block.sync
        def _(sp):
            for dst, src in ((wk, w["wk"]), (wv, w["wv"]), (wq, w["wq"]), (wih, w["wih"]), (whh, w["whh"])):
                sp.dma_start(dst[:, :, :], src).then_inc(loaded, 16)
            for dst, src in ((bih, w["bih"]), (bhh, w["bhh"]), (norm_w, w["norm"])):
                sp.dma_start(dst[:, :], src).then_inc(loaded, 16)

        @block.tensor
        def _(pe):
            pe.wait_ge(loaded, 8 * 16)
            unit = 0
            for m in range(KC):
                for n in range(B * NK // BANK):
                    if unit >= 4:
                        pe.wait_ge(kv_copied, unit - 3)
                    for c in range(KC):
                        ins = nc.tensor.matmul(ps[:, unit % 4, :], wk[:, c, m * P:(m + 1) * P],
                                               p_t[:, c, n * BANK:(n + 1) * BANK], start=(c == 0), stop=(c == KC - 1))
                    ins.then_inc(kv_made, 1)
                    unit += 1
            for t2 in range(TK // 2):
                pe.wait_ge(kv_copied, unit - 3)
                for j in range(2):
                    t = 2 * t2 + j
                    for c in range(KC):
                        ins = nc.tensor.matmul(ps[:, unit % 4, j * D:(j + 1) * D], p_t[:, c, t * P:(t + 1) * P],
                                               wv[:, c, :], start=(c == 0), stop=(c == KC - 1))
                ins.then_inc(kv_made, 1)
                unit += 1
            pe.wait_ge(kv_copied, unit)
            with pe.Fori(0, ITERS) as i:
                pe.wait_ge(sq_ready, i + 1)
                for n in range(2):
                    for c in range(KC):
                        ins = nc.tensor.matmul(ps[:, n, :], ones[:, :], sq[:, c, n * BANK:(n + 1) * BANK],
                                               start=(c == 0), stop=(c == KC - 1))
                ins.then_inc(sq_summed, 1)
                pe.wait_ge(sn_ready, i + 1)
                for m in range(KC):
                    for n in range(2):
                        for c in range(KC):
                            ins = nc.tensor.matmul(ps[:, 2 + 2 * m + n, :], wq[:, c, m * P:(m + 1) * P],
                                                   sn[:, c, n * BANK:(n + 1) * BANK], start=(c == 0), stop=(c == KC - 1))
                ins.then_inc(q_made, 1)
                pe.wait_ge(q_ready, i + 1)
                for b in range(B):
                    def update(t):
                        n = i * (B * NC_) + (b * NC_ + t)
                        pe.wait_ge(attn_ready, n + 1)
                        for m in range(KC):
                            nc.tensor.matmul(ps[:, 2 + m, :], v[:, b * NC_ + t, m * P:(m + 1) * P], attn[:, t % 2, :],
                                             start=(t == 0), stop=(t == NC_ - 1))
                        nc.tensor.matmul(ps[:, 4, :], ones[:, :], attn[:, t % 2, :], start=(t == 0),
                                         stop=(t == NC_ - 1)).then_inc(attn_used, 1)

                    if b:
                        pe.wait_ge(upd_ready, i * B + b)
                    for t in range(NC_):
                        n = i * (B * NC_) + (b * NC_ + t)
                        if b * NC_ + t >= 2:
                            pe.wait_ge(exp_done, n - 1)
                        for c in range(KC):
                            ins = nc.tensor.matmul(ps[:, t % 2, :], k_t[:, c, b * NK + t * P:b * NK + (t + 1) * P],
                                                   q_t[:, c, b * NQ:(b + 1) * NQ], start=(c == 0), stop=(c == KC - 1))
                        ins.then_inc(scored, 1)
                        if t >= 1:
                            update(t - 1)
                    update(NC_ - 1)
                pe.wait_ge(upd_ready, i * B + B)
                for u in range(HG):
                    n, m = u // KC, u % KC
                    if u >= 2:
                        pe.wait_ge(hn_ready, i * HG + u - 1)
                    tok = slice(n * BANK, (n + 1) * BANK)
                    for gate in range(3):
                        for c in range(KC):
                            nc.tensor.matmul(ps[:, 4 * (u % 2) + gate, :],
                                             wih[:, c, gate * D + m * P:gate * D + (m + 1) * P], upd[:, c, tok],
                                             start=(c == 0), stop=(gate == 2 and c == KC - 1))
                        for c in range(KC):
                            last = nc.tensor.matmul(ps[:, 4 * (u % 2) + (3 if gate == 2 else gate), :],
                                                    whh[:, c, gate * D + m * P:gate * D + (m + 1) * P], slots[:, c, tok],
                                                    start=(gate == 2 and c == 0), stop=(c == KC - 1))
                    last.then_inc(gates_made, 1)
            pe.wait_ge(slots_ready, ITERS * 1 + 1)
            for t in range(TQ):
                for c in range(KC):
                    ins = nc.tensor.transpose(ps[:, t // 2, (t % 2) * D + c * P:(t % 2) * D + (c + 1) * P],
                                              slots[:, c, t * P:(t + 1) * P], ident[:, :])
            ins.then_inc(turned, 1)

        @block.scalar
        def _(act):
            unit = 0
            for m in range(KC):
                for n in range(B * NK // BANK):
                    act.wait_ge(kv_made, unit + 1)
                    nc.scalar.activation(k_t[:, m, n * BANK:(n + 1) * BANK], ps[:, unit % 4, :], ACT.Copy
                                         ).then_inc(kv_copied, 1)
                    unit += 1
            for t2 in range(TK // 2):
                act.wait_ge(kv_made, unit + 1)
                nc.scalar.activation(v[:, 2 * t2:2 * t2 + 2, :].rearrange("p a n -> p (a n)"), ps[:, unit % 4, :],
                                     ACT.Copy).then_inc(kv_copied, 1)
                unit += 1
            with act.Fori(0, ITERS) as i:
                act.wait_ge(mean_ready, i + 1)
                nc.scalar.activation(dev[:, :], rs[:, :], ACT.Sqrt).then_inc(dev_ready, 1)
                act.wait_ge(q_made, i + 1)
                for m in range(KC):
                    ins = nc.scalar.activation(q_t[:, m, :], ps[:, 2 + 2 * m:4 + 2 * m, :].rearrange("p a n -> p (a n)"),
                                               ACT.Copy)
                ins.then_inc(q_ready, 1)
                for b in range(B):
                    for t in range(NC_):
                        n = i * (B * NC_) + (b * NC_ + t)
                        act.wait_ge(top_ready, n + 1)
                        nc.scalar.activation(probs[:, t % 2, :], ps[:, t % 2, :], ACT.Exp, bias=top[:, t % 2:t % 2 + 1],
                                             scale=SCALE, accum_out=esum[:, t % 2:t % 2 + 1]).then_inc(exp_done, 1)
                for u in range(HG):
                    n, m = u // KC, u % KC
                    tok = slice(n * BANK, (n + 1) * BANK)
                    act.wait_ge(gates_made, i * HG + u + 1)
                    nc.scalar.activation(r_t[:, m, tok], ps[:, 4 * (u % 2), :], ACT.Sigmoid, bias=brz[:, m:m + 1])
                    nc.scalar.activation(z_t[:, m, tok], ps[:, 4 * (u % 2) + 1, :], ACT.Sigmoid,
                                         bias=brz[:, 2 + m:3 + m]).then_inc(gates_done, 1)
                    act.wait_ge(hn_ready, i * HG + u + 1)
                    nc.scalar.activation(n_t[:, m, tok], n_t[:, m, tok], ACT.Tanh, bias=bih[:, 4 + m:5 + m]
                                         ).then_inc(n_ready, 1)

        PER_ITER = 2 + 6 + 2 + 3 * B * NC_ + B * 4 + HG + HG * 3

        @block.vector
        def _(dve):
            dve.wait_ge(loaded, 8 * 16)
            nc.vector.tensor_tensor(brz[:, :], bih[:, 0:4], bhh[:, 0:4], ALU.add).then_inc(slots_ready, 1)
            with dve.Fori(0, ITERS) as i:
                own = Chain(dve, steps, i * PER_ITER)
                dve.wait_ge(slots_ready, i + 1)
                for c in range(KC):
                    own.done(nc.vector.tensor_tensor(sq[:, c, :], slots[:, c, :], slots[:, c, :], ALU.mult))
                own.wait()
                nc.vector.sem_inc(sq_ready, 1)
                dve.wait_ge(sq_summed, i + 1)
                own.link(nc.vector.tensor_scalar(rs[:, :], ps[:, 0:2, :].rearrange("p a n -> p (a n)"), 1.0 / D, EPS,
                                                 ALU.mult, ALU.add))
                nc.vector.sem_inc(mean_ready, 1)
                dve.wait_ge(dev_ready, i + 1)
                own.link(nc.vector.reciprocal(rs[:, :], dev[:, :]))
                for c in range(KC):
                    own.done(nc.vector.tensor_tensor(sn[:, c, :], slots[:, c, :], rs[:, :], ALU.mult))
                own.wait()
                for c in range(KC):
                    own.done(nc.vector.tensor_scalar(sn[:, c, :], sn[:, c, :], norm_w[:, c:c + 1], None, ALU.mult))
                own.wait()
                nc.vector.sem_inc(sn_ready, 1)
                own.n += 2
                nc.vector.sem_inc(steps, 2)
                own.wait()
                for b in range(B):
                    for t in range(NC_):
                        n = i * (B * NC_) + (b * NC_ + t)
                        j = t % 2
                        dve.wait_ge(scored, n + 1)
                        own.link(nc.vector.reduce_max(top[:, 2 + j:3 + j], ps[:, j, :], AX.X))
                        own.link(nc.vector.tensor_scalar(top[:, j:j + 1], top[:, 2 + j:3 + j], -SCALE, None, ALU.mult))
                        nc.vector.sem_inc(top_ready, 1)
                        dve.wait_ge(exp_done, n + 1)
                        own.link(nc.vector.reciprocal(resum[:, j:j + 1], esum[:, j:j + 1]))
                        if b * NC_ + t >= 2:
                            dve.wait_ge(attn_used, n - 1)
                        nc.vector.tensor_scalar(attn[:, j, :], probs[:, j, :], resum[:, j:j + 1], None, ALU.mult
                                                ).then_inc(attn_ready, 1)
                    dve.wait_ge(attn_used, i * (B * NC_) + (b + 1) * NC_)
                    own.link(nc.vector.tensor_scalar(rden[:, :], ps[:, 4, :], EPS, None, ALU.add))
                    own.link(nc.vector.reciprocal(rden[:, :], rden[:, :]))
                    for m in range(KC):
                        own.done(nc.vector.tensor_tensor(upd[:, m, b * NQ:(b + 1) * NQ], rden[:, :], ps[:, 2 + m, :],
                                                         ALU.mult))
                    own.wait()
                    nc.vector.sem_inc(upd_ready, 1)
                for u in range(HG):
                    n, m = u // KC, u % KC
                    tok = slice(n * BANK, (n + 1) * BANK)
                    dve.wait_ge(gates_done, i * HG + u + 1)
                    own.link(nc.vector.scalar_tensor_tensor(n_t[:, m, tok], ps[:, 4 * (u % 2) + 3, :], bhh[:, 4 + m:5 + m],
                                                            r_t[:, m, tok], ALU.add, ALU.mult))
                    nc.vector.tensor_tensor(n_t[:, m, tok], n_t[:, m, tok], ps[:, 4 * (u % 2) + 2, :], ALU.add
                                            ).then_inc(hn_ready, 1)
                for u in range(HG):
                    n, m = u // KC, u % KC
                    tok = slice(n * BANK, (n + 1) * BANK)
                    dve.wait_ge(n_ready, i * HG + u + 1)
                    own.link(nc.vector.tensor_tensor(slots[:, m, tok], slots[:, m, tok], n_t[:, m, tok], ALU.subtract))
                    own.link(nc.vector.tensor_tensor(slots[:, m, tok], slots[:, m, tok], z_t[:, m, tok], ALU.mult))
                    own.link(nc.vector.tensor_tensor(slots[:, m, tok], slots[:, m, tok], n_t[:, m, tok], ALU.add))
                nc.vector.sem_inc(slots_ready, 1)
                assert own.n == PER_ITER, (own.n, PER_ITER)
            dve.wait_ge(turned, 1)
            for t4 in range(4):
                ins = nc.vector.tensor_tensor(x[:, 2 * t4:2 * t4 + 2, :].rearrange("p a n -> p (a n)"),
                                              x[:, 2 * t4:2 * t4 + 2, :].rearrange("p a n -> p (a n)"), ps[:, t4, :],
                                              ALU.add)
                ins.then_inc(turned, 1)
            dve.wait_ge(turned, 5)


def build(nc, A, out, stages=range(8)):
    Stage.spent = []
    with ExitStack() as top:
        ps = top.enter_context(nc.psum_tensor("ps", [P, 8, BANK], F32))

        def sb(name, shape, dt=F32, stack=top):
            return stack.enter_context(nc.sbuf_tensor(name, shape, dt))

        ident, ones, slot_sum = sb("ident", [P, P]), sb("ones", [P, P]), sb("slot_sum", [P, P])
        x = sb("x_rows", [P, TQ, D])
        ctx_rows_dram = A["ctx_1024"].rearrange("b (t p) d -> p (b t) d", p=P)

        def by_feature(name):
            return A[name + "_f"]

        constants(nc, ident, ones, slot_sum)
        load_x(nc, A["x"], x)
        def slots(tag, kv_t, nk, sparse, wo_dram, bo_dram, acc, keep=None):
            q_parts = nc.dram_tensor(tag + "_q_parts", (2, 8, 16, 4, NQ), F32).ap()
            k_parts = nc.dram_tensor(tag + "_k_parts", (8, 16, 2, 4, nk), F32).ap()
            v_groups = nc.dram_tensor(tag + "_v_groups", (8, P, nk), F32).ap()
            with ExitStack() as st:
                x_t = sb(tag + "_x_t", [P, KC, NT], stack=st)
                normalize(nc, tag + "ln", ps, ident, x, TQ, x_t, 1e-5, keep=keep)
                project_heads(nc, tag + "p", ps, x_t, x_t if kv_t is None else kv_t, nk, A[tag + "_w"], A[tag + "_b"],
                              q_parts, k_parts, v_groups)
            with ExitStack() as st:
                o_all = sb(tag + "_o_all", [P, 8, NQ], stack=st)
                head_attention(nc, tag + "a", ps, ident, slot_sum, nk, q_parts, k_parts, v_groups, A[tag + "_bv"],
                               o_all, sparse)
                project_out(nc, tag + "o", ps, o_all, 4, wo_dram, bo_dram, acc, by_batch=True)

        if 0 in stages:
            with ExitStack() as l0:
                q_t = sb("l0_q_t", [P, KC, NT], stack=l0)
                c_t = sb("l0_c_t", [P, KC, B * NK], stack=l0)
                with ExitStack() as t:
                    c = sb("l0_c_rows", [P, TK, D], stack=t)
                    normalize(nc, "l0lnc", ps, ident, c, TK, c_t, 1e-5, gain_dram=by_feature("L0_xattn_ln_ctx_g"),
                              shift_dram=by_feature("L0_xattn_ln_ctx_b"), src_dram=ctx_rows_dram)
                    normalize(nc, "l0lnx", ps, ident, x, TQ, q_t, 1e-5, norms=2,
                              gain_dram=by_feature("L0_xattn_ln_lat_g"), shift_dram=by_feature("L0_xattn_ln_lat_b"))
                o_all = sb("l0_o_all", [P, 8, NT], stack=l0)
                rope_attention(nc, "l0a", ps, ones, q_t, c_t, A["l0_w"], A["l0_cos"], A["l0_sin"], o_all)
                project_out(nc, "l0o", ps, o_all, 8, A["l0_wo"], A["L0_xattn_bo"], x)
        if 1 in stages:
            bit_conv_ffn(nc, "f0", ps, ident, ones, x, A["f0_w1"], A["f0_w2"], A["f0_taps"], A["f0_cb"])
        if 2 in stages or 6 in stages:
            ctx_t = sb("ctx_t", [P, KC, B * NK])
            with ExitStack() as t:
                c = sb("c_rows", [P, TK, D], stack=t)
                transpose_rows(nc, "ctxt", ps, ident, c, TK, ctx_t, ctx_rows_dram)
        if 2 in stages:
            slots("l1", ctx_t, NK, True, A["l1_wo"], A["L1_xattn_bo"], x)
        clear_semaphores(nc)
        if 3 in stages:
            with ExitStack() as st:
                x_t = sb("m1_x_t", [P, KC, NT], stack=st)
                cw = sb("m1_cw", [P, TQ, 9], stack=st)
                normalize(nc, "m1ln", ps, ident, x, TQ, x_t, 1e-5)
                route(nc, "m1r", ps, x_t, 9, A["m1_router"], A["m1_bias"], "top2", cw)
                experts(nc, "m1e", ps, x_t, 9, 1, 6, True, A["m1_up"], A["m1_down"], None, cw, x)
        if 4 in stages:
            with ExitStack() as st:
                slots_t = sb("g2_slots", [P, KC, NT], stack=st)
                p_t = sb("g2_p_t", [P, KC, B * NK], stack=st)
                with ExitStack() as t:
                    c = sb("g2_c_rows", [P, TK, D], stack=t)
                    normalize(nc, "g2lnc", ps, ident, c, TK, p_t, 1e-6, rms=True,
                              gain_dram=by_feature("L2_xattn_input_norm_w"), src_dram=ctx_rows_dram)
                    normalize(nc, "g2lnx", ps, ident, x, TQ, slots_t, 1e-5)
                slot_gru(nc, "g2", ps, ident, ones, slots_t, p_t,
                         {k: A["g2_" + k] for k in ("wk", "wv", "wq", "wih", "whh", "bih", "bhh", "norm")}, x)
        clear_semaphores(nc)
        if 5 in stages:
            with ExitStack() as st:
                src = sb("m2_src", [P, TQ, D], stack=st)
                x1 = sb("m2_x1", [P, TQ, D], stack=st)
                x_t = sb("m2_x1_t", [P, KC, NT], stack=st)
                cw = sb("m2_cw", [P, TQ, 8], stack=st)
                slots("m2", None, NQ, False, A["m2_wo"], A["L2_ffn_bo"], src, keep=src)
                normalize(nc, "m2ln1", ps, ident, src, TQ, x_t, 1e-5, keep=x1,
                          gain_dram=by_feature("L2_ffn_ln1_g"), shift_dram=by_feature("L2_ffn_ln1_b"))
                affine_rows(nc, "m2af1", x1, A["L2_ffn_ln1_g"], A["L2_ffn_ln1_b"], src, False)
                route(nc, "m2r", ps, x_t, 8, A["m2_router"], A["L2_ffn_gb"], "softmax", cw)
                experts(nc, "m2e", ps, x_t, 8, 1, 4, False, A["m2_up"], A["m2_down"], A["m2_b1"], cw, src)
                expert_biases(nc, "m2eb", ps, ident, cw, 8, A["L2_ffn_b2"], src)
                normalize(nc, "m2ln2", ps, ident, src, TQ, x_t, 1e-5, keep=x1)
                affine_rows(nc, "m2af2", x1, A["L2_ffn_ln2_g"], A["L2_ffn_ln2_b"], x, True)
        clear_semaphores(nc)
        if 6 in stages:
            slots("l3", ctx_t, NK, False, A["l3_wo"], None, x)
        if 7 in stages:
            with ExitStack() as st:
                x_t = sb("m3_x_t", [P, KC, NT], stack=st)
                cw = sb("m3_cw", [P, TQ, 18], stack=st)
                normalize(nc, "m3ln", ps, ident, x, TQ, x_t, 1e-5)
                route(nc, "m3r", ps, x_t, 16, A["m3_router"], A["m3_bias"], "grouped", cw)
                experts(nc, "m3e", ps, x_t, 6, 3, 1, True, A["m3_up"], A["m3_down"], None, cw, x)
        store_x(nc, x, out)


def layout(i):
    import numpy as np
    f = {k: np.ascontiguousarray(v) for k, v in i.items()}
    a = {k: f[k] for k in ("x", "ctx_1024", "L0_xattn_bo")}
    for k in ("L0_xattn_ln_lat_g", "L0_xattn_ln_lat_b", "L0_xattn_ln_ctx_g", "L0_xattn_ln_ctx_b"):
        a[k + "_f"] = np.ascontiguousarray(f[k].reshape(-1, 128).T)

    def groups(w, n):
        return w.reshape(2, 128, n, -1).transpose(2, 1, 0, 3)

    def padded(w):
        return np.pad(w.reshape(w.shape[0], 16, 16), ((0, 0), (0, 0), (0, 16))).reshape(w.shape[0], 512)

    def by_group(w):
        return w.reshape(w.shape[0], 4, 4, 16).transpose(0, 1, 3, 2).reshape(w.shape[0], 256)

    def slot_weights(tag, wq, bq, wk, bk, wv, bv):
        wq, wk, bq, bk = by_group(wq), by_group(wk), by_group(bq[None])[0], by_group(bk[None])[0]
        a[tag + "_w"] = np.ascontiguousarray(np.stack(
            [w.reshape(2, 128, 256).transpose(1, 0, 2) for w in (wq, wk, wv)], axis=1))
        a[tag + "_b"] = np.ascontiguousarray(np.stack([v.reshape(2, 128).T for v in (bq, bk)], axis=1))
        a[tag + "_bv"] = np.ascontiguousarray(np.tile(padded(bv[None])[0].reshape(4, 128), (2, 1)).T)

    def slot_rows(wo):
        return np.ascontiguousarray(
            np.pad(wo.reshape(16, 16, 256), ((0, 0), (0, 16), (0, 0))).reshape(4, 128, 256).transpose(1, 0, 2))

    n = "L1_xattn_"
    slot_weights("l1", *(f[n + k] for k in ("Wq", "bq", "Wk", "bk", "Wv", "bv")))
    a["l1_wo"] = slot_rows(f[n + "Wo"])
    a[n + "bo"] = f[n + "bo"]
    n = "L3_xattn_"
    slot_weights("l3", f[n + "Wq"].T, f[n + "bq"], f[n + "Wk"].T, f[n + "bk"], f[n + "Wv"].T, f[n + "bv"])
    a["l3_wo"] = slot_rows(np.eye(256, dtype=np.float32))
    wkv = f["L0_xattn_Wkv"]
    a["l0_w"] = np.ascontiguousarray(np.stack(
        [groups(f["L0_xattn_Wq"], 8), groups(wkv[:, :1024], 8), groups(wkv[:, 1024:], 8)], axis=2))
    a["l0_cos"] = np.ascontiguousarray(f["L0_xattn_cos"].T)
    a["l0_sin"] = np.ascontiguousarray(f["L0_xattn_sin"].T)
    a["l0_wo"] = np.ascontiguousarray(f["L0_xattn_Wo"].reshape(8, 128, 256).transpose(1, 0, 2))

    def router(w):
        return np.ascontiguousarray(w.T.reshape(2, 128, -1).transpose(1, 0, 2))

    def expert_weights(tag, ups, down, per_round):
        e, hid = ups[0].shape[:2]
        ch = -(-hid // 128)
        fill = ((0, 0), (0, ch * 128 - hid), (0, 0))
        u = np.stack([np.pad(w, fill).reshape(e, ch, 128, 2, 128) for w in ups], axis=1)
        u = u.reshape(e // per_round, per_round, len(ups), ch, 128, 2, 128).transpose(0, 6, 5, 2, 1, 3, 4)
        a[tag + "_up"] = np.ascontiguousarray(u.reshape(e // per_round, 128, -1))
        d = np.pad(down.transpose(0, 2, 1), fill).reshape(e // per_round, per_round * ch, 128, 256)
        a[tag + "_down"] = np.ascontiguousarray(d.transpose(0, 2, 1, 3).reshape(e // per_round, 128, -1))

    n = "L1_ffn_"
    cat = lambda x, y: np.concatenate([f[n + x], f[n + y]], axis=0)
    a["m1_router"] = router(cat("gate_weight", "new_gate_weight"))
    a["m1_bias"] = np.concatenate([np.zeros(8, np.float32), f[n + "gate_bias"]])
    expert_weights("m1", [cat("w1", "new_w1"), cat("w3", "new_w3")], cat("w2", "new_w2"), 1)
    n = "L3_ffn_"
    a["m3_router"] = router(f[n + "router_weight"])
    a["m3_bias"] = f[n + "e_bias"]
    shared = lambda w: w.reshape(2, 128, 256)
    expert_weights("m3", [np.concatenate([f[n + "gate_w"], shared(f[n + "sh_gate_w"])]),
                          np.concatenate([f[n + "up_w"], shared(f[n + "sh_up_w"])])],
                   np.concatenate([f[n + "down_w"], f[n + "sh_down_w"].reshape(256, 2, 128).transpose(1, 0, 2)]), 3)
    n = "L2_ffn_"
    slot_weights("m2", *(f[n + k] for k in ("Wq", "bq", "Wk", "bk", "Wv", "bv")))
    a["m2_wo"] = slot_rows(f[n + "Wo"])
    a["m2_router"] = router(f[n + "gW"].T)
    for k in ("bo", "gb", "b2", "ln1_g", "ln1_b", "ln2_g", "ln2_b"):
        a[n + k] = f[n + k]
    for k in ("L2_ffn_ln1_g", "L2_ffn_ln1_b", "L2_xattn_input_norm_w"):
        a[k + "_f"] = np.ascontiguousarray(f[k].reshape(-1, 128).T)
    expert_weights("m2", [f[n + "W1"].transpose(0, 2, 1)], f[n + "W2"].transpose(0, 2, 1), 1)
    a["m2_b1"] = np.ascontiguousarray(f[n + "b1"].reshape(32, 128).T)
    rows = lambda w: np.ascontiguousarray(w.reshape(-1, 128, w.shape[1]).transpose(1, 0, 2))
    a["f0_w1"] = rows(f["L0_ffn_w1"].T)
    a["f0_w2"] = rows(f["L0_ffn_w2"].T)
    a["f0_taps"] = rows(f["L0_ffn_conv_w"][:, 0, :])
    a["f0_cb"] = np.ascontiguousarray(f["L0_ffn_conv_b"].reshape(8, 128).T)
    n = "L2_xattn_"
    for k, src in (("wk", "Wk"), ("wv", "Wv"), ("wq", "Wq"), ("wih", "gru_wih"), ("whh", "gru_whh")):
        a["g2_" + k] = rows(f[n + src].T)
    for k, src in (("bih", "gru_bih"), ("bhh", "gru_bhh"), ("norm", "slot_norm_w")):
        a["g2_" + k] = np.ascontiguousarray(f[n + src].reshape(-1, 128).T)
    return a


def kernel(**inputs):
    import concourse.bacc as bacc
    from concourse.bass_utils import run_bass_kernel_spmd

    nc = bacc.Bacc("TRN2", target_bir_lowering=False, num_devices=1)
    arrays = layout(inputs)
    aps = {k: nc.dram_tensor(k, v.shape, mybir.dt.from_np(v.dtype), kind="ExternalInput").ap()
           for k, v in arrays.items()}
    out = nc.dram_tensor("out", (B, NQ, D), F32, kind="ExternalOutput").ap()
    build(nc, aps, out)
    return run_bass_kernel_spmd(nc, [arrays], core_ids=[0]).results[0]["out"]
```

```python
import concourse.bass as bass
from concourse import mybir
from contextlib import ExitStack
import numpy as np

F32 = mybir.dt.float32
BF16 = mybir.dt.bfloat16
F32R = mybir.dt.float32r
ALU = mybir.AluOpType
ACT = mybir.ActivationFunctionType
AX = mybir.AxisListType

P = 128
D = 256
KC = D // P
B = 2
NQ = 512
NT = B * NQ
TQ = NT // P
NK = 1024
TK = B * NK // P
BANK = 512
ROUND = 1.5 * 2.0 ** 23


class Stage:

    spent = []

    def __init__(self, nc, name):
        self.nc, self.name, self.stack = nc, name, ExitStack()

    def __enter__(self):
        return self

    def __exit__(self, *a):
        return self.stack.__exit__(*a)

    def sb(self, name, shape, dt=F32):
        return self.stack.enter_context(self.nc.sbuf_tensor(f"{self.name}_{name}_s", shape, dt))

    def sem(self, name):
        handle = self.nc.alloc_semaphore(f"{self.name}_{name}")
        Stage.spent.append(handle)
        return handle

    def block(self):
        return self.stack.enter_context(self.nc.Block())


class Ahead:

    def __init__(self, nc, name, stack):
        self.stage, self.loads = stack.enter_context(Stage(nc, name)), []

    def load(self, name, shape, src, sem=None):
        dst = self.stage.sb(name, shape)
        sem = sem or self.stage.sem(name + "_loaded")
        self.loads.append((dst[tuple(slice(None) for _ in shape)], src, sem))
        return dst, sem

    def issue(self, sp):
        for dst, src, sem in self.loads:
            sp.dma_start(dst, src).then_inc(sem, 16)


def clear_semaphores(nc):
    nc.clear_and_free_semaphores(Stage.spent)
    Stage.spent = []
    nc.all_engine_barrier()


class Chain:

    def __init__(self, eng, sem, base=0):
        self.eng, self.sem, self.base, self.n = eng, sem, base, 0

    def done(self, ins):
        ins.then_inc(self.sem, 1)
        self.n += 1
        return self.n

    def wait(self):
        self.eng.wait_ge(self.sem, self.base + self.n)

    def link(self, ins):
        self.done(ins)
        self.wait()


def constants(nc, ident, ones, slot_sum):
    with Stage(nc, "const") as s:
        filled, made = s.sem("filled"), s.sem("made")
        block = s.block()

        @block.gpsimd
        def _(pool):
            pool.memset(ident[:, :], 0.0).then_inc(filled, 1)
            pool.memset(ones[:, :], 1.0).then_inc(filled, 1)
            pool.memset(slot_sum[:, :], 0.0).then_inc(filled, 1)
            pool.wait_ge(filled, 3)
            pool.affine_select(out=ident[:, :], in_=ident[:, :], compare_op=ALU.not_equal, fill=1.0, base=0,
                               pattern=[[-1, P]], channel_multiplier=1).then_inc(made, 1)
            v = slot_sum[:, :].rearrange("p (a c) -> p a c", a=4)
            pool.affine_select(out=v, in_=v, compare_op=ALU.not_equal, fill=1.0, base=-16,
                               pattern=[[-32, 4], [0, 32]], channel_multiplier=1).then_inc(made, 1)
            pool.wait_ge(made, 2)


def load_x(nc, x_dram, x_sb):
    with Stage(nc, "loadx") as s:
        loaded = s.sem("loaded")
        block = s.block()

        @block.sync
        def _(sp):
            sp.dma_start(x_sb[:, :, :], x_dram.rearrange("b (t p) d -> p (b t) d", p=P)).then_inc(loaded, 16)
            sp.wait_ge(loaded, 16)


def store_x(nc, x_sb, out_dram):
    with Stage(nc, "storex") as s:
        stored = s.sem("stored")
        block = s.block()

        @block.sync
        def _(sp):
            sp.dma_start(out_dram.rearrange("b (t p) d -> p (b t) d", p=P), x_sb[:, :, :]).then_inc(stored, 16)
            sp.wait_ge(stored, 16)


def normalize(nc, name, ps, ident, src, nt, dst_t, eps, norms=1, rms=False, gain_dram=None, shift_dram=None,
              keep=None, src_dram=None, ahead=None):
    with Stage(nc, name) as s:
        rows = keep if keep is not None else s.sb("rows", [P, nt, D])
        stats = s.sb("stats", [P, nt, 6])
        mv = s.sb("mv", [P, nt, 2])
        var_eps = s.sb("var_eps", [P, nt])
        dev = s.sb("dev", [P, nt])
        rstd = s.sb("rstd", [P, nt])
        gs = s.sb("gs", [P, 2, KC])
        loaded, src_loaded = s.sem("loaded"), s.sem("src_loaded")
        steps = s.sem("steps")
        var_ready = s.sem("var_ready")
        dev_ready = s.sem("dev_ready")
        rows_ready = s.sem("rows_ready")
        turned = s.sem("turned")
        copied = s.sem("copied")
        block = s.block()
        affine = gain_dram is not None

        @block.sync
        def _(sp):
            if src_dram is not None:
                sp.dma_start(src[:, :, :], src_dram).then_inc(src_loaded, 16)
            if affine:
                sp.dma_start(gs[:, 0, :], gain_dram).then_inc(loaded, 16)
                if shift_dram is not None:
                    sp.dma_start(gs[:, 1, :], shift_dram).then_inc(loaded, 16)
            if ahead is not None:
                ahead.issue(sp)

        @block.vector
        def _(dve):
            c = Chain(dve, steps)
            if src_dram is not None:
                dve.wait_ge(src_loaded, 16)
            for n in range(norms):
                x = src if n == 0 else rows
                for t in range(nt):
                    c.done(nc.vector.bn_stats(stats[:, t, :], x[:, t, :]))
                c.wait()
                for t in range(nt):
                    c.done(nc.vector.bn_aggr(mv[:, t, :], stats[:, t, :]))
                c.wait()
                if rms:
                    c.link(nc.vector.tensor_tensor(var_eps[:, :], mv[:, :, 0], mv[:, :, 0], ALU.mult))
                    c.link(nc.vector.tensor_tensor(dev[:, :], var_eps[:, :], mv[:, :, 1], ALU.add))
                    c.done(nc.vector.tensor_scalar(var_eps[:, :], dev[:, :], eps, None, ALU.add))
                else:
                    c.done(nc.vector.tensor_scalar(var_eps[:, :], mv[:, :, 1], eps, None, ALU.add))
                c.wait()
                nc.vector.sem_inc(var_ready, 1)
                dve.wait_ge(dev_ready, n + 1)
                c.link(nc.vector.reciprocal(rstd[:, :], dev[:, :]))
                for t in range(nt):
                    if rms:
                        ins = nc.vector.tensor_scalar(rows[:, t, :], x[:, t, :], rstd[:, t:t + 1], None, ALU.mult)
                    else:
                        ins = nc.vector.tensor_scalar(rows[:, t, :], x[:, t, :], mv[:, t, 0:1], rstd[:, t:t + 1],
                                                      ALU.subtract, ALU.mult)
                    c.done(ins)
                c.wait()
            nc.vector.sem_inc(rows_ready, 1)

        @block.tensor
        def _(pe):
            pe.wait_ge(rows_ready, 1)
            unit = 0
            for k in range(KC):
                for t4 in range(nt // 4):
                    if unit >= 4:
                        pe.wait_ge(copied, unit - 3)
                    for j in range(4):
                        t = 4 * t4 + j
                        ins = nc.tensor.transpose(ps[:, unit % 4, j * P:(j + 1) * P], rows[:, t, k * P:(k + 1) * P],
                                                  ident[:, :])
                    ins.then_inc(turned, 1)
                    unit += 1

        @block.scalar
        def _(act):
            for n in range(norms):
                act.wait_ge(var_ready, n + 1)
                nc.scalar.activation(dev[:, :], var_eps[:, :], ACT.Sqrt).then_inc(dev_ready, 1)
            if affine:
                act.wait_ge(loaded, 32 if shift_dram is not None else 16)
            unit = 0
            for k in range(KC):
                for t4 in range(nt // 4):
                    act.wait_ge(turned, unit + 1)
                    out = dst_t[:, k, t4 * BANK:(t4 + 1) * BANK]
                    if affine and shift_dram is not None:
                        ins = nc.scalar.activation(out, ps[:, unit % 4, :], ACT.Identity, bias=gs[:, 1, k:k + 1],
                                                   scale=gs[:, 0, k:k + 1])
                    elif affine:
                        ins = nc.scalar.activation(out, ps[:, unit % 4, :], ACT.Copy, scale=gs[:, 0, k:k + 1])
                    else:
                        ins = nc.scalar.activation(out, ps[:, unit % 4, :], ACT.Copy)
                    ins.then_inc(copied, 1)
                    unit += 1
            act.wait_ge(copied, unit)


def transpose_rows(nc, name, ps, ident, src, nt, dst_t, src_dram):
    with Stage(nc, name) as s:
        loaded = s.sem("loaded")
        turned, copied = s.sem("turned"), s.sem("copied")
        block = s.block()

        @block.sync
        def _(sp):
            sp.dma_start(src[:, :, :], src_dram).then_inc(loaded, 16)

        @block.tensor
        def _(pe):
            pe.wait_ge(loaded, 16)
            unit = 0
            for k in range(KC):
                for t4 in range(nt // 4):
                    if unit >= 4:
                        pe.wait_ge(copied, unit - 3)
                    for j in range(4):
                        t = 4 * t4 + j
                        ins = nc.tensor.transpose(ps[:, unit % 4, j * P:(j + 1) * P], src[:, t, k * P:(k + 1) * P],
                                                  ident[:, :])
                    ins.then_inc(turned, 1)
                    unit += 1

        @block.scalar
        def _(act):
            unit = 0
            for k in range(KC):
                for t4 in range(nt // 4):
                    act.wait_ge(turned, unit + 1)
                    nc.scalar.activation(dst_t[:, k, t4 * BANK:(t4 + 1) * BANK], ps[:, unit % 4, :],
                                         ACT.Copy).then_inc(copied, 1)
                    unit += 1
            act.wait_ge(copied, unit)


def project_out(nc, name, ps, o_all, ngroups, wo_dram, bo_dram, acc, by_batch=False):
    with Stage(nc, name) as s:
        wo = s.sb("wo", [P, ngroups, D])
        bo = s.sb("bo", [P, D])
        w_loaded, b_loaded = s.sem("w_loaded"), s.sem("b_loaded")
        multiplied, added, biased = s.sem("multiplied"), s.sem("added"), s.sem("biased")
        block = s.block()

        @block.sync
        def _(sp):
            sp.dma_start(wo[:, :, :], wo_dram).then_inc(w_loaded, 16)
            if bo_dram is not None:
                sp.dma_start(bo[:, :], bo_dram.partition_broadcast(P)).then_inc(b_loaded, 16)

        @block.tensor
        def _(pe):
            pe.wait_ge(w_loaded, 16)
            for t in range(TQ):
                if t >= 4:
                    pe.wait_ge(added, t - 3)
                for g in range(ngroups):
                    o = (o_all[:, t // 4 * ngroups + g, t % 4 * P:(t % 4 + 1) * P] if by_batch
                         else o_all[:, g, t * P:(t + 1) * P])
                    ins = nc.tensor.matmul(ps[:, t % 4, 0:D], o, wo[:, g, :],
                                           start=(g == 0), stop=(g == ngroups - 1))
                ins.then_inc(multiplied, 1)

        @block.vector
        def _(dve):
            if bo_dram is not None:
                dve.wait_ge(b_loaded, 16)
                for t in range(TQ):
                    nc.vector.tensor_tensor(acc[:, t, :], acc[:, t, :], bo[:, :], ALU.add).then_inc(biased, 1)
                dve.wait_ge(biased, TQ)
            for t in range(TQ):
                dve.wait_ge(multiplied, t + 1)
                nc.vector.tensor_tensor(acc[:, t, :], acc[:, t, :], ps[:, t % 4, 0:D], ALU.add).then_inc(added, 1)
            dve.wait_ge(added, TQ)


def rope_attention(nc, name, ps, ones, q_t, ctx_t, w_dram, cos_dram, sin_dram, o_all):
    DH = 64
    G = 8
    SCALE = DH ** -0.5
    NC_ = NK // P
    NH = NK // BANK
    SLOTS = 4
    PROJECT_AT, DENOMINATORS_AT = (0, 1, 4, 4, 6), 4
    LOW_QUERIES_AT, ROTATE_AT, LOW_KEYS_AT, FINISH_AT = 1, (2, 4), (5, 6), 6
    HIGH_QUERIES_AT, HIGH_KEYS_AT, VALUES_AT = 0, (3, 5), (4, 6)
    with Stage(nc, name) as s:
        w = s.sb("w", [P, 2, 3, KC, P])
        q_hi, q_lo = s.sb("q_hi", [P, 2, 2, NQ], F32R), s.sb("q_lo", [P, 2, 2, NQ], F32R)
        k_parts = s.sb("k_parts", [P, 2, 2, NK], F32R)
        cos, sin = s.sb("cos", [P, NK]), s.sb("sin", [P, NK])
        k_cos, k_sin, k_rot = s.sb("k_cos", [P, BANK]), s.sb("k_sin", [P, BANK]), s.sb("k_rot", [P, NK])
        v = s.sb("v", [P, 2, NC_, P])
        clipped = s.sb("clipped", [P, SLOTS, 2 * NQ])
        probs = s.sb("probs", [P, SLOTS, 2 * NQ])
        prob_sum = s.sb("prob_sum", [P, 2, 2 * NQ])
        o_raw, rden = s.sb("o_raw", [P, NQ]), s.sb("rden", [P, NQ])
        tables, negated = s.sem("tables"), s.sem("negated")
        w_loaded, w_free = [s.sem("w_loaded0"), s.sem("w_loaded1")], s.sem("w_free")
        projected = s.sem("projected")
        q_hi_ready = s.sem("q_hi_ready")
        q_ready = s.sem("q_ready")
        k_turned = s.sem("k_turned")
        k_read = s.sem("k_read")
        k_rot_ready = s.sem("k_rot_ready")
        k_hi_ready = s.sem("k_hi_ready")
        k_ready = s.sem("k_ready")
        v_ready = s.sem("v_ready")
        scored = s.sem("scored")
        clip_done = s.sem("clip_done")
        exp_done = s.sem("exp_done")
        pv_done = s.sem("pv_done")
        summed = s.sem("summed")
        den_made = s.sem("den_made")
        o_copied = s.sem("o_copied")
        rden_ready, o_done = s.sem("rden_ready"), s.sem("o_done")
        block = s.block()

        def over_groups(eng, first, step):
            first()
            for b in range(B):
                def run(g, parity, last, after):
                    step(b * G + g, b, g, parity, last, after)

                run(0, 0, (b - 1, G - 1) if b else None, (b, 1))
                with eng.Fori(0, G // 2 - 1) as i:
                    run(2 * i + 1, 1, (b, 2 * i), (b, 2 * i + 2))
                    run(2 * i + 2, 0, (b, 2 * i + 1), (b, 2 * i + 3))
                run(G - 1, 1, (b, G - 2), (b + 1, 0) if b < B - 1 else None)

        @block.sync
        def _(sp):
            for j in range(4):
                sp.dma_start(cos[32 * j:32 * j + 32, :], cos_dram).then_inc(tables, 16)
                sp.dma_start(sin[32 * j:32 * j + 32, :], sin_dram).then_inc(tables, 16)
            for b in range(B):
                with sp.Fori(0, G // 2) as i:
                    for p in range(2):
                        sp.wait_ge(w_free, 2 * i + (b * G + p + 1))
                        sp.dma_start(w[:, p, :, :, :], w_dram[bass.ds(2 * i + p, 1)].rearrange("a p k c n -> (a p) k c n")
                                     ).then_inc(w_loaded[p], 16)

        @block.tensor
        def _(pe):
            def project(n, b, p, unit):
                if unit == 0:
                    pe.wait_ge(w_loaded[p], (n - p) * 8 + 16)
                    pe.wait_ge(v_ready, 2 * n + 2)
                if unit == 2:
                    pe.wait_ge(q_ready, n + 1)
                if unit >= 3:
                    pe.wait_ge(k_read, NH * n + unit - 2)
                for c in range(KC):
                    if unit == 0:
                        ins = nc.tensor.matmul(ps[:, 4, :], w[:, p, 0, c, :], q_t[:, c, b * NQ:(b + 1) * NQ],
                                               start=(c == 0), stop=(c == KC - 1))
                    elif unit <= 2:
                        at = b * NK + (unit - 1) * BANK
                        ins = nc.tensor.matmul(ps[:, 4 + unit % 2, :], w[:, p, 1, c, :], ctx_t[:, c, at:at + BANK],
                                               start=(c == 0), stop=(c == KC - 1))
                if unit >= 3:
                    for j in range(4):
                        at = b * NK + (4 * (unit - 3) + j) * P
                        for c in range(KC):
                            ins = nc.tensor.matmul(ps[:, 4 + unit % 2, j * P:(j + 1) * P], ctx_t[:, c, at:at + P],
                                                   w[:, p, 2, c, :], start=(c == 0), stop=(c == KC - 1))
                ins.then_inc(projected, 1)
                if unit == 4:
                    pe.wait_ge(projected, 5 * n + 5)
                    nc.tensor.sem_inc(w_free, 1)

            def scores(n, p, t):
                if t == 0:
                    pe.wait_ge(q_ready, n + 1)
                    pe.wait_ge(k_ready, NH * n + 1)
                if t == NC_ // NH:
                    pe.wait_ge(k_ready, NH * n + NH)
                pe.wait_ge(clip_done, NC_ * n + t + 1)
                for h in range(2):
                    for part, q in enumerate((q_hi, q_lo)):
                        ins = nc.tensor.matmul(ps[:, 2 * (t % 2) + h, :], k_parts[:, p, h, t * P:(t + 1) * P],
                                               q[:, p, h, :], start=(part == 0), stop=(part == 1))
                ins.then_inc(scored, 1)

            def value_product(n, p, t):
                if t == 0:
                    pe.wait_ge(v_ready, 2 * n + 4)
                    pe.wait_ge(o_copied, n + 1)
                pe.wait_ge(exp_done, NC_ * n + t + 1 + SLOTS)
                for h in range(2):
                    ins = nc.tensor.matmul(ps[64 * h:64 * h + 64, 6, :], v[:, p, t, 64 * h:64 * h + 64],
                                           probs[:, t % SLOTS, h * NQ:(h + 1) * NQ], start=(t == 0), stop=(t == NC_ - 1))
                ins.then_inc(pv_done, 1)

            def denominators(n, p):
                pe.wait_ge(summed, NC_ * n + NC_ + SLOTS)
                pe.wait_ge(o_done, n + 1)
                for h in range(2):
                    ins = nc.tensor.matmul(ps[64 * h:64 * h + 64, 7, :], ones[:, 0:64],
                                           prob_sum[:, p, h * NQ:(h + 1) * NQ], start=True, stop=True)
                ins.then_inc(den_made, 1)

            def first():
                for sem, free in ((w_free, 2), (v_ready, 2), (clip_done, 2), (exp_done, SLOTS), (pv_done, SLOTS),
                                  (summed, SLOTS), (den_made, 2), (o_copied, 1), (o_done, 1)):
                    nc.tensor.sem_inc(sem, free)
                for unit in range(5):
                    project(0, 0, 0, unit)

            def step(n, b, g, p, last, after):
                for t in range(NC_):
                    scores(n, p, t)
                    if t >= 2:
                        value_product(n, p, t - 2)
                    elif last is not None:
                        value_product(n - 1, 1 - p, NC_ - 2 + t)
                    if after is not None:
                        for unit in range(5):
                            if t == PROJECT_AT[unit]:
                                project(n + 1, after[0], 1 - p, unit)
                    if last is not None and t == DENOMINATORS_AT:
                        denominators(n - 1, 1 - p)
                if after is None:
                    value_product(n, p, NC_ - 2)
                    value_product(n, p, NC_ - 1)
                    denominators(n, p)

            over_groups(pe, first, step)

        @block.vector
        def _(dve):
            def low_queries(n, p):
                dve.wait_ge(q_hi_ready, 4 * n + 4)
                for h in range(2):
                    own = slice(64 * h, 64 * h + 64)
                    for half in range(2):
                        ins = nc.vector.scalar_tensor_tensor(
                            q_lo[64 * half:64 * half + 64, p, h, :], ps[own, 4, :], SCALE,
                            q_hi[own, p, h, :].bitcast(F32), ALU.mult, ALU.subtract)
                ins.then_inc(q_ready, 1)

            def rotate(n, j):
                at, bank = slice(j * BANK, (j + 1) * BANK), 5 - j
                dve.wait_ge(projected, 5 * n + j + 2)
                if not (isinstance(n, int) and n == 0):
                    dve.wait_ge(k_ready, NH * n + j - 1)
                if not (isinstance(n, int) and n == 0 and j == 0):
                    dve.wait_ge(k_rot_ready, NH * n + j)
                nc.vector.tensor_tensor(k_cos[:, :], cos[:, at], ps[:, bank, :], ALU.mult).then_inc(k_turned, 1)
                for i in range(4):
                    o = i ^ 1
                    nc.vector.tensor_tensor(k_sin[32 * i:32 * i + 32, :], ps[32 * o:32 * o + 32, bank, :],
                                            sin[32 * o:32 * o + 32, at], ALU.mult).then_inc(k_turned, 1)
                dve.wait_ge(k_turned, 5 * (NH * n + j) + 5)
                nc.vector.sem_inc(k_read, 1)
                nc.vector.tensor_tensor(k_rot[:, at], k_cos[:, :], k_sin[:, :], ALU.add).then_inc(k_rot_ready, 1)

            def low_keys(n, p, j):
                at = slice(j * BANK, (j + 1) * BANK)
                dve.wait_ge(k_hi_ready, 2 * (NH * n + j) + 2)
                for h in range(2):
                    own = slice(64 * h, 64 * h + 64)
                    ins = nc.vector.tensor_tensor(k_parts[64 - 64 * h:128 - 64 * h, p, h, at], k_rot[own, at],
                                                  k_parts[own, p, h, at].bitcast(F32), ALU.subtract)
                ins.then_inc(k_ready, 1)

            def clip(n, t):
                dve.wait_ge(scored, NC_ * n + t + 1)
                dve.wait_ge(exp_done, NC_ * n + t + 1)
                nc.vector.tensor_scalar(
                    clipped[:, t % SLOTS, :], ps[:, 2 * (t % 2):2 * (t % 2) + 2, :].rearrange("p a n -> p (a n)"),
                    11.0, -11.0, ALU.min, ALU.max).then_inc(clip_done, 1)

            def finish(n, b, g):
                dve.wait_ge(o_done, n + 1)
                dve.wait_ge(den_made, n + 3)
                nc.vector.reciprocal(rden[:, :], ps[:, 7, :]).then_inc(rden_ready, 1)
                dve.wait_ge(rden_ready, n + 1)
                dve.wait_ge(o_copied, n + 2)
                nc.vector.tensor_tensor(o_all[:, bass.ds(g, 1), b * NQ:(b + 1) * NQ].rearrange("p a n -> p (a n)"),
                                        o_raw[:, :], rden[:, :], ALU.mult).then_inc(o_done, 1)

            def first():
                dve.wait_ge(tables, 8 * 16)
                nc.vector.tensor_scalar(sin[32:64, :], sin[32:64, :], -1.0, None, ALU.mult).then_inc(negated, 1)
                nc.vector.tensor_scalar(sin[96:128, :], sin[96:128, :], -1.0, None, ALU.mult).then_inc(negated, 1)
                dve.wait_ge(negated, 2)
                low_queries(0, 0)
                for j in range(NH):
                    rotate(0, j)
                    low_keys(0, 0, j)

            def step(n, b, g, p, last, after):
                for t in range(NC_):
                    clip(n, t)
                    if after is not None:
                        if t == LOW_QUERIES_AT:
                            low_queries(n + 1, 1 - p)
                        for j in range(NH):
                            if t == ROTATE_AT[j]:
                                rotate(n + 1, j)
                        for j in range(NH):
                            if t == LOW_KEYS_AT[j]:
                                low_keys(n + 1, 1 - p, j)
                    if last is not None and t == FINISH_AT:
                        finish(n - 1, *last)
                if after is None:
                    finish(n, b, g)

            over_groups(dve, first, step)
            dve.wait_ge(o_done, B * G + 1)

        @block.scalar
        def _(act):
            def high_queries(n, p):
                act.wait_ge(projected, 5 * n + 1)
                for h in range(2):
                    for half in range(2):
                        nc.scalar.activation(q_hi[64 * half:64 * half + 64, p, h, :], ps[64 * h:64 * h + 64, 4, :],
                                             ACT.Copy, scale=SCALE).then_inc(q_hi_ready, 1)

            def high_keys(n, p, j):
                at = slice(j * BANK, (j + 1) * BANK)
                act.wait_ge(k_rot_ready, NH * n + j + 1)
                for h in range(2):
                    nc.scalar.activation(k_parts[64 * h:64 * h + 64, p, h, at], k_rot[64 * h:64 * h + 64, at],
                                         ACT.Copy).then_inc(k_hi_ready, 1)

            def values(n, p, j):
                act.wait_ge(projected, 5 * n + 4 + j)
                nc.scalar.activation(v[:, p, 4 * j:4 * j + 4, :].rearrange("p t n -> p (t n)"), ps[:, 5 - j, :],
                                     ACT.Copy).then_inc(v_ready, 1)

            def exponentials(n, t):
                act.wait_ge(clip_done, NC_ * n + t + 3)
                act.wait_ge(pv_done, NC_ * n + t + 1)
                act.wait_ge(summed, NC_ * n + t + 1)
                nc.scalar.activation(probs[:, t % SLOTS, :], clipped[:, t % SLOTS, :], ACT.Exp).then_inc(exp_done, 1)

            def copy_output(n):
                act.wait_ge(o_done, n + 1)
                act.wait_ge(pv_done, NC_ * n + NC_ + SLOTS)
                nc.scalar.activation(o_raw[:, :], ps[:, 6, :], ACT.Copy).then_inc(o_copied, 1)

            def first():
                high_queries(0, 0)
                for j in range(NH):
                    high_keys(0, 0, j)
                for j in range(2):
                    values(0, 0, j)

            def step(n, b, g, p, last, after):
                for t in range(NC_):
                    exponentials(n, t)
                    if t == 1 and last is not None:
                        copy_output(n - 1)
                    if after is not None:
                        if t == HIGH_QUERIES_AT:
                            high_queries(n + 1, 1 - p)
                        for j in range(NH):
                            if t == HIGH_KEYS_AT[j]:
                                high_keys(n + 1, 1 - p, j)
                            if t == VALUES_AT[j]:
                                values(n + 1, 1 - p, j)
                if after is None:
                    copy_output(n)

            over_groups(act, first, step)

        @block.gpsimd
        def _(pool):
            def step(n, b, g, p, last, after):
                pool.wait_ge(den_made, n + 1)
                for t in range(1, NC_):
                    pool.wait_ge(exp_done, NC_ * n + t + 1 + SLOTS)
                    if t > 1:
                        pool.wait_ge(summed, NC_ * n + t + SLOTS)
                    nc.gpsimd.tensor_tensor(prob_sum[:, p, :], probs[:, 0, :] if t == 1 else prob_sum[:, p, :],
                                            probs[:, t % SLOTS, :], ALU.add).then_inc(summed, 2 if t == 1 else 1)

            over_groups(pool, lambda: None, step)


def project_heads(nc, name, ps, x_t, kv_t, nk, w, bias, loaded, q_parts, k_parts, v_groups):
    SCALE = 16 ** -0.5
    TV = B * nk // P
    with Stage(nc, name) as s:
        v_all = s.sb("v_all", [P, 8, nk // P, 4, 32])
        full = s.sb("full", [P, 3, BANK])
        hi, lo = s.sb("hi", [P, 3, BANK], F32R), s.sb("lo", [P, 3, BANK], F32R)
        scaled = s.sem("scaled")
        made = s.sem("made")
        full_ready = s.sem("full_ready")
        hi_ready = s.sem("hi_ready")
        lo_ready = s.sem("lo_ready")
        hi_stored = [s.sem(f"hi_stored{j}") for j in range(3)]
        lo_stored = [s.sem(f"lo_stored{j}") for j in range(3)]
        v_ready, v_cleared, v_stored = s.sem("v_ready"), s.sem("v_cleared"), s.sem("v_stored")
        block = s.block()
        units = [(0, m, b, 0) for m in range(KC) for b in range(B)]
        units += [(1, m, b, j) for m in range(KC) for b in range(B) for j in range(nk // BANK)]
        U = len(units)

        def dest(what, part, m, b, j):
            if what == 0:
                return q_parts[part, b * 4 + 2 * m:b * 4 + 2 * m + 2].rearrange("g r h n -> (g r h) n")
            return k_parts[b * 4 + 2 * m:b * 4 + 2 * m + 2, :, part, :, j * BANK:(j + 1) * BANK].rearrange(
                "g r h n -> (g r) h n")

        @block.sync
        def _(sp):
            for u, (what, m, b, j) in enumerate(units):
                sp.wait_ge(hi_ready, u + 1)
                sp.dma_start(dest(what, 0, m, b, j), hi[:, u % 3, :].bitcast(F32)).then_inc(hi_stored[u % 3], 16)
                sp.wait_ge(lo_ready, u + 1)
                sp.dma_start(dest(what, 1, m, b, j), lo[:, u % 3, :].bitcast(F32)).then_inc(lo_stored[u % 3], 16)
            for b in range(B):
                sp.wait_ge(v_ready, (b + 1) * TV // B)
                sp.dma_start(v_groups[4 * b:4 * b + 4].rearrange("g p n -> p g n"),
                             v_all[:, 4 * b:4 * b + 4, :, :, :].rearrange("p g c h n -> p g (c h n)")
                             ).then_inc(v_stored, 16)
            sp.wait_ge(v_stored, 32)
            for j in range(3):
                sp.wait_ge(hi_stored[j], 16 * len(range(j, U, 3)))
                sp.wait_ge(lo_stored[j], 16 * len(range(j, U, 3)))

        @block.tensor
        def _(pe):
            pe.wait_ge(loaded, 32)
            for u, (what, m, b, j) in enumerate(units):
                if u >= 4:
                    pe.wait_ge(full_ready, u - 3)
                src = x_t[:, :, b * NQ:(b + 1) * NQ] if what == 0 else kv_t[:, :, b * nk + j * BANK:b * nk + (j + 1) * BANK]
                for c in range(KC):
                    ins = nc.tensor.matmul(ps[:, u % 4, :], w[:, what, c, m * P:(m + 1) * P], src[:, c, :],
                                           start=(c == 0), stop=(c == KC - 1))
                ins.then_inc(made, 1)
            for t in range(TV):
                if t >= 4:
                    pe.wait_ge(v_ready, t - 3)
                for c in range(KC):
                    ins = nc.tensor.matmul(ps[:, 4 + t % 4, 0:D], kv_t[:, c, t * P:(t + 1) * P], w[:, 2, c, :],
                                           start=(c == 0), stop=(c == KC - 1))
                ins.then_inc(made, 1)

        @block.scalar
        def _(act):
            act.wait_ge(scaled, 1)
            for u, (what, m, b, j) in enumerate(units):
                act.wait_ge(made, u + 1)
                if u >= 3:
                    act.wait_ge(lo_ready, u - 2)
                nc.scalar.activation(full[:, u % 3, :], ps[:, u % 4, :], ACT.Identity, bias=bias[:, what, m:m + 1],
                                     scale=SCALE if what == 0 else 1.0).then_inc(full_ready, 1)

        @block.vector
        def _(dve):
            dve.wait_ge(loaded, 32)
            nc.vector.tensor_scalar(bias[:, 0, :], bias[:, 0, :], SCALE, None, ALU.mult).then_inc(scaled, 1)
            for u in range(U):
                dve.wait_ge(full_ready, u + 1)
                if u >= 3:
                    dve.wait_ge(hi_stored[u % 3], 16 * (u // 3))
                    dve.wait_ge(lo_stored[u % 3], 16 * (u // 3))
                nc.vector.tensor_copy(hi[:, u % 3, :], full[:, u % 3, :]).then_inc(hi_ready, 1)
                dve.wait_ge(hi_ready, u + 1)
                nc.vector.tensor_tensor(lo[:, u % 3, :], full[:, u % 3, :], hi[:, u % 3, :].bitcast(F32), ALU.subtract
                                        ).then_inc(lo_ready, 1)
            dve.wait_ge(v_cleared, 2)
            for t in range(TV):
                dve.wait_ge(made, U + t + 1)
                b, c = divmod(t, nk // P)
                nc.vector.tensor_copy(v_all[:, b * 4:b * 4 + 4, c, :, 0:16],
                                      ps[:, 4 + t % 4, 0:D].rearrange("p (g h n) -> p g h n", g=4, h=4)
                                      ).then_inc(v_ready, 1)

        @block.gpsimd
        def _(pool):
            pool.memset(v_all[:, :, :, :, :].rearrange("p g c h n -> p (g c h n)"), 0.0).then_inc(v_cleared, 1)
            pool.wait_ge(v_cleared, 1)
            pool.memset(v_all[:, :, :, :, 16:17].rearrange("p g c h o -> p (g c) (h o)"), 1.0).then_inc(v_cleared, 1)


def head_attention(nc, name, ps, ident, slot_sum, nk, q_parts, k_parts, v_groups, bv_dram, o_all, sparse):
    G, S = 8, 4
    NC_ = nk // P
    NH = nk // BANK
    QT = NQ // P
    ROWS = S * QT
    FIRST = ROWS * NH
    SECOND = NC_ * 2
    EARLY = 4
    CAND = NC_ * 8
    BEFORE = [0] + [min(FIRST, EARLY + u * (FIRST - EARLY) // (SECOND - 1)) for u in range(SECOND)]
    LOADS = 16 * 5
    with Stage(nc, name) as s:
        qa = s.sb("qa", [P, 2, S, NQ], F32R)
        ka = s.sb("ka", [P, 2, S, nk], F32R)
        v = s.sb("v", [P, 2, NC_, S, 32])
        bv = s.sb("bv", [P, G])
        shift = s.sb("shift", [P, ROWS])
        half_max = s.sb("half_max", [P, ROWS, NH])
        minus_hi, minus_lo = s.sb("minus_hi", [ROWS, P], F32R), s.sb("minus_lo", [ROWS, P], F32R)
        probs = s.sb("probs", [P, 4, 2 * NQ])
        o_raw = s.sb("o_raw", [P, NQ])
        rden = s.sb("rden", [P, NQ])
        if sparse:
            T = {}
            T["sc"] = s.sb("sc", [P, ROWS, nk])
            T["cand"] = s.sb("cand", [P, ROWS, CAND])
            T["above"] = s.sb("above", [P, ROWS, CAND])
            T["best"] = s.sb("best", [P, ROWS, 8])
            T["ranks"] = s.sb("ranks", [P, 8])
            for n in ("count", "total", "rcount", "tau", "ntau"):
                T[n] = s.sb(n, [P, ROWS])
            T["over"] = s.sb("over", [P, nk], BF16)
            T["over2"] = s.sb("over2", [P, 2, nk], BF16)
            T["zero"] = s.sb("zero", [P, nk], BF16)
            T["worst"] = s.sb("worst", [P, 1])
            T["worst_all"] = s.sb("worst_all", [1, 1])
            T["flag"] = s.sb("flag", [1, 1], mybir.dt.int32)
        filled = [s.sem("filled0"), s.sem("filled1")]
        ones_set, bv_loaded = s.sem("ones_set"), s.sem("bv_loaded")
        qk_loaded = [s.sem("qk_loaded0"), s.sem("qk_loaded1")]
        rows_made = s.sem("rows_made")
        rows_used = s.sem("rows_used")
        rows_kept = s.sem("rows_kept")
        shift_ready = s.sem("shift_ready")
        shift_turned = s.sem("shift_turned")
        hi_ready, lo_ready = s.sem("hi_ready"), s.sem("lo_ready")
        shift_clearing = s.sem("shift_clearing")
        shift_cleared = s.sem("shift_cleared")
        shift_placed = s.sem("shift_placed")
        scored = s.sem("scored")
        exp_done = s.sem("exp_done")
        pv_done = s.sem("pv_done")
        o_copied, o_summed, o_scaled, o_done = s.sem("o_copied"), s.sem("o_summed"), s.sem("o_scaled"), s.sem("o_done")
        rden_ready = s.sem("rden_ready")
        steps = s.sem("steps")
        if sparse:
            for n in ("rows_seen", "tau_set", "summed", "worst_ready", "worst_turned", "rescue"):
                T[n] = s.sem(n)
        block = s.block()

        def over_groups(eng, first, step):
            first()
            with eng.Fori(0, G // 2 - 1) as i:
                step(2 * i, 0, True)
                step(2 * i + 1, 1, True)
            step(G - 2, 0, True)
            step(G - 1, 1, False)

        @block.sync
        def _(sp):
            def load(n, buf):
                for i in range(2):
                    sp.dma_start(qa[32 * i:32 * i + 32, buf, :, :].rearrange("r h n -> r (h n)").bitcast(F32),
                                 q_parts[i, bass.ds(n, 1)].rearrange("o r h n -> (o r) (h n)").unsqueeze(1).to_broadcast(
                                     [16, 2, S * NQ])).then_inc(qk_loaded[buf], 16)
                    sp.dma_start(ka[32 * i:32 * i + 32, buf, :, :].rearrange("r h n -> r (h n)").bitcast(F32),
                                 k_parts[bass.ds(n, 1)].rearrange("o r a h n -> (o r a) (h n)")
                                 ).then_inc(qk_loaded[buf], 16)
                sp.dma_start(v[:, buf, :, :, :].rearrange("p c h n -> p (c h n)"),
                             v_groups[bass.ds(n, 1)].rearrange("o p n -> (o p) n")).then_inc(qk_loaded[buf], 16)

            def place(n, buf):
                sp.wait_ge(lo_ready, n + 1)
                for part, src in enumerate((minus_hi, minus_lo)):
                    sp.dma_start(qa[64 + part:65 + part, buf, :, :].rearrange("o h (t n) -> o (h t) n", n=P).bitcast(F32),
                                 src[:, :].bitcast(F32)).then_inc(shift_placed, 16)

            sp.dma_start(bv[:, :], bv_dram).then_inc(bv_loaded, 16)
            load(0, 0)
            load(1, 1)

            def step(n, buf, more):
                if not sparse:
                    place(n + 1, 1 - buf)
                if not isinstance(n, int):
                    sp.wait_ge(pv_done, NC_ * n + NC_)
                    load(n + 2, buf)
                if sparse:
                    place(n + 1, 1 - buf)

            place(0, 0)
            with sp.Fori(0, G // 2 - 1) as i:
                step(2 * i, 0, True)
                step(2 * i + 1, 1, True)
            step(G - 2, 0, True)

        @block.gpsimd
        def _(pool):
            pool.memset(ka[64:128, 1, :, :].bitcast(F32), 1.0).then_inc(filled[1], 1)
            pool.memset(qa[64:128, 1, :, :].bitcast(F32), 0.0).then_inc(filled[1], 1)

            def clear(n, buf):
                pool.wait_ge(pv_done, NC_ * n + NC_)
                nc.gpsimd.sem_inc(shift_clearing, 1)
                pool.memset(qa[64:66, buf, :, :].bitcast(F32), 0.0).then_inc(shift_cleared, 1)

            with pool.Fori(0, G // 2 - 1) as i:
                clear(2 * i, 0)
                clear(2 * i + 1, 1)

        @block.tensor
        def _(pe):
            def first_bank(n, buf, f):
                if f == 0:
                    pe.wait_ge(qk_loaded[buf], (n - buf) * (LOADS // 2) + LOADS)
                    pe.wait_ge(shift_cleared, n + 1)
                if f < 2:
                    pe.wait_ge(rows_used, n * FIRST + 2)
                else:
                    pe.wait_ge(rows_used, n * FIRST + f + 1)
                if sparse:
                    pe.wait_ge(rows_kept, n * FIRST + f + 1)
                r, j = divmod(f, NH)
                h, t = divmod(r, QT)
                nc.tensor.matmul(ps[:, f % 2, :], qa[:, buf, h, t * P:(t + 1) * P],
                                 ka[:, buf, h, j * BANK:(j + 1) * BANK], start=True, stop=True).then_inc(rows_made, 1)

            def turn(n):
                pe.wait_ge(shift_ready, n + 1)
                if not (isinstance(n, int) and n == 0):
                    pe.wait_ge(o_done, n)
                nc.tensor.transpose(ps[0:ROWS, 7, 0:P], shift[:, :], ident[:, :]).then_inc(shift_turned, 1)

            def second_pair(n, buf, u):
                t = u // 2
                if u == 0:
                    pe.wait_ge(shift_placed, 32 * n + 32)
                    pe.wait_ge(o_copied, n + 1)
                if u < 2:
                    pe.wait_ge(exp_done, n * SECOND + 2)
                else:
                    pe.wait_ge(exp_done, n * SECOND + u + 1)
                for j in range(2):
                    ins = nc.tensor.matmul(ps[:, 2 + 2 * (u % 2) + j, :], ka[:, buf, 2 * (u % 2) + j, t * P:(t + 1) * P],
                                           qa[:, buf, 2 * (u % 2) + j, :], start=True, stop=True)
                ins.then_inc(scored, 1)

            def value_products(n, buf, t):
                pe.wait_ge(exp_done, n * SECOND + 2 * t + 4)
                for h in range(S):
                    ins = nc.tensor.matmul(ps[32 * h:32 * h + 32, 6, :], v[:, buf, t, h, :],
                                           probs[:, (2 * t + h // 2) % 4, (h % 2) * NQ:(h % 2 + 1) * NQ],
                                           start=(t == 0), stop=(t == NC_ - 1))
                ins.then_inc(pv_done, 1)

            def denominators(n, more):
                pe.wait_ge(o_copied, n + 2)
                if more:
                    pe.wait_ge(lo_ready, n + 2)
                nc.tensor.matmul(ps[:, 7, :], slot_sum[:, :], o_raw[:, :], start=True, stop=True).then_inc(o_summed, 1)

            def worst(n):
                pe.wait_ge(T["worst_ready"], n + 1)
                nc.tensor.transpose(ps[0:1, 7, 0:P], T["worst"][:, :], ident[:, :]).then_inc(T["worst_turned"], 1)

            def first():
                pe.wait_ge(filled[0], 2)
                nc.tensor.sem_inc(rows_used, 2)
                nc.tensor.sem_inc(shift_cleared, 2)
                nc.tensor.sem_inc(o_done, 1)
                nc.tensor.sem_inc(exp_done, 2)
                nc.tensor.sem_inc(o_copied, 1)
                if sparse:
                    nc.tensor.sem_inc(rows_kept, 2)
                for f in range(FIRST):
                    first_bank(0, 0, f)
                if sparse:
                    worst(0)
                turn(0)
                pe.wait_ge(filled[1], 2)

            def step(n, buf, more):
                f = 0
                for u in range(SECOND):
                    if sparse and more:
                        for f in range(BEFORE[u], BEFORE[u + 1]):
                            first_bank(n + 1, 1 - buf, f)
                        f = FIRST
                    second_pair(n, buf, u)
                    if u % 2 == 1 and u >= 3:
                        value_products(n, buf, u // 2 - 1)
                    if more and not sparse and u >= SECOND // 4:
                        while f < min(FIRST, (u + 1 - SECOND // 4) * 4 * FIRST // (SECOND * 2)):
                            first_bank(n + 1, 1 - buf, f)
                            f += 1
                value_products(n, buf, NC_ - 1)
                if more:
                    for f in range(f, FIRST):
                        first_bank(n + 1, 1 - buf, f)
                    if not sparse:
                        turn(n + 1)
                denominators(n, more and not sparse)
                if more and sparse:
                    pe.wait_ge(o_done, n + 2)
                    worst(n + 1)
                    turn(n + 1)

            over_groups(pe, first, step)

        @block.vector
        def _(dve):
            def first_product(n):
                for f in range(FIRST):
                    r, j = divmod(f, NH)
                    dve.wait_ge(rows_made, n * FIRST + f + 1)
                    if sparse:
                        nc.vector.sem_inc(T["rows_seen"], 1)
                        for c in range(BANK // P):
                            ins = nc.vector.max(T["cand"][:, r, 8 * (c + j * 4):8 * (c + j * 4) + 8],
                                                ps[:, f % 2, c * P:(c + 1) * P])
                    else:
                        ins = nc.vector.reduce_max(half_max[:, r, j:j + 1], ps[:, f % 2, :], AX.X)
                    ins.then_inc(rows_used, 1)
                dve.wait_ge(rows_used, n * FIRST + FIRST + 2)
                if sparse:
                    thresholds(nc, dve, T, n, ps, rows_kept, shift, ROWS, nk, steps)
                    nc.vector.sem_inc(shift_ready, 1)
                else:
                    nc.vector.reduce_max(shift[:, :], half_max[:, :, :], AX.X).then_inc(shift_ready, 1)

            def cut(n):
                dve.wait_ge(shift_turned, n + 1)
                if not (isinstance(n, int) and n == 0):
                    dve.wait_ge(shift_placed, 32 * n)
                nc.vector.tensor_scalar(minus_hi[:, :], ps[0:ROWS, 7, 0:P], -1.0, None, ALU.mult).then_inc(hi_ready, 1)
                dve.wait_ge(hi_ready, n + 1)
                nc.vector.scalar_tensor_tensor(minus_lo[:, :], ps[0:ROWS, 7, 0:P], -1.0, minus_hi[:, :].bitcast(F32),
                                               ALU.mult, ALU.subtract).then_inc(lo_ready, 1)

            def finish(n):
                dve.wait_ge(o_summed, n + 1)
                nc.vector.reciprocal(rden[:, :], ps[:, 7, :]).then_inc(rden_ready, 1)
                dve.wait_ge(rden_ready, n + 1)
                nc.vector.tensor_tensor(rden[:, :], o_raw[:, :], rden[:, :], ALU.mult).then_inc(o_scaled, 1)
                dve.wait_ge(o_scaled, n + 1)
                nc.vector.tensor_scalar(o_all[:, bass.ds(n, 1), :].rearrange("p a n -> p (a n)"), rden[:, :],
                                        bv[:, bass.ds(n, 1)], None, ALU.add).then_inc(o_done, 1)

            def first():
                if sparse:
                    for j in range(8):
                        nc.vector.memset(T["ranks"][:, j:j + 1], 1.0 / (j + 1)).then_inc(ones_set, 1)
                    nc.vector.memset(T["zero"][:, :], 0.0).then_inc(ones_set, 1)
                    dve.wait_ge(ones_set, 9)
                nc.vector.memset(qa[64:128, 0, :, :].bitcast(F32), 0.0).then_inc(filled[0], 1)
                nc.vector.memset(ka[64:128, 0, :, :].bitcast(F32), 1.0).then_inc(filled[0], 1)
                dve.wait_ge(bv_loaded, 16)
                first_product(0)
                cut(0)

            def step(n, buf, more):
                if more:
                    if sparse:
                        first_product_and_finish(n)
                    else:
                        first_product(n + 1)
                    cut(n + 1)
                    if not sparse:
                        finish(n)
                else:
                    finish(n)

            def first_product_and_finish(n):
                T["between"] = lambda: finish(n)
                first_product(n + 1)
                T["between"] = None

            if sparse:
                T["between"] = None
            over_groups(dve, first, step)
            dve.wait_ge(o_done, G + 1)

        @block.scalar
        def _(act):
            def keep(n, start, end):
                for f in range(start, end):
                    r, j = divmod(f, NH)
                    act.wait_ge(rows_used, n * FIRST + f + 3)
                    nc.scalar.activation(T["sc"][:, r, j * BANK:(j + 1) * BANK], ps[:, f % 2, :], ACT.Copy
                                         ).then_inc(rows_kept, 1)

            def first():
                if sparse:
                    keep(0, 0, FIRST)
                    sums(nc, act, T, 0, ROWS, nk, rows_kept, FIRST)

            def step(n, buf, more):
                for u in range(SECOND):
                    if sparse and more:
                        keep(n + 1, BEFORE[u], BEFORE[u + 1])
                    act.wait_ge(scored, n * SECOND + u + 1)
                    if u >= 4:
                        act.wait_ge(pv_done, n * NC_ + u // 2 - 1)
                    nc.scalar.activation(probs[:, u % 4, :],
                                         ps[:, 2 + 2 * (u % 2):4 + 2 * (u % 2), :].rearrange("p a n -> p (a n)"),
                                         ACT.Relu if sparse else ACT.Exp).then_inc(exp_done, 1)
                act.wait_ge(o_done, n + 1)
                act.wait_ge(pv_done, n * NC_ + NC_)
                nc.scalar.activation(o_raw[:, :], ps[:, 6, :], ACT.Copy).then_inc(o_copied, 1)
                if more and sparse:
                    sums(nc, act, T, n + 1, ROWS, nk, rows_kept, FIRST)

            over_groups(act, first, step)


CANDIDATE_STEPS = 2
EXCESS = 5e-4
RESCUE = 20


def threshold_shares(rows):
    return rows * 9 // 16, rows, rows * 9 // 16


def sums(nc, act, T, n, rows, nk, rows_kept, first):
    act.wait_ge(rows_kept, n * first + first + 2)
    shares = threshold_shares(rows)
    done = n * sum(shares)
    for k, share in enumerate(shares):
        act.wait_ge(T["tau_set"], n * len(shares) + k + 1)
        for r in range(share):
            if not (isinstance(n, int) and n == 0 and k == 0 and r == 0):
                act.wait_ge(T["summed"], done)
            nc.scalar.activation(T["over"][:, :], T["sc"][:, r, :], ACT.Relu, bias=T["ntau"][:, r:r + 1],
                                 accum_out=T["total"][:, r:r + 1]).then_inc(T["summed"], 1)
            done = done + 1


def thresholds(nc, dve, T, n, ps, rows_kept, shift, rows, nk, steps):
    cand, above, best, tau, ntau = T["cand"], T["above"], T["best"], T["tau"], T["ntau"]
    count, total, rcount = T["count"], T["total"], T["rcount"]
    CAND = cand.shape[2]
    shares = threshold_shares(rows)
    PER = rows + 9 + 6 * CANDIDATE_STEPS + 1 + 3 * rows - shares[0] - shares[2] + 6 + 5 + 2 + 2 + 2 + 1
    own = Chain(dve, steps, n * PER)
    summed = n * sum(shares)

    def wide(a, m):
        return a[:, :].unsqueeze(2).to_broadcast([P, rows, m])

    def count_candidates():
        own.link(nc.vector.tensor_tensor(above[:, :, :], cand[:, :, :], wide(tau, CAND), ALU.is_gt))
        own.link(nc.vector.reduce_sum(count[:, :], above[:, :, :], AX.X))

    def sum_rest(share):
        nc.vector.sem_inc(T["tau_set"], 1)
        for r in range(share, rows):
            own.done(nc.vector.scalar_tensor_tensor(T["over2"][:, r % 2, :], T["sc"][:, r, :], tau[:, r:r + 1],
                                                    T["zero"][:, :], ALU.subtract, ALU.max,
                                                    accum_out=total[:, r:r + 1]))
            if r > share:
                dve.wait_ge(steps, own.base + own.n - 1)
        own.wait()

    def update():
        own.link(nc.vector.scalar_tensor_tensor(total[:, :], total[:, :], -1.0, rcount[:, :], ALU.add, ALU.mult))
        own.link(nc.vector.tensor_tensor(tau[:, :], tau[:, :], total[:, :], ALU.add))
        own.link(nc.vector.tensor_scalar(ntau[:, :], tau[:, :], -1.0, None, ALU.mult))

    nc.vector.sem_inc(T["rows_seen"], 1)
    for r in range(rows):
        own.done(nc.vector.max(best[:, r, :], cand[:, r, :]))
    own.wait()
    for j in range(1, 8):
        own.link(nc.vector.tensor_tensor(best[:, :, j], best[:, :, j], best[:, :, j - 1], ALU.add))
    own.link(nc.vector.scalar_tensor_tensor(best[:, :, :], best[:, :, :], -1.0,
                                            T["ranks"][:, :].unsqueeze(1).to_broadcast([P, rows, 8]), ALU.add, ALU.mult))
    own.link(nc.vector.reduce_max(tau[:, :], best[:, :, :], AX.X))
    for k in range(CANDIDATE_STEPS):
        count_candidates()
        own.link(nc.vector.tensor_tensor(above[:, :, :], above[:, :, :], cand[:, :, :], ALU.mult))
        own.link(nc.vector.reduce_sum(total[:, :], above[:, :, :], AX.X))
        own.link(nc.vector.reciprocal(rcount[:, :], count[:, :]))
        own.link(nc.vector.scalar_tensor_tensor(tau[:, :], total[:, :], -1.0, rcount[:, :], ALU.add, ALU.mult))
    own.link(nc.vector.tensor_scalar(ntau[:, :], tau[:, :], -1.0, None, ALU.mult))
    dve.wait_ge(rows_kept, n * rows * (nk // BANK) + rows * (nk // BANK) + 2)

    sum_rest(shares[0])
    count_candidates()
    own.link(nc.vector.reciprocal(rcount[:, :], count[:, :]))
    dve.wait_ge(T["summed"], summed + shares[0])
    update()

    sum_rest(shares[1])
    for r in range(rows):
        own.done(nc.vector.tensor_scalar(T["over2"][:, r % 2, :], T["sc"][:, r, :], tau[:, r:r + 1], 0.0, ALU.is_gt,
                                         ALU.add, accum_out=count[:, r:r + 1]))
        if r > 0:
            dve.wait_ge(steps, own.base + own.n - 1)
    own.wait()
    own.link(nc.vector.tensor_scalar(count[:, :], count[:, :], 1.0, None, ALU.max))
    own.link(nc.vector.reciprocal(rcount[:, :], count[:, :]))
    if T["between"] is not None:
        T["between"]()
    dve.wait_ge(T["summed"], summed + shares[0] + shares[1])
    update()

    sum_rest(shares[2])
    dve.wait_ge(T["summed"], summed + sum(shares))
    own.link(nc.vector.tensor_scalar(total[:, :], total[:, :], -1.0, None, ALU.add))
    own.link(nc.vector.tensor_reduce(T["worst"][:, :], total[:, :], AX.X, ALU.max, apply_absolute_value=True))
    nc.vector.sem_inc(T["worst_ready"], 1)
    own.link(nc.vector.tensor_tensor(total[:, :], total[:, :], rcount[:, :], ALU.mult))
    own.link(nc.vector.tensor_tensor(tau[:, :], tau[:, :], total[:, :], ALU.add))
    dve.wait_ge(T["worst_turned"], n + 1)
    own.link(nc.vector.reduce_max(T["worst_all"][:, :], ps[0:1, 7, 0:P], AX.X))
    own.link(nc.vector.tensor_scalar(T["flag"][:, :], T["worst_all"][:, :], EXCESS, None, ALU.is_gt))
    nc.vector.sem_inc(T["rows_seen"], 1)
    late = dve.value_load(T["flag"][0:1, 0:1], min_val=0, max_val=1)
    PER_STEP = 2 * rows + 3
    LONG = 1 + RESCUE * PER_STEP
    with dve.If(late > 0):
        nc.vector.tensor_copy(tau[:, :], best[:, :, 0]).then_inc(T["rescue"], 1)
        dve.wait_ge(T["rescue"], n * LONG + 1)
        nc.vector.sem_inc(T["rows_seen"], 1)
        with dve.Fori(0, RESCUE) as k:
            more = Chain(dve, T["rescue"], n * LONG + 1 + k * PER_STEP)
            for r in range(rows):
                more.link(nc.vector.tensor_scalar(T["over2"][:, 0, :], T["sc"][:, r, :], tau[:, r:r + 1], 0.0,
                                                  ALU.is_gt, ALU.add, accum_out=count[:, r:r + 1]))
                more.link(nc.vector.scalar_tensor_tensor(T["over2"][:, 0, :], T["sc"][:, r, :], tau[:, r:r + 1],
                                                         T["zero"][:, :], ALU.subtract, ALU.max,
                                                         accum_out=total[:, r:r + 1]))
            more.link(nc.vector.reciprocal(rcount[:, :], count[:, :]))
            more.link(nc.vector.scalar_tensor_tensor(total[:, :], total[:, :], -1.0, rcount[:, :], ALU.add, ALU.mult))
            more.link(nc.vector.tensor_tensor(tau[:, :], tau[:, :], total[:, :], ALU.add))
            assert more.n == PER_STEP
    with dve.Else():
        nc.vector.sem_inc(T["rescue"], LONG)
    own.link(nc.vector.tensor_copy(shift[:, :], tau[:, :]))
    assert own.n == PER, (own.n, PER)

LOW, HIGH = -3.0e38, 3.0e38


def top_mask(nc, own, vals, n, k, buf, top, mask):
    tiles = vals.shape[1]
    own.link(nc.vector.memset(buf[:, :, :], LOW))
    own.link(nc.vector.tensor_copy(buf[:, :, 0:n], vals))
    for t in range(tiles):
        own.done(nc.vector.max(top[:, t, :], buf[:, t, :]))
    own.wait()
    own.link(nc.vector.memset(top[:, :, k:8], LOW))
    for t in range(tiles):
        own.done(nc.vector.match_replace(out=buf[:, t, :], in_to_replace=top[:, t, :], in_values=buf[:, t, :],
                                         imm_value=HIGH))
    own.wait()
    own.link(nc.vector.tensor_scalar(mask, buf[:, :, 0:n], HIGH, None, ALU.is_equal))


def route(nc, name, ps, x_t, n, w_dram, bias_dram, kind, cw):
    with Stage(nc, name) as s:
        w = s.sb("w", [P, KC, n])
        bias = s.sb("bias", [P, n])
        logits = s.sb("logits", [P, TQ, n])
        scores = s.sb("scores", [P, TQ, n])
        picked = s.sb("picked", [P, TQ, n])
        mask = s.sb("mask", [P, TQ, n])
        buf = s.sb("buf", [P, TQ, 24])
        top = s.sb("top", [P, TQ, 8])
        total = s.sb("total", [P, TQ])
        rtotal = s.sb("rtotal", [P, TQ])
        if kind == "grouped":
            low_high = s.sb("low_high", [P, TQ, 4, 2, 2])
            best = s.sb("best", [P, TQ, 4])
            gmask = s.sb("gmask", [P, TQ, 4])
            gbuf = s.sb("gbuf", [P, TQ, 16])
            biased = s.sb("biased", [P, TQ, n])
            masked = s.sb("masked", [P, TQ, n])
        loaded, made = s.sem("loaded"), s.sem("made")
        logits_ready, scores_ready, steps = s.sem("logits_ready"), s.sem("scores_ready"), s.sem("steps")
        block = s.block()

        def wide(a, m):
            return a.unsqueeze(2).to_broadcast([P, TQ, m])

        @block.sync
        def _(sp):
            sp.dma_start(w[:, :, :], w_dram).then_inc(loaded, 16)
            sp.dma_start(bias[:, :], bias_dram.partition_broadcast(P)).then_inc(loaded, 16)

        @block.tensor
        def _(pe):
            pe.wait_ge(loaded, 32)
            for t in range(TQ):
                for c in range(KC):
                    ins = nc.tensor.matmul(ps[:, 0, t * n:(t + 1) * n], x_t[:, c, t * P:(t + 1) * P], w[:, c, :],
                                           start=(c == 0), stop=(c == KC - 1))
            ins.then_inc(made, 1)

        @block.scalar
        def _(act):
            act.wait_ge(logits_ready, 1)
            nc.scalar.activation(scores[:, :, :], logits[:, :, :], ACT.Exp if kind == "softmax" else ACT.Sigmoid
                                 ).then_inc(scores_ready, 1)

        @block.vector
        def _(dve):
            own = Chain(dve, steps)
            dve.wait_ge(loaded, 32)
            dve.wait_ge(made, 1)
            all_logits = ps[:, 0, 0:TQ * n].rearrange("p (t n) -> p t n", t=TQ)
            row_bias = bias[:, :].unsqueeze(1).to_broadcast([P, TQ, n])
            if kind == "grouped":
                own.link(nc.vector.tensor_copy(logits[:, :, :], all_logits))
            else:
                own.link(nc.vector.tensor_tensor(logits[:, :, :], row_bias, all_logits, ALU.add))
            if kind == "softmax":
                own.link(nc.vector.reduce_max(total[:, :], logits[:, :, :], AX.X))
                own.link(nc.vector.tensor_tensor(logits[:, :, :], logits[:, :, :], wide(total[:, :], n),
                                                 ALU.subtract))
            nc.vector.sem_inc(logits_ready, 1)
            dve.wait_ge(scores_ready, 1)
            if kind == "softmax":
                own.link(nc.vector.reduce_sum(total[:, :], scores[:, :, :], AX.X))
                own.link(nc.vector.reciprocal(rtotal[:, :], total[:, :]))
                own.link(nc.vector.tensor_tensor(scores[:, :, :], scores[:, :, :], wide(rtotal[:, :], n), ALU.mult))
                top_mask(nc, own, scores[:, :, :], n, 2, buf, top, mask[:, :, :])
                own.link(nc.vector.tensor_tensor(cw[:, :, 0:n], scores[:, :, :], mask[:, :, :], ALU.mult))
                return
            if kind == "top2":
                top_mask(nc, own, scores[:, :, :], n, 2, buf, top, mask[:, :, :])
                factor = 1.0
            else:
                own.link(nc.vector.tensor_tensor(biased[:, :, :], scores[:, :, :], row_bias, ALU.add))
                v = biased[:, :, :].rearrange("p t (g a c) -> p (t g) a c", g=4, a=2)
                lh = low_high[:, :, :, :, :].rearrange("p t g a c -> p (t g) a c")
                own.done(nc.vector.tensor_tensor(lh[:, :, 0, :], v[:, :, :, 0], v[:, :, :, 1], ALU.add))
                own.link(nc.vector.tensor_tensor(lh[:, :, 1, :], v[:, :, :, 0], v[:, :, :, 1], ALU.max))
                b4 = best[:, :, :].rearrange("p t g -> p (t g)")
                own.link(nc.vector.tensor_tensor(b4, lh[:, :, 1, 0], lh[:, :, 1, 1], ALU.add))
                own.link(nc.vector.tensor_tensor(b4, b4, lh[:, :, 0, 0], ALU.max))
                own.link(nc.vector.tensor_tensor(b4, b4, lh[:, :, 0, 1], ALU.max))
                top_mask(nc, own, best[:, :, :], 4, 2, gbuf, top, gmask[:, :, :])
                own.link(nc.vector.tensor_tensor(
                    masked[:, :, :].rearrange("p t (g c) -> p (t g) c", g=4),
                    biased[:, :, :].rearrange("p t (g c) -> p (t g) c", g=4),
                    gmask[:, :, :].rearrange("p t g -> p (t g)").unsqueeze(2).to_broadcast([P, TQ * 4, 4]),
                    ALU.mult))
                top_mask(nc, own, masked[:, :, :], n, 4, buf, top, mask[:, :, :])
                factor = 2.5
            own.link(nc.vector.tensor_tensor(picked[:, :, :], scores[:, :, :], mask[:, :, :], ALU.mult))
            own.link(nc.vector.reduce_sum(total[:, :], picked[:, :, :], AX.X))
            own.link(nc.vector.tensor_scalar(total[:, :], total[:, :], 1e-20, None, ALU.add))
            own.link(nc.vector.reciprocal(rtotal[:, :], total[:, :]))
            if factor != 1.0:
                own.link(nc.vector.tensor_scalar(rtotal[:, :], rtotal[:, :], factor, None, ALU.mult))
            own.link(nc.vector.tensor_tensor(cw[:, :, 0:n], picked[:, :, :], wide(rtotal[:, :], n), ALU.mult))
            if cw.shape[2] > n:
                own.link(nc.vector.memset(cw[:, :, n:], 1.0))


def experts_ahead(nc, name, stack, rounds, per_round, chunks, gated, up_dram, down_dram, b1_dram=None):
    ahead = Ahead(nc, name + "w", stack)
    ch = per_round * chunks
    ahead.first = [ahead.load("up", [P, KC * (2 if gated else 1) * ch * P], up_dram[0]),
                   ahead.load("down", [P, ch * D], down_dram[0])]
    if b1_dram is not None:
        ahead.first.append(ahead.load("b1", [P, rounds * ch], b1_dram))
    return ahead


def experts(nc, name, ps, x_t, rounds, per_round, chunks, gated, ahead, up_dram, down_dram, cw, acc):
    CH = per_round * chunks
    WAYS = 2 if gated else 1
    HALVES = NT // BANK
    UNITS = HALVES * CH
    OUTS = TQ * per_round
    PASSES = ((0, 0), (0, 1), (1, 0))
    with Stage(nc, name) as s:
        (up, up_loaded), (down, down_loaded) = ahead.first[:2]
        up_parts = [s.sb(f"up_part{j}", [P, KC, WAYS, CH, P], F32R) for j in range(2)]
        down_parts = [s.sb(f"down_part{j}", [P, CH, D], F32R) for j in range(2)]
        x_parts = [s.sb(f"x_part{j}", [P, KC, NT], F32R) for j in range(2)]
        h_parts = [s.sb(f"h_part{j}", [P, CH, NT], F32R) for j in range(2)]
        act_out = s.sb("act_out", [P, 2, BANK])
        h = s.sb("h", [P, 2, BANK])
        if not gated:
            b1, b1_loaded = ahead.first[2]
        up_free, down_free = s.sem("up_free"), s.sem("down_free")
        up_hi_ready, down_hi_ready = s.sem("up_hi_ready"), s.sem("down_hi_ready")
        up_ready, down_ready = s.sem("up_ready"), s.sem("down_ready")
        x_hi_ready, x_ready = s.sem("x_hi_ready"), s.sem("x_ready")
        cut_seen = s.sem("cut_seen")
        upped = s.sem("upped")
        activated = s.sem("activated")
        h_made = s.sem("h_made")
        h_hi_ready = s.sem("h_hi_ready")
        h_ready = s.sem("h_ready")
        downed = s.sem("downed")
        added = s.sem("added")
        block = s.block()

        def flat(t):
            return t[:, :, :, :, :].rearrange("p k w c n -> p (k w c n)") if len(t.shape) == 5 else \
                t[:, :, :].rearrange("p c n -> p (c n)")

        @block.sync
        def _(sp):
            with sp.Fori(0, rounds - 1) as i:
                sp.wait_ge(up_ready, i + 1)
                sp.dma_start(up[:, :], up_dram[bass.ds(i + 1, 1)].rearrange("a p n -> (a p) n")).then_inc(up_loaded, 16)
                sp.wait_ge(down_ready, i + 1)
                sp.dma_start(down[:, :], down_dram[bass.ds(i + 1, 1)].rearrange("a p n -> (a p) n")
                             ).then_inc(down_loaded, 16)

        @block.tensor
        def _(pe):
            nc.tensor.sem_inc(up_free, 1)
            nc.tensor.sem_inc(down_free, 1)
            nc.tensor.sem_inc(added, 4)
            nc.tensor.sem_inc(h_made, 2)
            nc.tensor.sem_inc(h_ready, 2)
            pe.wait_ge(x_ready, 1)
            with pe.Fori(0, rounds) as i:
                pe.wait_ge(up_ready, i + 1)
                for u in range(UNITS):
                    half, c = u // CH, u % CH
                    pe.wait_ge(h_made, UNITS * i + u + 1)
                    for way in range(WAYS):
                        for n, (k, (a, b)) in enumerate((k, parts) for k in range(KC) for parts in PASSES):
                            ins = nc.tensor.matmul(ps[:, 2 * (u % 2) + way, :], up_parts[a][:, k, way, c, :],
                                                   x_parts[b][:, k, half * BANK:(half + 1) * BANK],
                                                   start=(n == 0), stop=(n == KC * len(PASSES) - 1))
                    ins.then_inc(upped, 1)
                pe.wait_ge(upped, UNITS * i + UNITS)
                nc.tensor.sem_inc(up_free, 1)
                pe.wait_ge(down_ready, i + 1)
                n = 0
                for half in range(HALVES):
                    pe.wait_ge(h_ready, UNITS * i + (half + 1) * CH + 2)
                    for e in range(per_round):
                        for t in range(half * TQ // HALVES, (half + 1) * TQ // HALVES):
                            pe.wait_ge(added, OUTS * i + n + 1)
                            for m, (c, (a, b)) in enumerate((c, parts) for c in range(chunks) for parts in PASSES):
                                ins = nc.tensor.matmul(ps[:, 4 + n % 4, 0:D],
                                                       h_parts[a][:, e * chunks + c, t * P:(t + 1) * P],
                                                       down_parts[b][:, e * chunks + c, :], start=(m == 0),
                                                       stop=(m == chunks * len(PASSES) - 1))
                            ins.then_inc(downed, 1)
                            n += 1
                pe.wait_ge(downed, OUTS * i + OUTS)
                nc.tensor.sem_inc(down_free, 1)

        @block.scalar
        def _(act):
            def high(i, loaded, free, parts, src, ready):
                act.wait_ge(free, i + 1)
                act.wait_ge(loaded, 16 * i + 16)
                nc.scalar.sem_inc(cut_seen, 1)
                nc.scalar.activation(flat(parts[0]), src[:, :], ACT.Copy).then_inc(ready, 1)

            if not gated:
                act.wait_ge(b1_loaded, 16)
            high(0, up_loaded, up_free, up_parts, up, up_hi_ready)

            def round_(i, more):
                for u in range(UNITS):
                    if u == min(2, UNITS - 1):
                        high(i, down_loaded, down_free, down_parts, down, down_hi_ready)
                    half, c = u // CH, u % CH
                    act.wait_ge(upped, UNITS * i + u + 1)
                    if gated:
                        act.wait_ge(h_made, UNITS * i + u + 1)
                        nc.scalar.activation(act_out[:, u % 2, :], ps[:, 2 * (u % 2), :], ACT.Silu).then_inc(activated, 1)
                    else:
                        act.wait_ge(h_ready, UNITS * i + u + 1)
                        nc.scalar.sem_inc(cut_seen, 1)
                        nc.scalar.activation(h[:, u % 2, :], ps[:, 2 * (u % 2), :], ACT.Relu,
                                             bias=b1[:, bass.ds(i * CH + c, 1)]).then_inc(h_made, 1)
                if more:
                    high(i + 1, up_loaded, up_free, up_parts, up, up_hi_ready)

            with act.Fori(0, rounds - 1) as i:
                round_(i, True)
            round_(rounds - 1, False)

        @block.vector
        def _(dve):
            for k in range(KC):
                nc.vector.tensor_copy(x_parts[0][:, k, :], x_t[:, k, :]).then_inc(x_hi_ready, 1)
            dve.wait_ge(x_hi_ready, KC)
            for k in range(KC):
                ins = nc.vector.tensor_tensor(x_parts[1][:, k, :], x_t[:, k, :], x_parts[0][:, k, :].bitcast(F32),
                                              ALU.subtract)
            ins.then_inc(x_ready, 1)
            with dve.Fori(0, rounds) as i:
                for u in range(UNITS):
                    half, c = u // CH, u % CH
                    at = slice(half * BANK, (half + 1) * BANK)
                    if gated:
                        dve.wait_ge(activated, UNITS * i + u + 1)
                        dve.wait_ge(h_ready, UNITS * i + u + 1)
                        nc.vector.tensor_tensor(h[:, u % 2, :], act_out[:, u % 2, :], ps[:, 2 * (u % 2) + 1, :], ALU.mult
                                                ).then_inc(h_made, 1)
                    dve.wait_ge(h_made, UNITS * i + u + 3)
                    nc.vector.tensor_copy(h_parts[0][:, c, at], h[:, u % 2, :]).then_inc(h_hi_ready, 1)
                    dve.wait_ge(h_hi_ready, UNITS * i + u + 1)
                    nc.vector.tensor_tensor(h_parts[1][:, c, at], h[:, u % 2, :], h_parts[0][:, c, at].bitcast(F32),
                                            ALU.subtract).then_inc(h_ready, 1)
                n = 0
                for half in range(HALVES):
                    for e in range(per_round):
                        for t in range(half * TQ // HALVES, (half + 1) * TQ // HALVES):
                            dve.wait_ge(downed, OUTS * i + n + 1)
                            dve.wait_ge(added, OUTS * i + n + 1)
                            nc.vector.scalar_tensor_tensor(acc[:, t, :], ps[:, 4 + n % 4, 0:D],
                                                           cw[:, t, bass.ds(i * per_round + e, 1)], acc[:, t, :],
                                                           op0=ALU.mult, op1=ALU.add).then_inc(added, 1)
                            n += 1
            dve.wait_ge(added, OUTS * rounds + 4)

        @block.gpsimd
        def _(pool):
            def low(i, hi_ready, parts, src, ready):
                pool.wait_ge(hi_ready, i + 1)
                nc.gpsimd.tensor_tensor(flat(parts[1]), src[:, :], flat(parts[0]).bitcast(F32), ALU.subtract
                                        ).then_inc(ready, 1)

            low(0, up_hi_ready, up_parts, up, up_ready)
            with pool.Fori(0, rounds - 1) as i:
                low(i, down_hi_ready, down_parts, down, down_ready)
                low(i + 1, up_hi_ready, up_parts, up, up_ready)
            low(rounds - 1, down_hi_ready, down_parts, down, down_ready)


def affine_rows(nc, name, rows, gain_dram, shift_dram, dst, add):
    with Stage(nc, name) as s:
        gain, shift = s.sb("gain", [P, D]), s.sb("shift", [P, D])
        loaded, steps = s.sem("loaded"), s.sem("steps")
        block = s.block()

        @block.sync
        def _(sp):
            sp.dma_start(gain[:, :], gain_dram.partition_broadcast(P)).then_inc(loaded, 16)
            sp.dma_start(shift[:, :], shift_dram.partition_broadcast(P)).then_inc(loaded, 16)

        @block.vector
        def _(dve):
            own = Chain(dve, steps)
            dve.wait_ge(loaded, 32)
            g = gain[:, :].unsqueeze(1).to_broadcast([P, TQ, D])
            b = shift[:, :].unsqueeze(1).to_broadcast([P, TQ, D])
            own.link(nc.vector.tensor_tensor(rows[:, :, :], rows[:, :, :], g, ALU.mult))
            if add:
                own.link(nc.vector.tensor_tensor(dst[:, :, :], dst[:, :, :], b, ALU.add))
                own.link(nc.vector.tensor_tensor(dst[:, :, :], dst[:, :, :], rows[:, :, :], ALU.add))
            else:
                own.link(nc.vector.tensor_tensor(dst[:, :, :], rows[:, :, :], b, ALU.add))


def expert_biases(nc, name, ps, ident, cw, n, b2_dram, acc):
    with Stage(nc, name) as s:
        b2 = s.sb("b2", [n, D])
        cw_t = s.sb("cw_t", [n, NT])
        loaded, turned, copied = s.sem("loaded"), s.sem("turned"), s.sem("copied")
        made, added = s.sem("made"), s.sem("added")
        block = s.block()

        @block.sync
        def _(sp):
            sp.dma_start(b2[:, :], b2_dram).then_inc(loaded, 16)

        @block.tensor
        def _(pe):
            for t in range(TQ):
                ins = nc.tensor.transpose(ps[0:n, t // 4, (t % 4) * P:(t % 4 + 1) * P], cw[:, t, :], ident[:, :])
            ins.then_inc(turned, 1)
            pe.wait_ge(copied, 1)
            pe.wait_ge(loaded, 16)
            for t in range(TQ):
                if t >= 4:
                    pe.wait_ge(added, t - 3)
                nc.tensor.matmul(ps[:, 4 + t % 4, 0:D], cw_t[:, t * P:(t + 1) * P], b2[:, :], start=True, stop=True
                                 ).then_inc(made, 1)

        @block.scalar
        def _(act):
            act.wait_ge(turned, 1)
            nc.scalar.activation(cw_t[:, :], ps[0:n, 0:2, :].rearrange("p a n -> p (a n)"), ACT.Copy
                                 ).then_inc(copied, 1)

        @block.vector
        def _(dve):
            for t in range(TQ):
                dve.wait_ge(made, t + 1)
                nc.vector.tensor_tensor(acc[:, t, :], acc[:, t, :], ps[:, 4 + t % 4, 0:D], ALU.add).then_inc(added, 1)
            dve.wait_ge(added, TQ)


def bit_conv_ffn(nc, name, ps, ident, ones, x, w1_dram, w2_dram, cw_dram, cb_dram):
    CH = 1024 // P
    LO = NQ + 2
    with Stage(nc, name) as s:
        w1 = s.sb("w1", [P, KC, 1024])
        w2 = s.sb("w2", [P, CH, D])
        w1q, w2q = s.sb("w1q", [P, KC, 1024], BF16), s.sb("w2q", [P, CH, D], BF16)
        wabs = s.sb("wabs", [P, 2048])
        wsum = s.sb("wsum", [P, 2])
        wscale, winv = s.sb("wscale", [P, 2]), s.sb("winv", [P, 2])
        rows = s.sb("rows", [P, TQ, D])
        stats, mv = s.sb("stats", [P, TQ, 6]), s.sb("mv", [P, TQ, 2])
        var_eps, dev, rstd = s.sb("var_eps", [P, TQ]), s.sb("dev", [P, TQ]), s.sb("rstd", [P, TQ])
        big, scale, inv = s.sb("big", [P, TQ]), s.sb("scale", [P, TQ]), s.sb("inv", [P, TQ])
        diag = s.sb("diag", [P, TQ, P])
        by_token = s.sb("by_token", [P, NT])
        xq_t = s.sb("xq_t", [P, KC, NT], BF16)
        hid = s.sb("hid", [P, 2, B, LO])
        conv = s.sb("conv", [P, 2, B, NQ])
        act_t = s.sb("act_t", [P, CH, NT])
        hq = s.sb("hq", [P, CH, NT], BF16)
        tmp = s.sb("tmp", [P, 2, NT])
        big4 = s.sb("big4", [P, TQ, 2])
        taps = s.sb("taps", [P, CH, 3])
        cb = s.sb("cb", [P, CH])
        out_scale = s.sb("out_scale", [P, TQ])
        loaded, steps = s.sem("loaded"), s.sem("steps")
        w_summed = s.sem("w_summed")
        w_totalled = s.sem("w_totalled")
        var_ready, dev_ready = s.sem("var_ready"), s.sem("dev_ready")
        rows_ready = s.sem("rows_ready")
        turned, copied, w1_ready = s.sem("turned"), s.sem("copied"), s.sem("w1_ready")
        diag_ready, spread, spread_copied = s.sem("diag_ready"), s.sem("spread"), s.sem("spread_copied")
        upped, conved, activated = s.sem("upped"), s.sem("conved"), s.sem("activated")
        hid_used = s.sem("hid_used")
        act_turned, maxed = s.sem("act_turned"), s.sem("maxed")
        hq_ready, downed, added = s.sem("hq_ready"), s.sem("downed"), s.sem("added")
        block = s.block()

        @block.sync
        def _(sp):
            sp.dma_start(w1[:, :, :], w1_dram).then_inc(loaded, 16)
            sp.dma_start(w2[:, :, :], w2_dram).then_inc(loaded, 16)
            sp.dma_start(taps[:, :, :], cw_dram).then_inc(loaded, 16)
            sp.dma_start(cb[:, :], cb_dram).then_inc(loaded, 16)

        @block.scalar
        def _(act):
            act.wait_ge(loaded, 64)
            nc.scalar.activation(wabs[:, :], w1[:, :, :].rearrange("p k n -> p (k n)"), ACT.Abs,
                                 accum_out=wsum[:, 0:1]).then_inc(w_summed, 1)
            act.wait_ge(w_summed, 1)
            nc.scalar.activation(wabs[:, :], w2[:, :, :].rearrange("p k n -> p (k n)"), ACT.Abs,
                                 accum_out=wsum[:, 1:2]).then_inc(w_summed, 1)
            act.wait_ge(var_ready, 1)
            nc.scalar.activation(dev[:, :], var_eps[:, :], ACT.Sqrt).then_inc(dev_ready, 1)
            for n in range(4):
                act.wait_ge(turned, n + 1)
                nc.scalar.activation(xq_t[:, n // 2, (n % 2) * BANK:(n % 2 + 1) * BANK], ps[:, n, :], ACT.Copy
                                     ).then_inc(copied, 1)
            for n in range(2):
                act.wait_ge(spread, 1)
                nc.scalar.activation(by_token[:, n * BANK:(n + 1) * BANK], ps[:, 4 + n, :], ACT.Copy
                                     ).then_inc(spread_copied, 1)
            for c in range(CH):
                act.wait_ge(conved, c + 1)
                nc.scalar.activation(act_t[:, c, :], conv[:, c % 2, :, :].rearrange("p b n -> p (b n)"), ACT.Silu,
                                     bias=cb[:, c:c + 1]).then_inc(activated, 1)
            for n in range(2):
                act.wait_ge(spread, 2)
                nc.scalar.activation(by_token[:, n * BANK:(n + 1) * BANK], ps[:, 4 + n, :], ACT.Copy
                                     ).then_inc(spread_copied, 1)

        @block.tensor
        def _(pe):
            pe.wait_ge(w_summed, 2)
            nc.tensor.matmul(ps[:, 7, 0:2], ones[:, :], wsum[:, :], start=True, stop=True).then_inc(w_totalled, 1)
            pe.wait_ge(rows_ready, 1)
            for k in range(KC):
                for t in range(TQ):
                    ins = nc.tensor.transpose(ps[:, 2 * k + t // 4, (t % 4) * P:(t % 4 + 1) * P],
                                              rows[:, t, k * P:(k + 1) * P], ident[:, :])
                    if t % 4 == 3:
                        ins.then_inc(turned, 1)
            pe.wait_ge(diag_ready, 1)
            for t in range(TQ):
                ins = nc.tensor.matmul(ps[:, 4 + t // 4, (t % 4) * P:(t % 4 + 1) * P], ones[:, :], diag[:, t, :],
                                       start=True, stop=True)
            ins.then_inc(spread, 1)
            pe.wait_ge(copied, 4)
            pe.wait_ge(w1_ready, 1)
            for c in range(CH):
                if c >= 2:
                    pe.wait_ge(hid_used, 2 * (c - 1))
                for b in range(B):
                    for k in range(KC):
                        ins = nc.tensor.matmul(ps[:, 2 * (c % 2) + b, :], w1q[:, k, c * P:(c + 1) * P],
                                               xq_t[:, k, b * NQ:(b + 1) * NQ], start=(k == 0), stop=(k == KC - 1))
                ins.then_inc(upped, 1)
            pe.wait_ge(activated, CH)
            for t in range(TQ):
                if t >= 2:
                    pe.wait_ge(maxed, t - 1)
                for c in range(CH):
                    ins = nc.tensor.transpose(ps[:, 2 * (t % 2) + c // 4, (c % 4) * P:(c % 4 + 1) * P],
                                              act_t[:, c, t * P:(t + 1) * P], ident[:, :])
                ins.then_inc(act_turned, 1)
            pe.wait_ge(diag_ready, 2)
            for t in range(TQ):
                ins = nc.tensor.matmul(ps[:, 4 + t // 4, (t % 4) * P:(t % 4 + 1) * P], ones[:, :], diag[:, t, :],
                                       start=True, stop=True)
            ins.then_inc(spread, 1)
            pe.wait_ge(hq_ready, CH)
            for t in range(TQ):
                if t >= 4:
                    pe.wait_ge(added, t - 3)
                for c in range(CH):
                    ins = nc.tensor.matmul(ps[:, t % 4, 0:D], hq[:, c, t * P:(t + 1) * P], w2q[:, c, :],
                                           start=(c == 0), stop=(c == CH - 1))
                ins.then_inc(downed, 1)

        @block.vector
        def _(dve):
            own = Chain(dve, steps)
            own.link(nc.vector.memset(hid[:, :, :, :], 0.0))
            for t in range(TQ):
                own.done(nc.vector.bn_stats(stats[:, t, :], x[:, t, :]))
            own.wait()
            for t in range(TQ):
                own.done(nc.vector.bn_aggr(mv[:, t, :], stats[:, t, :]))
            own.wait()
            own.link(nc.vector.tensor_scalar(var_eps[:, :], mv[:, :, 1], 1e-5, None, ALU.add))
            nc.vector.sem_inc(var_ready, 1)
            dve.wait_ge(dev_ready, 1)
            own.link(nc.vector.reciprocal(rstd[:, :], dev[:, :]))
            for t in range(TQ):
                own.done(nc.vector.tensor_scalar(rows[:, t, :], x[:, t, :], mv[:, t, 0:1], rstd[:, t:t + 1],
                                                 ALU.subtract, ALU.mult))
            own.wait()

            def scales():
                own.link(nc.vector.tensor_scalar(big[:, :], big[:, :], 1e-5, None, ALU.max))
                own.link(nc.vector.reciprocal(scale[:, :], big[:, :]))
                own.link(nc.vector.tensor_scalar(scale[:, :], scale[:, :], 127.0, None, ALU.mult))
                own.link(nc.vector.reciprocal(inv[:, :], scale[:, :]))

            own.link(nc.vector.tensor_reduce(big[:, :], rows[:, :, :], AX.X, ALU.max, apply_absolute_value=True))
            scales()
            for t in range(TQ):
                own.done(nc.vector.tensor_scalar(rows[:, t, :], rows[:, t, :], scale[:, t:t + 1], None, ALU.mult))
            own.wait()
            allr = rows[:, :, :].rearrange("p t n -> p (t n)")
            own.link(nc.vector.tensor_scalar(allr, allr, ROUND, -ROUND, ALU.add, ALU.add))
            own.link(nc.vector.tensor_scalar(allr, allr, 127.0, -128.0, ALU.min, ALU.max))
            nc.vector.sem_inc(rows_ready, 1)
            dve.wait_ge(w_totalled, 1)
            own.link(nc.vector.tensor_scalar(winv[:, :], ps[:, 7, 0:2], 1.0 / (1024 * D), 1e-5, ALU.mult, ALU.max))
            own.link(nc.vector.reciprocal(wscale[:, :], winv[:, :]))
            own.link(nc.vector.reciprocal(winv[:, :], wscale[:, :]))
            for t in range(TQ):
                own.done(nc.vector.tensor_scalar(diag[:, t, :], ident[:, :], inv[:, t:t + 1], winv[:, 0:1], ALU.mult,
                                                 ALU.mult))
            own.wait()
            nc.vector.sem_inc(diag_ready, 1)
            for n, (w, wq) in enumerate(((w1[:, :, :].rearrange("p k n -> p (k n)"), w1q[:, :, :].rearrange("p k n -> p (k n)")),
                                         (w2[:, :, :].rearrange("p k n -> p (k n)"), w2q[:, :, :].rearrange("p k n -> p (k n)")))):
                own.link(nc.vector.tensor_scalar(w, w, wscale[:, n:n + 1], None, ALU.mult))
                own.link(nc.vector.tensor_scalar(w, w, ROUND, -ROUND, ALU.add, ALU.add))
                own.link(nc.vector.tensor_scalar(wq, w, 1.0, -1.0, ALU.min, ALU.max))
                if n == 0:
                    nc.vector.sem_inc(w1_ready, 1)
            dve.wait_ge(spread_copied, 2)
            for c in range(CH):
                dve.wait_ge(upped, c + 1)
                for b in range(B):
                    own.done(nc.vector.tensor_tensor(hid[:, c % 2, b, 1:1 + NQ], by_token[:, b * NQ:(b + 1) * NQ],
                                                     ps[:, 2 * (c % 2) + b, :], ALU.mult))
                own.wait()
                nc.vector.sem_inc(hid_used, 2)
                if c >= 2:
                    dve.wait_ge(activated, c - 1)
                y, v = conv[:, c % 2, :, :], hid[:, c % 2, :, :]
                own.link(nc.vector.tensor_scalar(y, v[:, :, 0:NQ], taps[:, c, 0:1], None, ALU.mult))
                own.link(nc.vector.scalar_tensor_tensor(y, v[:, :, 1:NQ + 1], taps[:, c, 1:2], y, ALU.mult, ALU.add))
                own.link(nc.vector.scalar_tensor_tensor(y, v[:, :, 2:NQ + 2], taps[:, c, 2:3], y, ALU.mult, ALU.add))
                nc.vector.sem_inc(conved, 1)
            for t in range(TQ):
                dve.wait_ge(act_turned, t + 1)
                own.link(nc.vector.tensor_reduce(big[:, t:t + 1], ps[:, 2 * (t % 2):2 * (t % 2) + 2, :].rearrange("p a n -> p (a n)"),
                                                 AX.X, ALU.max, apply_absolute_value=True))
                nc.vector.sem_inc(maxed, 1)
            scales()
            own.link(nc.vector.tensor_scalar(out_scale[:, :], inv[:, :], winv[:, 1:2], None, ALU.mult))
            for t in range(TQ):
                own.done(nc.vector.tensor_scalar(diag[:, t, :], ident[:, :], scale[:, t:t + 1], None, ALU.mult))
            own.wait()
            nc.vector.sem_inc(diag_ready, 1)
            dve.wait_ge(spread_copied, 4)
            for c in range(CH):
                y = tmp[:, c % 2, :]
                own.link(nc.vector.tensor_tensor(y, act_t[:, c, :], by_token[:, :], ALU.mult))
                own.link(nc.vector.tensor_scalar(y, y, ROUND, -ROUND, ALU.add, ALU.add))
                nc.vector.tensor_scalar(hq[:, c, :], y, 127.0, -128.0, ALU.min, ALU.max).then_inc(hq_ready, 1)
            for t in range(TQ):
                dve.wait_ge(downed, t + 1)
                nc.vector.scalar_tensor_tensor(x[:, t, :], ps[:, t % 4, 0:D], out_scale[:, t:t + 1], x[:, t, :],
                                               ALU.mult, ALU.add).then_inc(added, 1)
            dve.wait_ge(added, TQ)


def slot_inputs(nc, name, ps, p_t, w, k_parts, v, weights):
    with Stage(nc, name) as s:
        wk, wv = s.sb("wk", [P, KC, D]), s.sb("wv", [P, KC, D])
        raw = {"wq": s.sb("wq", [P, KC, D]), "wih": s.sb("wih", [P, KC, 3 * D]), "whh": s.sb("whh", [P, KC, 3 * D])}
        norm_w = s.sb("norm_w", [P, KC])
        loaded, w_loaded = s.sem("loaded"), s.sem("w_loaded")
        made = s.sem("made")
        hi_ready = s.sem("hi_ready")
        lo_ready = s.sem("lo_ready")
        scaled, w_hi_ready, w_ready = s.sem("scaled"), s.sem("w_hi_ready"), s.sem("w_ready")
        block = s.block()
        KEYS = KC * B * NK // BANK
        UNITS = KEYS + TK // 2

        def key_bank(u):
            m, n = divmod(u, B * NK // BANK)
            return m, slice(n * BANK, (n + 1) * BANK)

        @block.sync
        def _(sp):
            sp.dma_start(wk[:, :, :], w["wk"]).then_inc(loaded, 16)
            sp.dma_start(wv[:, :, :], w["wv"]).then_inc(loaded, 16)
            for k in raw:
                sp.dma_start(raw[k][:, :, :], w[k]).then_inc(w_loaded, 16)
            sp.dma_start(norm_w[:, :], w["norm"]).then_inc(w_loaded, 16)

        @block.tensor
        def _(pe):
            pe.wait_ge(loaded, 32)
            for u in range(UNITS):
                if u >= 4:
                    pe.wait_ge(hi_ready, u - 3)
                    pe.wait_ge(lo_ready, min(u - 3, KEYS))
                if u < KEYS:
                    m, at = key_bank(u)
                    for c in range(KC):
                        ins = nc.tensor.matmul(ps[:, u % 4, :], wk[:, c, m * P:(m + 1) * P], p_t[:, c, at],
                                               start=(c == 0), stop=(c == KC - 1))
                else:
                    for j in range(2):
                        t = 2 * (u - KEYS) + j
                        for c in range(KC):
                            ins = nc.tensor.matmul(ps[:, u % 4, j * D:(j + 1) * D], p_t[:, c, t * P:(t + 1) * P],
                                                   wv[:, c, :], start=(c == 0), stop=(c == KC - 1))
                ins.then_inc(made, 1)

        @block.scalar
        def _(act):
            for u in range(UNITS):
                act.wait_ge(made, u + 1)
                if u < KEYS:
                    m, at = key_bank(u)
                    dst = k_parts[0][:, m, at]
                else:
                    t = 2 * (u - KEYS)
                    dst = v[:, t:t + 2, :].rearrange("p a n -> p (a n)")
                nc.scalar.activation(dst, ps[:, u % 4, :], ACT.Copy).then_inc(hi_ready, 1)
            act.wait_ge(scaled, 2)
            act.wait_ge(w_loaded, 64)
            for k in raw:
                nc.scalar.activation(weights[k][0][:, :, :].rearrange("p k n -> p (k n)"),
                                     raw[k][:, :, :].rearrange("p k n -> p (k n)"), ACT.Copy).then_inc(w_hi_ready, 1)

        @block.vector
        def _(dve):
            dve.wait_ge(w_loaded, 64)
            for c in range(KC):
                nc.vector.tensor_scalar(raw["wq"][:, c, :], raw["wq"][:, c, :], norm_w[:, c:c + 1], None, ALU.mult
                                        ).then_inc(scaled, 1)
            for u in range(KEYS):
                m, at = key_bank(u)
                dve.wait_ge(hi_ready, u + 1)
                nc.vector.tensor_tensor(k_parts[1][:, m, at], ps[:, u % 4, :], k_parts[0][:, m, at].bitcast(F32),
                                        ALU.subtract).then_inc(lo_ready, 1)

        @block.gpsimd
        def _(pool):
            for j, k in enumerate(raw):
                pool.wait_ge(w_hi_ready, j + 1)
                nc.gpsimd.tensor_tensor(weights[k][1][:, :, :].rearrange("p k n -> p (k n)"),
                                        raw[k][:, :, :].rearrange("p k n -> p (k n)"),
                                        weights[k][0][:, :, :].rearrange("p k n -> p (k n)").bitcast(F32), ALU.subtract
                                        ).then_inc(w_ready, 1)
            pool.wait_ge(w_ready, 3)


def slot_gru(nc, name, ps, ident, ones, slots, k_parts, v, weights, w, x):
    ITERS = 3
    EPS = 1e-6
    SCALE = D ** -0.5
    NC_ = NK // P
    CHUNKS = B * NC_
    HG = NT // BANK * KC
    LAG = 3
    PASSES = ((0, 0), (0, 1), (1, 0))
    FIRST, SECOND = (0, 1, 5, 6), (2, 3, 4, 7)
    with Stage(nc, name) as s:
        bih, bhh = s.sb("bih", [P, 6]), s.sb("bhh", [P, 6])
        brz = s.sb("brz", [P, 4])
        slot_parts = [s.sb(f"slot_part{j}", [P, KC, NT], F32R) for j in range(2)]
        qu_parts = [s.sb(f"qu_part{j}", [P, KC, NT], F32R) for j in range(2)]
        sq = s.sb("sq", [P, KC, BANK])
        rs = s.sb("rs", [P, 2, BANK])
        dev = s.sb("dev", [P, BANK])
        top = s.sb("top", [P, 8])
        esum, resum = s.sb("esum", [P, 4]), s.sb("resum", [P, 4])
        probs, attn = s.sb("probs", [P, 4, NQ]), s.sb("attn", [P, 4, NQ])
        attn_sum = s.sb("attn_sum", [P, NQ])
        rden = s.sb("rden", [P, NQ])
        full = s.sb("full", [P, KC, BANK])
        r_t, z_t, n_t = s.sb("r_t", [P, 2, BANK]), s.sb("z_t", [P, HG, BANK]), s.sb("n_t", [P, HG, BANK])
        loaded = s.sem("loaded")
        steps = s.sem("steps")
        parts_ready = s.sem("parts_ready")
        sq_ready, sq_summed = s.sem("sq_ready"), s.sem("sq_summed")
        mean_ready, dev_ready, rs_ready = s.sem("mean_ready"), s.sem("dev_ready"), s.sem("rs_ready")
        q_made, q_ready = s.sem("q_made"), s.sem("q_ready")
        scored, top_ready, exp_done = s.sem("scored"), s.sem("top_ready"), s.sem("exp_done")
        attn_ready = s.sem("attn_ready")
        attn_used = s.sem("attn_used")
        attn_summed = s.sem("attn_summed")
        den_made = s.sem("den_made")
        upd_read = s.sem("upd_read")
        upd_ready = s.sem("upd_ready")
        gates_made, gates_done = s.sem("gates_made"), s.sem("gates_done")
        hn_ready, n_ready = s.sem("hn_ready"), s.sem("n_ready")
        b_ready, turned = s.sem("b_ready"), s.sem("turned")
        block = s.block()

        @block.sync
        def _(sp):
            sp.dma_start(bih[:, :], w["bih"]).then_inc(loaded, 16)
            sp.dma_start(bhh[:, :], w["bhh"]).then_inc(loaded, 16)

        @block.tensor
        def _(pe):
            for sem, free in ((sq_summed, 1), (rs_ready, 1), (attn_ready, 4), (attn_used, 4), (attn_summed, 4),
                              (den_made, 1), (hn_ready, 2)):
                nc.tensor.sem_inc(sem, free)

            def product(bank, parts, a_at, other, b_at, first=True, last=True):
                n = 0
                for c in range(KC):
                    for a, b in PASSES:
                        ins = nc.tensor.matmul(ps[:, bank, :], parts[a][:, c, a_at], other[b][:, c, b_at],
                                               start=(first and n == 0), stop=(last and n == KC * len(PASSES) - 1))
                        n += 1
                return ins

            with pe.Fori(0, ITERS) as i:
                for n in range(2):
                    pe.wait_ge(parts_ready, HG * i + KC * n + KC)
                    for m in range(KC):
                        product(FIRST[KC * n + m], weights["wq"], slice(m * P, (m + 1) * P), slot_parts,
                                slice(n * BANK, (n + 1) * BANK)).then_inc(q_made, 1)
                    pe.wait_ge(hn_ready, HG * i + 2)
                    pe.wait_ge(sq_ready, 2 * i + n + 1)
                    for c in range(KC):
                        ins = nc.tensor.matmul(ps[:, 2 + n, :], ones[:, :], sq[:, c, :], start=(c == 0),
                                               stop=(c == KC - 1))
                    ins.then_inc(sq_summed, 1)

                def update(k):
                    b, t = divmod(k, NC_)
                    if t == 0:
                        pe.wait_ge(upd_read, B * i + b) if b else pe.wait_ge(rs_ready, 2 * i + 3)
                    pe.wait_ge(attn_ready, CHUNKS * i + k + 5)
                    for m in range(KC):
                        ins = nc.tensor.matmul(ps[:, 2 + m, :], v[:, k, m * P:(m + 1) * P], attn[:, k % 4, :],
                                               start=(t == 0), stop=(t == NC_ - 1))
                    ins.then_inc(attn_used, 1)
                    if t == NC_ - 1:
                        pe.wait_ge(attn_summed, CHUNKS * i + k + 5)
                        nc.tensor.matmul(ps[:, 4, :], ones[:, :], attn_sum[:, :], start=True, stop=True
                                         ).then_inc(den_made, 1)

                for k in range(CHUNKS):
                    b, t = divmod(k, NC_)
                    pe.wait_ge(q_ready, HG * i + max(KC * b + KC, min(k + 1, HG)))
                    if k >= 4:
                        pe.wait_ge(exp_done, CHUNKS * i + k - 3)
                    product(FIRST[k % 4], k_parts, slice(k * P, (k + 1) * P), qu_parts,
                            slice(b * NQ, (b + 1) * NQ)).then_inc(scored, 1)
                    if k >= LAG:
                        update(k - LAG)
                for k in range(CHUNKS - LAG, CHUNKS):
                    update(k)
                for u in range(HG):
                    n, m = divmod(u, KC)
                    banks = SECOND if u % 2 else FIRST
                    pe.wait_ge(upd_ready, B * i + n + 1)
                    if u == 0:
                        pe.wait_ge(exp_done, CHUNKS * i + CHUNKS)
                    if u == 1:
                        pe.wait_ge(upd_read, B * i + B)
                    pe.wait_ge(hn_ready, HG * i + u + 1)
                    tok = slice(n * BANK, (n + 1) * BANK)
                    for gate in range(3):
                        at = slice(gate * D + m * P, gate * D + (m + 1) * P)
                        product(banks[gate], weights["wih"], at, qu_parts, tok, last=(gate == 2))
                        last = product(banks[3 if gate == 2 else gate], weights["whh"], at, slot_parts, tok,
                                       first=(gate == 2))
                    last.then_inc(gates_made, 1)
            pe.wait_ge(parts_ready, HG * ITERS + HG)
            for t in range(TQ):
                for c in range(KC):
                    ins = nc.tensor.transpose(ps[:, t // 2, (t % 2) * D + c * P:(t % 2) * D + (c + 1) * P],
                                              slots[:, c, t * P:(t + 1) * P], ident[:, :])
            ins.then_inc(turned, 1)

        @block.scalar
        def _(act):
            act.wait_ge(b_ready, 1)
            with act.Fori(0, ITERS) as i:
                def squares(n):
                    act.wait_ge(parts_ready, HG * i + KC * n + KC)
                    act.wait_ge(sq_summed, 2 * i + n + 1)
                    nc.scalar.activation(sq[:, :, :], slots[:, :, n * BANK:(n + 1) * BANK], ACT.Square).then_inc(sq_ready, 1)

                squares(0)
                squares(1)
                for n in range(2):
                    act.wait_ge(mean_ready, 2 * i + n + 1)
                    act.wait_ge(rs_ready, 2 * i + n + 1)
                    nc.scalar.activation(dev[:, :], rs[:, n, :], ACT.Sqrt).then_inc(dev_ready, 1)
                for k in range(CHUNKS):
                    j = k % 4
                    act.wait_ge(top_ready, CHUNKS * i + k + 1)
                    act.wait_ge(attn_ready, CHUNKS * i + k + 1)
                    nc.scalar.activation(probs[:, j, :], ps[:, FIRST[j], :], ACT.Exp, bias=top[:, j:j + 1],
                                         scale=SCALE, accum_out=esum[:, j:j + 1]).then_inc(exp_done, 1)

                def tanh(u):
                    act.wait_ge(hn_ready, HG * i + u + 3)
                    nc.scalar.activation(n_t[:, u, :], n_t[:, u, :], ACT.Tanh, bias=bih[:, 4 + u % KC:5 + u % KC]
                                         ).then_inc(n_ready, 1)

                for u in range(HG):
                    m = u % KC
                    banks = SECOND if u % 2 else FIRST
                    act.wait_ge(gates_made, HG * i + u + 1)
                    act.wait_ge(hn_ready, HG * i + u + 1)
                    nc.scalar.activation(r_t[:, u % 2, :], ps[:, banks[0], :], ACT.Sigmoid, bias=brz[:, m:m + 1])
                    nc.scalar.activation(z_t[:, u, :], ps[:, banks[1], :], ACT.Sigmoid,
                                         bias=brz[:, 2 + m:3 + m]).then_inc(gates_done, 1)
                    tanh(u)

        PER_ITER = 2 + 2 + 2 * HG + 3 * CHUNKS + B * (2 + 2 * KC) + HG + 4 * HG

        @block.vector
        def _(dve):
            dve.wait_ge(loaded, 32)
            nc.vector.tensor_tensor(brz[:, :], bih[:, 0:4], bhh[:, 0:4], ALU.add).then_inc(b_ready, 1)
            def cut(own, dst, m, tok, src, ready):
                own.link(nc.vector.tensor_copy(dst[0][:, m, tok], src))
                nc.vector.tensor_tensor(dst[1][:, m, tok], src, dst[0][:, m, tok].bitcast(F32), ALU.subtract
                                        ).then_inc(ready, 1)

            before = Chain(dve, b_ready, 1)
            for u in range(HG):
                n, m = divmod(u, KC)
                tok = slice(n * BANK, (n + 1) * BANK)
                cut(before, slot_parts, m, tok, slots[:, m, tok], parts_ready)
            with dve.Fori(0, ITERS) as i:
                own = Chain(dve, steps, i * PER_ITER)
                for n in range(2):
                    dve.wait_ge(sq_summed, 2 * i + n + 2)
                    own.link(nc.vector.tensor_scalar(rs[:, n, :], ps[:, 2 + n, :], 1.0 / D, EPS, ALU.mult, ALU.add))
                    nc.vector.sem_inc(mean_ready, 1)
                for n in range(2):
                    dve.wait_ge(dev_ready, 2 * i + n + 1)
                    own.link(nc.vector.reciprocal(rs[:, n, :], dev[:, :]))
                    nc.vector.sem_inc(rs_ready, 1)
                    for m in range(KC):
                        u = KC * n + m
                        dve.wait_ge(q_made, HG * i + u + 1)
                        if n:
                            dve.wait_ge(q_ready, HG * i + u - 1)
                        own.link(nc.vector.tensor_tensor(full[:, m, :], ps[:, FIRST[u], :], rs[:, n, :], ALU.mult))
                        cut(own, qu_parts, m, slice(n * BANK, (n + 1) * BANK), full[:, m, :], q_ready)

                def attention(k):
                    j = k % 4
                    dve.wait_ge(exp_done, CHUNKS * i + k + 1)
                    own.link(nc.vector.reciprocal(resum[:, j:j + 1], esum[:, j:j + 1]))
                    dve.wait_ge(attn_used, CHUNKS * i + k + 1)
                    dve.wait_ge(attn_summed, CHUNKS * i + k + 1)
                    nc.vector.tensor_scalar(attn[:, j, :], probs[:, j, :], resum[:, j:j + 1], None, ALU.mult
                                            ).then_inc(attn_ready, 1)

                def finish(b):
                    dve.wait_ge(den_made, B * i + b + 2)
                    own.link(nc.vector.tensor_scalar(rden[:, :], ps[:, 4, :], EPS, None, ALU.add))
                    own.link(nc.vector.reciprocal(rden[:, :], rden[:, :]))
                    dve.wait_ge(q_ready, HG * i + HG)
                    if b:
                        dve.wait_ge(upd_ready, B * i + b)
                    for m in range(KC):
                        own.done(nc.vector.tensor_tensor(full[:, m, :], rden[:, :], ps[:, 2 + m, :], ALU.mult))
                    own.wait()
                    nc.vector.sem_inc(upd_read, 1)
                    tok = slice(b * NQ, (b + 1) * NQ)
                    for m in range(KC):
                        own.done(nc.vector.tensor_copy(qu_parts[0][:, m, tok], full[:, m, :]))
                    own.wait()
                    for m in range(KC):
                        ins = nc.vector.tensor_tensor(qu_parts[1][:, m, tok], full[:, m, :],
                                                      qu_parts[0][:, m, tok].bitcast(F32), ALU.subtract)
                    ins.then_inc(upd_ready, 1)

                for k in range(CHUNKS):
                    j = k % 4
                    dve.wait_ge(scored, CHUNKS * i + k + 1)
                    own.link(nc.vector.reduce_max(top[:, 4 + j:5 + j], ps[:, FIRST[j], :], AX.X))
                    own.link(nc.vector.tensor_scalar(top[:, j:j + 1], top[:, 4 + j:5 + j], -SCALE, None, ALU.mult))
                    nc.vector.sem_inc(top_ready, 1)
                    if k:
                        attention(k - 1)
                    if k == NC_ + LAG:
                        finish(0)
                attention(CHUNKS - 1)
                finish(1)

                def candidate(u):
                    m = u % KC
                    banks = SECOND if u % 2 else FIRST
                    dve.wait_ge(gates_done, HG * i + u + 1)
                    own.link(nc.vector.scalar_tensor_tensor(n_t[:, u, :], ps[:, banks[3], :], bhh[:, 4 + m:5 + m],
                                                            r_t[:, u % 2, :], ALU.add, ALU.mult))
                    nc.vector.tensor_tensor(n_t[:, u, :], n_t[:, u, :], ps[:, banks[2], :], ALU.add).then_inc(hn_ready, 1)

                def state(u):
                    n, m = divmod(u, KC)
                    tok = slice(n * BANK, (n + 1) * BANK)
                    dve.wait_ge(n_ready, HG * i + u + 1)
                    dve.wait_ge(gates_made, HG * i + KC * n + KC)
                    own.link(nc.vector.tensor_tensor(slots[:, m, tok], slots[:, m, tok], n_t[:, u, :], ALU.subtract))
                    own.link(nc.vector.tensor_tensor(slots[:, m, tok], slots[:, m, tok], z_t[:, u, :], ALU.mult))
                    own.link(nc.vector.tensor_tensor(slots[:, m, tok], slots[:, m, tok], n_t[:, u, :], ALU.add))
                    cut(own, slot_parts, m, tok, slots[:, m, tok], parts_ready)

                candidate(0)
                candidate(1)
                state(0)
                candidate(2)
                state(1)
                candidate(3)
                state(2)
                state(3)
                assert own.n == PER_ITER, (own.n, PER_ITER)
            dve.wait_ge(turned, 1)
            for t4 in range(4):
                ins = nc.vector.tensor_tensor(x[:, 2 * t4:2 * t4 + 2, :].rearrange("p a n -> p (a n)"),
                                              x[:, 2 * t4:2 * t4 + 2, :].rearrange("p a n -> p (a n)"), ps[:, t4, :],
                                              ALU.add)
                ins.then_inc(turned, 1)
            dve.wait_ge(turned, 5)

        @block.gpsimd
        def _(pool):
            with pool.Fori(0, ITERS) as i:
                for k in range(CHUNKS):
                    b, t = divmod(k, NC_)
                    if t == 0:
                        continue
                    if t == 1:
                        pool.wait_ge(den_made, B * i + b + 1)
                    else:
                        pool.wait_ge(attn_summed, CHUNKS * i + k + 4)
                    pool.wait_ge(attn_ready, CHUNKS * i + k + 5)
                    nc.gpsimd.tensor_tensor(attn_sum[:, :], attn[:, 0, :] if t == 1 else attn_sum[:, :],
                                            attn[:, k % 4, :], ALU.add).then_inc(attn_summed, 2 if t == 1 else 1)


def build(nc, A, out, stages=range(8)):
    Stage.spent = []
    with ExitStack() as top:
        ps = top.enter_context(nc.psum_tensor("ps", [P, 8, BANK], F32))

        def sb(name, shape, dt=F32, stack=top):
            return stack.enter_context(nc.sbuf_tensor(name, shape, dt))

        ident, ones, slot_sum = sb("ident", [P, P]), sb("ones", [P, P]), sb("slot_sum", [P, P])
        x = sb("x_rows", [P, TQ, D])
        ctx_rows_dram = A["ctx_1024"].rearrange("b (t p) d -> p (b t) d", p=P)

        def by_feature(name):
            return A[name + "_f"]

        constants(nc, ident, ones, slot_sum)
        load_x(nc, A["x"], x)
        def slots(tag, kv_t, nk, sparse, wo_dram, bo_dram, acc, keep=None):
            q_parts = nc.dram_tensor(tag + "_q_parts", (2, 8, 16, 4, NQ), F32).ap()
            k_parts = nc.dram_tensor(tag + "_k_parts", (8, 16, 2, 4, nk), F32).ap()
            v_groups = nc.dram_tensor(tag + "_v_groups", (8, P, nk), F32).ap()
            with ExitStack() as st:
                x_t = sb(tag + "_x_t", [P, KC, NT], stack=st)
                ahead = Ahead(nc, tag + "w", st)
                w, loaded = ahead.load("w", [P, 3, KC, D], A[tag + "_w"])
                bias, _ = ahead.load("bias", [P, 2, KC], A[tag + "_b"], loaded)
                normalize(nc, tag + "ln", ps, ident, x, TQ, x_t, 1e-5, keep=keep, ahead=ahead)
                project_heads(nc, tag + "p", ps, x_t, x_t if kv_t is None else kv_t, nk, w, bias, loaded,
                              q_parts, k_parts, v_groups)
            with ExitStack() as st:
                o_all = sb(tag + "_o_all", [P, 8, NQ], stack=st)
                head_attention(nc, tag + "a", ps, ident, slot_sum, nk, q_parts, k_parts, v_groups, A[tag + "_bv"],
                               o_all, sparse)
                project_out(nc, tag + "o", ps, o_all, 4, wo_dram, bo_dram, acc, by_batch=True)

        if 0 in stages:
            with ExitStack() as l0:
                q_t = sb("l0_q_t", [P, KC, NT], stack=l0)
                c_t = sb("l0_c_t", [P, KC, B * NK], stack=l0)
                with ExitStack() as t:
                    c = sb("l0_c_rows", [P, TK, D], stack=t)
                    normalize(nc, "l0lnc", ps, ident, c, TK, c_t, 1e-5, gain_dram=by_feature("L0_xattn_ln_ctx_g"),
                              shift_dram=by_feature("L0_xattn_ln_ctx_b"), src_dram=ctx_rows_dram)
                    normalize(nc, "l0lnx", ps, ident, x, TQ, q_t, 1e-5, norms=2,
                              gain_dram=by_feature("L0_xattn_ln_lat_g"), shift_dram=by_feature("L0_xattn_ln_lat_b"))
                o_all = sb("l0_o_all", [P, 8, NT], stack=l0)
                rope_attention(nc, "l0a", ps, ones, q_t, c_t, A["l0_w"], A["l0_cos"], A["l0_sin"], o_all)
                project_out(nc, "l0o", ps, o_all, 8, A["l0_wo"], A["L0_xattn_bo"], x)
        if 1 in stages:
            bit_conv_ffn(nc, "f0", ps, ident, ones, x, A["f0_w1"], A["f0_w2"], A["f0_taps"], A["f0_cb"])
        if 2 in stages or 6 in stages:
            ctx_t = sb("ctx_t", [P, KC, B * NK])
            with ExitStack() as t:
                c = sb("c_rows", [P, TK, D], stack=t)
                transpose_rows(nc, "ctxt", ps, ident, c, TK, ctx_t, ctx_rows_dram)
        if 2 in stages:
            slots("l1", ctx_t, NK, True, A["l1_wo"], A["L1_xattn_bo"], x)
        clear_semaphores(nc)
        if 3 in stages:
            with ExitStack() as st:
                x_t = sb("m1_x_t", [P, KC, NT], stack=st)
                cw = sb("m1_cw", [P, TQ, 9], stack=st)
                ahead = experts_ahead(nc, "m1e", st, 9, 1, 6, True, A["m1_up"], A["m1_down"])
                normalize(nc, "m1ln", ps, ident, x, TQ, x_t, 1e-5, ahead=ahead)
                route(nc, "m1r", ps, x_t, 9, A["m1_router"], A["m1_bias"], "top2", cw)
                experts(nc, "m1e", ps, x_t, 9, 1, 6, True, ahead, A["m1_up"], A["m1_down"], cw, x)
        if 4 in stages:
            with ExitStack() as st:
                slots_t = sb("g2_slots", [P, KC, NT], stack=st)
                k_parts = [sb(f"g2_k{j}", [P, KC, B * NK], F32R, stack=st) for j in range(2)]
                v = sb("g2_v", [P, TK, D], stack=st)
                weights = {k: [sb(f"g2_{k}{j}", [P, KC, n * D], F32R, stack=st) for j in range(2)]
                           for k, n in (("wq", 1), ("wih", 3), ("whh", 3))}
                w = {k: A["g2_" + k] for k in ("wk", "wv", "wq", "wih", "whh", "bih", "bhh", "norm")}
                with ExitStack() as t:
                    p_t = sb("g2_p_t", [P, KC, B * NK], stack=t)
                    with ExitStack() as rows:
                        c = sb("g2_c_rows", [P, TK, D], stack=rows)
                        normalize(nc, "g2lnc", ps, ident, c, TK, p_t, 1e-6, rms=True,
                                  gain_dram=by_feature("L2_xattn_input_norm_w"), src_dram=ctx_rows_dram)
                    normalize(nc, "g2lnx", ps, ident, x, TQ, slots_t, 1e-5)
                    slot_inputs(nc, "g2i", ps, p_t, w, k_parts, v, weights)
                slot_gru(nc, "g2", ps, ident, ones, slots_t, k_parts, v, weights, w, x)
        clear_semaphores(nc)
        if 5 in stages:
            with ExitStack() as st:
                src = sb("m2_src", [P, TQ, D], stack=st)
                x1 = sb("m2_x1", [P, TQ, D], stack=st)
                x_t = sb("m2_x1_t", [P, KC, NT], stack=st)
                cw = sb("m2_cw", [P, TQ, 8], stack=st)
                slots("m2", None, NQ, False, A["m2_wo"], A["L2_ffn_bo"], src, keep=src)
                ahead = experts_ahead(nc, "m2e", st, 8, 1, 4, False, A["m2_up"], A["m2_down"], A["m2_b1"])
                normalize(nc, "m2ln1", ps, ident, src, TQ, x_t, 1e-5, keep=x1, ahead=ahead,
                          gain_dram=by_feature("L2_ffn_ln1_g"), shift_dram=by_feature("L2_ffn_ln1_b"))
                affine_rows(nc, "m2af1", x1, A["L2_ffn_ln1_g"], A["L2_ffn_ln1_b"], src, False)
                route(nc, "m2r", ps, x_t, 8, A["m2_router"], A["L2_ffn_gb"], "softmax", cw)
                experts(nc, "m2e", ps, x_t, 8, 1, 4, False, ahead, A["m2_up"], A["m2_down"], cw, src)
                expert_biases(nc, "m2eb", ps, ident, cw, 8, A["L2_ffn_b2"], src)
                normalize(nc, "m2ln2", ps, ident, src, TQ, x_t, 1e-5, keep=x1)
                affine_rows(nc, "m2af2", x1, A["L2_ffn_ln2_g"], A["L2_ffn_ln2_b"], x, True)
        clear_semaphores(nc)
        if 6 in stages:
            slots("l3", ctx_t, NK, False, A["l3_wo"], None, x)
        if 7 in stages:
            with ExitStack() as st:
                x_t = sb("m3_x_t", [P, KC, NT], stack=st)
                cw = sb("m3_cw", [P, TQ, 18], stack=st)
                ahead = experts_ahead(nc, "m3e", st, 6, 3, 1, True, A["m3_up"], A["m3_down"])
                normalize(nc, "m3ln", ps, ident, x, TQ, x_t, 1e-5, ahead=ahead)
                route(nc, "m3r", ps, x_t, 16, A["m3_router"], A["m3_bias"], "grouped", cw)
                experts(nc, "m3e", ps, x_t, 6, 3, 1, True, ahead, A["m3_up"], A["m3_down"], cw, x)
        store_x(nc, x, out)


def layout(i):
    import numpy as np
    f = {k: np.ascontiguousarray(v) for k, v in i.items()}
    a = {k: f[k] for k in ("x", "ctx_1024", "L0_xattn_bo")}
    for k in ("L0_xattn_ln_lat_g", "L0_xattn_ln_lat_b", "L0_xattn_ln_ctx_g", "L0_xattn_ln_ctx_b"):
        a[k + "_f"] = np.ascontiguousarray(f[k].reshape(-1, 128).T)

    def groups(w, n):
        return w.reshape(2, 128, n, -1).transpose(2, 1, 0, 3)

    def padded(w):
        return np.pad(w.reshape(w.shape[0], 16, 16), ((0, 0), (0, 0), (0, 16))).reshape(w.shape[0], 512)

    def by_group(w):
        return w.reshape(w.shape[0], 4, 4, 16).transpose(0, 1, 3, 2).reshape(w.shape[0], 256)

    def slot_weights(tag, wq, bq, wk, bk, wv, bv):
        wq, wk, bq, bk = by_group(wq), by_group(wk), by_group(bq[None])[0], by_group(bk[None])[0]
        a[tag + "_w"] = np.ascontiguousarray(np.stack(
            [w.reshape(2, 128, 256).transpose(1, 0, 2) for w in (wq, wk, wv)], axis=1))
        a[tag + "_b"] = np.ascontiguousarray(np.stack([v.reshape(2, 128).T for v in (bq, bk)], axis=1))
        a[tag + "_bv"] = np.ascontiguousarray(np.tile(padded(bv[None])[0].reshape(4, 128), (2, 1)).T)

    def slot_rows(wo):
        return np.ascontiguousarray(
            np.pad(wo.reshape(16, 16, 256), ((0, 0), (0, 16), (0, 0))).reshape(4, 128, 256).transpose(1, 0, 2))

    n = "L1_xattn_"
    slot_weights("l1", *(f[n + k] for k in ("Wq", "bq", "Wk", "bk", "Wv", "bv")))
    a["l1_wo"] = slot_rows(f[n + "Wo"])
    a[n + "bo"] = f[n + "bo"]
    n = "L3_xattn_"
    slot_weights("l3", f[n + "Wq"].T, f[n + "bq"], f[n + "Wk"].T, f[n + "bk"], f[n + "Wv"].T, f[n + "bv"])
    a["l3_wo"] = slot_rows(np.eye(256, dtype=np.float32))
    wkv = f["L0_xattn_Wkv"]
    a["l0_w"] = np.ascontiguousarray(np.stack(
        [groups(f["L0_xattn_Wq"], 8), groups(wkv[:, :1024], 8), groups(wkv[:, 1024:], 8)], axis=2))
    a["l0_cos"] = np.ascontiguousarray(f["L0_xattn_cos"].T)
    a["l0_sin"] = np.ascontiguousarray(f["L0_xattn_sin"].T)
    a["l0_wo"] = np.ascontiguousarray(f["L0_xattn_Wo"].reshape(8, 128, 256).transpose(1, 0, 2))

    def router(w):
        return np.ascontiguousarray(w.T.reshape(2, 128, -1).transpose(1, 0, 2))

    def expert_weights(tag, ups, down, per_round):
        e, hid = ups[0].shape[:2]
        ch = -(-hid // 128)
        fill = ((0, 0), (0, ch * 128 - hid), (0, 0))
        u = np.stack([np.pad(w, fill).reshape(e, ch, 128, 2, 128) for w in ups], axis=1)
        u = u.reshape(e // per_round, per_round, len(ups), ch, 128, 2, 128).transpose(0, 6, 5, 2, 1, 3, 4)
        a[tag + "_up"] = np.ascontiguousarray(u.reshape(e // per_round, 128, -1))
        d = np.pad(down.transpose(0, 2, 1), fill).reshape(e // per_round, per_round * ch, 128, 256)
        a[tag + "_down"] = np.ascontiguousarray(d.transpose(0, 2, 1, 3).reshape(e // per_round, 128, -1))

    n = "L1_ffn_"
    cat = lambda x, y: np.concatenate([f[n + x], f[n + y]], axis=0)
    a["m1_router"] = router(cat("gate_weight", "new_gate_weight"))
    a["m1_bias"] = np.concatenate([np.zeros(8, np.float32), f[n + "gate_bias"]])
    expert_weights("m1", [cat("w1", "new_w1"), cat("w3", "new_w3")], cat("w2", "new_w2"), 1)
    n = "L3_ffn_"
    a["m3_router"] = router(f[n + "router_weight"])
    a["m3_bias"] = f[n + "e_bias"]
    shared = lambda w: w.reshape(2, 128, 256)
    expert_weights("m3", [np.concatenate([f[n + "gate_w"], shared(f[n + "sh_gate_w"])]),
                          np.concatenate([f[n + "up_w"], shared(f[n + "sh_up_w"])])],
                   np.concatenate([f[n + "down_w"], f[n + "sh_down_w"].reshape(256, 2, 128).transpose(1, 0, 2)]), 3)
    n = "L2_ffn_"
    slot_weights("m2", *(f[n + k] for k in ("Wq", "bq", "Wk", "bk", "Wv", "bv")))
    a["m2_wo"] = slot_rows(f[n + "Wo"])
    a["m2_router"] = router(f[n + "gW"].T)
    for k in ("bo", "gb", "b2", "ln1_g", "ln1_b", "ln2_g", "ln2_b"):
        a[n + k] = f[n + k]
    for k in ("L2_ffn_ln1_g", "L2_ffn_ln1_b", "L2_xattn_input_norm_w"):
        a[k + "_f"] = np.ascontiguousarray(f[k].reshape(-1, 128).T)
    expert_weights("m2", [f[n + "W1"].transpose(0, 2, 1)], f[n + "W2"].transpose(0, 2, 1), 1)
    a["m2_b1"] = np.ascontiguousarray(f[n + "b1"].reshape(32, 128).T)
    rows = lambda w: np.ascontiguousarray(w.reshape(-1, 128, w.shape[1]).transpose(1, 0, 2))
    a["f0_w1"] = rows(f["L0_ffn_w1"].T)
    a["f0_w2"] = rows(f["L0_ffn_w2"].T)
    a["f0_taps"] = rows(f["L0_ffn_conv_w"][:, 0, :])
    a["f0_cb"] = np.ascontiguousarray(f["L0_ffn_conv_b"].reshape(8, 128).T)
    n = "L2_xattn_"
    for k, src in (("wk", "Wk"), ("wv", "Wv"), ("wq", "Wq"), ("wih", "gru_wih"), ("whh", "gru_whh")):
        a["g2_" + k] = rows(f[n + src].T)
    for k, src in (("bih", "gru_bih"), ("bhh", "gru_bhh"), ("norm", "slot_norm_w")):
        a["g2_" + k] = np.ascontiguousarray(f[n + src].reshape(-1, 128).T)
    return a


def kernel(**inputs):
    import concourse.bacc as bacc
    from concourse.bass_utils import run_bass_kernel_spmd

    nc = bacc.Bacc("TRN2", target_bir_lowering=False, num_devices=1)
    arrays = layout(inputs)
    aps = {k: nc.dram_tensor(k, v.shape, mybir.dt.from_np(v.dtype), kind="ExternalInput").ap()
           for k, v in arrays.items()}
    out = nc.dram_tensor("out", (B, NQ, D), F32, kind="ExternalOutput").ap()
    build(nc, aps, out)
    return run_bass_kernel_spmd(nc, [arrays], core_ids=[0]).results[0]["out"]
```
